# Optimizing a Trainium2 kernel written in Bass

```python
import numpy as np
import jax
import jax.numpy as jnp

def _softmax(x, axis=-1):
    return jax.nn.softmax(x, axis=axis)

def _gelu(x):
    return jax.nn.gelu(x, approximate=True)

def _silu(x):
    return jax.nn.silu(x)

def _sigmoid(x):
    return jax.nn.sigmoid(x)

def _layernorm(x, axis=-1, eps=1e-05):
    m = jnp.mean(x, axis=axis, keepdims=True)
    v = jnp.var(x, axis=axis, keepdims=True)
    return (x - m) / jnp.sqrt(v + eps)

def _scatter_add(tgt, idx, src, axis=0):
    return tgt.at[idx].add(src)

def _segment_sum(src, seg, n):
    return jax.ops.segment_sum(src, seg, n)
kernel_name = 'mk_vit_tower_cls_d1_tok_img768_r4_e5889c'

def setup_inputs(seed: int=0):
    np.random.seed(seed)
    _w = jnp.asarray

    def _rec_inputs():
        import jax
        import jax.numpy as jnp
        _rk = jax.random.key(seed)
        x = -0.00016672 + 0.999947 * jax.random.normal(jax.random.fold_in(_rk, 1), (32, 3, 128, 128), jnp.float32)
        cls_tok = 0.02 * jax.random.normal(jax.random.fold_in(_rk, 5), (1, 1, 192), jnp.float32)
        return (x, cls_tok)
    x, cls_tok = _rec_inputs()

    def _L0_tok_setup():
        import jax, jax.numpy as jnp
        import numpy as np
        PATCH = 16
        key = jax.random.key(seed)
        kx, kw, kb = jax.random.split(key, 3)
        B, C, H, W = (64, 3, 96, 96)
        n_embd = 192
        Cpp = C * PATCH * PATCH
        x = jax.random.normal(kx, (B, C, H, W), dtype=jnp.float32)
        bound = 1.0 / np.sqrt(Cpp)
        W_proj = jax.random.uniform(kw, (n_embd, Cpp), dtype=jnp.float32, minval=-bound, maxval=bound)
        b_proj = jax.random.uniform(kb, (n_embd,), dtype=jnp.float32, minval=-bound, maxval=bound)
        return {'x': x, 'W_proj': W_proj, 'b_proj': b_proj}
    _L0_tok_all = _L0_tok_setup()
    _L0_tok_in = {k: v for k, v in _L0_tok_all.items() if k in ('W_proj', 'b_proj')}
    del _L0_tok_all

    def _L0_attn_setup():
        import jax, jax.numpy as jnp
        import numpy as np
        D_HEAD = 64
        IGNORE = -100000.0
        key = jax.random.key(seed)
        ks = jax.random.split(key, 5)
        B, S, D, H, M = (2, 512, 192, 12, D_HEAD)
        scale = 0.05
        return {'x': jax.random.normal(ks[0], (B, S, D), jnp.float32), 'W_Q': jax.random.normal(ks[1], (H, D, M), jnp.float32) * scale, 'b_Q': jnp.zeros((H, M), jnp.float32), 'W_K': jax.random.normal(ks[2], (H, D, M), jnp.float32) * scale, 'b_K': jnp.zeros((H, M), jnp.float32), 'W_V': jax.random.normal(ks[3], (H, D, M), jnp.float32) * scale, 'b_V': jnp.zeros((H, M), jnp.float32), 'W_O': jax.random.normal(ks[4], (H, M, D), jnp.float32) * scale, 'b_O': jnp.zeros((D,), jnp.float32)}
    _L0_attn_all = _L0_attn_setup()
    _L0_attn_in = {k: v for k, v in _L0_attn_all.items() if k in ('W_Q', 'b_Q', 'W_K', 'b_K', 'W_V', 'b_V', 'W_O', 'b_O')}
    del _L0_attn_all

    def _L0_ffn_setup():
        import jax, jax.numpy as jnp
        import numpy as np
        from jax import lax
        DIM = 192
        INTER = 128
        E = 8
        G = 4
        TOPK_G = 2
        TOPK = 2
        ROUTE_SCALE = 1.0

        def _gate(x2, gate_weight, gate_bias):
            T = x2.shape[0]
            scores = jax.nn.sigmoid(x2 @ gate_weight.T)
            s = scores + gate_bias
            sv = s.reshape(T, G, E // G)
            top2, _ = lax.top_k(sv, 2)
            group_scores = top2.sum(-1)
            _, gidx = lax.top_k(group_scores, TOPK_G)
            gmask = jnp.zeros((T, G), bool).at[jnp.arange(T)[:, None], gidx].set(True)
            masked = jnp.where(gmask[:, :, None], sv, -jnp.inf).reshape(T, E)
            _, idx = lax.top_k(masked, TOPK)
            w = jnp.take_along_axis(scores, idx, axis=1)
            w = w / (w.sum(-1, keepdims=True) + 1e-06) * ROUTE_SCALE
            return (w, idx)
        key = jax.random.key(seed)
        ks = jax.random.split(key, 9)
        s = 1.0 / np.sqrt(DIM)
        si = 1.0 / np.sqrt(INTER)
        return {'x': jax.random.normal(ks[0], (4, 1024, DIM), jnp.float32), 'gate_weight': jax.random.uniform(ks[1], (E, DIM), jnp.float32, -s, s), 'gate_bias': jnp.zeros((E,), jnp.float32), 'w1': jax.random.uniform(ks[2], (E, INTER, DIM), jnp.float32, -s, s), 'w2': jax.random.uniform(ks[3], (E, DIM, INTER), jnp.float32, -si, si), 'w3': jax.random.uniform(ks[4], (E, INTER, DIM), jnp.float32, -s, s), 'sw1': jax.random.uniform(ks[5], (INTER, DIM), jnp.float32, -s, s), 'sw2': jax.random.uniform(ks[6], (DIM, INTER), jnp.float32, -si, si), 'sw3': jax.random.uniform(ks[7], (INTER, DIM), jnp.float32, -s, s)}
    _L0_ffn_all = _L0_ffn_setup()
    _L0_ffn_in = {k: v for k, v in _L0_ffn_all.items() if k in ('gate_weight', 'gate_bias', 'w1', 'w2', 'w3', 'sw1', 'sw2', 'sw3')}
    del _L0_ffn_all
    return {'x': x, 'cls_tok': cls_tok, 'L0_tok_W_proj': _L0_tok_in['W_proj'], 'L0_tok_b_proj': _L0_tok_in['b_proj'], 'L0_attn_W_Q': _L0_attn_in['W_Q'], 'L0_attn_b_Q': _L0_attn_in['b_Q'], 'L0_attn_W_K': _L0_attn_in['W_K'], 'L0_attn_b_K': _L0_attn_in['b_K'], 'L0_attn_W_V': _L0_attn_in['W_V'], 'L0_attn_b_V': _L0_attn_in['b_V'], 'L0_attn_W_O': _L0_attn_in['W_O'], 'L0_attn_b_O': _L0_attn_in['b_O'], 'L0_ffn_gate_weight': _L0_ffn_in['gate_weight'], 'L0_ffn_gate_bias': _L0_ffn_in['gate_bias'], 'L0_ffn_w1': _L0_ffn_in['w1'], 'L0_ffn_w2': _L0_ffn_in['w2'], 'L0_ffn_w3': _L0_ffn_in['w3'], 'L0_ffn_sw1': _L0_ffn_in['sw1'], 'L0_ffn_sw2': _L0_ffn_in['sw2'], 'L0_ffn_sw3': _L0_ffn_in['sw3']}

def reference(x, cls_tok, L0_tok_W_proj, L0_tok_b_proj, L0_attn_W_Q, L0_attn_b_Q, L0_attn_W_K, L0_attn_b_K, L0_attn_W_V, L0_attn_b_V, L0_attn_W_O, L0_attn_b_O, L0_ffn_gate_weight, L0_ffn_gate_bias, L0_ffn_w1, L0_ffn_w2, L0_ffn_w3, L0_ffn_sw1, L0_ffn_sw2, L0_ffn_sw3):
    import jax
    import jax.numpy as jnp

    def _L0_tok_ref(x, W_proj, b_proj):
        import jax, jax.numpy as jnp
        import numpy as np
        PATCH = 16
        B, C, H, W = x.shape
        p = PATCH
        x = x.reshape(B, C, H // p, p, W // p, p)
        patches = jnp.transpose(x, (0, 2, 4, 1, 3, 5))
        patches = patches.reshape(B, H // p * (W // p), C * p * p)
        out = jnp.einsum('bnc,ec->bne', patches, W_proj) + b_proj
        return out

    def _L0_attn_ref(x, W_Q, b_Q, W_K, b_K, W_V, b_V, W_O, b_O):
        import jax, jax.numpy as jnp
        import numpy as np
        D_HEAD = 64
        IGNORE = -100000.0
        q = jnp.einsum('bqd,hdm->bqhm', x, W_Q) + b_Q
        k = jnp.einsum('bkd,hdm->bkhm', x, W_K) + b_K
        v = jnp.einsum('bkd,hdm->bkhm', x, W_V) + b_V
        scores = jnp.einsum('bqhm,bkhm->bhqk', q, k) / jnp.sqrt(jnp.asarray(D_HEAD, q.dtype))
        S = x.shape[1]
        causal = jnp.arange(S)[:, None] >= jnp.arange(S)[None, :]
        scores = jnp.where(causal[None, None, :, :], scores, jnp.asarray(IGNORE, scores.dtype))
        pattern = jax.nn.softmax(scores, axis=-1)
        z = jnp.einsum('bhqk,bkhm->bqhm', pattern, v)
        attn_out = jnp.einsum('bqhm,hmd->bqd', z, W_O) + b_O
        return attn_out

    def _L0_ffn_ref(x, gate_weight, gate_bias, w1, w2, w3, sw1, sw2, sw3):
        import jax, jax.numpy as jnp
        import numpy as np
        from jax import lax
        DIM = 192
        INTER = 128
        E = 8
        G = 4
        TOPK_G = 2
        TOPK = 2
        ROUTE_SCALE = 1.0

        def _gate(x2, gate_weight, gate_bias):
            T = x2.shape[0]
            scores = jax.nn.sigmoid(x2 @ gate_weight.T)
            s = scores + gate_bias
            sv = s.reshape(T, G, E // G)
            top2, _ = lax.top_k(sv, 2)
            group_scores = top2.sum(-1)
            _, gidx = lax.top_k(group_scores, TOPK_G)
            gmask = jnp.zeros((T, G), bool).at[jnp.arange(T)[:, None], gidx].set(True)
            masked = jnp.where(gmask[:, :, None], sv, -jnp.inf).reshape(T, E)
            _, idx = lax.top_k(masked, TOPK)
            w = jnp.take_along_axis(scores, idx, axis=1)
            w = w / (w.sum(-1, keepdims=True) + 1e-06) * ROUTE_SCALE
            return (w, idx)
        B, S, D = x.shape
        x2 = x.reshape(-1, D)
        T = x2.shape[0]
        weights, indices = _gate(x2, gate_weight, gate_bias)
        cw = jnp.zeros((T, E), x.dtype).at[jnp.arange(T)[:, None], indices].add(weights)
        h1 = jnp.einsum('td,eid->tei', x2, w1)
        h3 = jnp.einsum('td,eid->tei', x2, w3)
        h = jax.nn.silu(h1) * h3
        y = jnp.einsum('tei,edi,te->td', h, w2, cw)
        z = jax.nn.silu(x2 @ sw1.T) * (x2 @ sw3.T) @ sw2.T
        return (y + z).reshape(B, S, D)
    h = _L0_tok_ref(x, L0_tok_W_proj, L0_tok_b_proj)
    h = jnp.concatenate([jnp.broadcast_to(cls_tok, (h.shape[0], 1, h.shape[2])), h], axis=1)
    h = h + _L0_attn_ref(_layernorm(h, axis=-1), L0_attn_W_Q, L0_attn_b_Q, L0_attn_W_K, L0_attn_b_K, L0_attn_W_V, L0_attn_b_V, L0_attn_W_O, L0_attn_b_O)
    h = h + _L0_ffn_ref(_layernorm(h, axis=-1), L0_ffn_gate_weight, L0_ffn_gate_bias, L0_ffn_w1, L0_ffn_w2, L0_ffn_w3, L0_ffn_sw1, L0_ffn_sw2, L0_ffn_sw3)
    return h

_drawn_inputs = setup_inputs


def setup_inputs(seed=0):
    import zlib

    import numpy as np

    out = dict(_drawn_inputs(seed))
    spreads = {'L0_attn_b_Q': (0.0, 0.279),
     'L0_attn_b_K': (0.0, 0.8),
     'L0_attn_b_V': (0.0, 0.1),
     'L0_attn_b_O': (0.0, 0.1),
     'L0_ffn_gate_bias': (0.0, 0.1)}
    factors = {}
    for name, (base, spread) in spreads.items():
        noise = np.random.default_rng([zlib.crc32(name.encode()), seed]).standard_normal(out[name].shape)
        drawn = base * np.exp(spread * noise) if base else spread * noise
        out[name] = jnp.asarray(drawn.astype(out[name].dtype))
    for name, factor in factors.items():
        out[name] = (out[name] * factor).astype(out[name].dtype)
    return out
```

```python
from contextlib import ExitStack

import concourse.bass as bass
from concourse import mybir

F32 = mybir.dt.float32
F32R = mybir.dt.float32r
ALU = mybir.AluOpType
ACT = mybir.ActivationFunctionType
AX_X = mybir.AxisListType.X

P = 128
HUGE = 3.0e38
IGNORE = -100000.0
LN_EPS = 1e-05
SUM_EPS = 1e-06


class Signal:

    def __init__(self, sem, per_group, before=0):
        self.sem, self.per_group, self.before = sem, per_group, before

    def at(self, g, n):
        return g * self.per_group + (self.before + n)


def vit_tower(nc, xt, w_proj, w_qkv, w_o, w_gate, w_ffn, w_2, b_proj, b_q, b_k, b_v, b_o,
              gate_bias, cls_tok, out):
    NG, _, KC, TG = xt.shape
    D = w_proj.shape[2]
    DR = D - P
    HP = w_o.shape[1]
    DH = 64
    HD = HP * P
    NE = w_2.shape[1]
    NR = NE - 1
    NQ = DH
    NK = NQ + 1
    IMG = TG // NQ
    NT = TG // P
    SC = 2 * NK
    NH2 = HP // 2
    VR = 64
    CB = HP
    NGRP = 4
    assert D == P + DR and DR == 64 and TG == 512 and NQ == 64

    with ExitStack() as ctx:
        def sb(name, shape, dt=F32):
            return ctx.enter_context(nc.sbuf_tensor(name, shape, dt))

        def sem(name):
            return ctx.enter_context(nc.semaphore(name))

        bank = [ctx.enter_context(nc.psum_tensor(f"bank{i}", [P, 512], F32)) for i in range(8)]

        ident = sb("ident", [P, P])
        causal = sb("causal", [P, NK])
        onehot = sb("onehot", [40, NR, P], F32R)
        wproj = sb("wproj", [P, KC, D])
        wo = sb("wo", [P, HP, D])
        w2 = sb("w2", [P, NE, D])
        NW = w_qkv.shape[1]
        qkv_a = sb("qkv_a", [P, 2, NW], F32R)
        qkv_d = sb("qkv_d", [P, 2, NW], F32R)
        NF = w_ffn.shape[1]
        ffn_a = sb("ffn_a", [P, 2, NF], F32R)
        ffn_d = sb("ffn_d", [P, 2, NF], F32R)
        gate_a = sb("gate_a", [P, 2, NR], F32R)
        gate_d = sb("gate_d", [P, 2, NR], F32R)
        gate_raw = sb("gate_raw", [P, 2, NR])
        bproj = sb("bproj", [P, D])
        bq = sb("bq", [P, HP])
        bk = sb("bk", [P, HP])
        bv = sb("bv", [P, HP])
        bo = sb("bo", [1, D])
        gbias = sb("gbias", [P, NR])
        ones = sb("ones", [P, 2])
        power = sb("power", [P, NT])
        eps = sb("eps", [P, NT])
        ones_row = sb("ones_row", [1, P])
        const_row = sb("const_row", [1, VR])
        vw = sb("vw", [VR, D])
        earlier = sb("earlier", [P, NR, NR])

        xg = sb("xg", [P, KC, TG])
        h0 = sb("h0", [P, NT, D])
        h1 = sb("h1", [P, NT, D])
        xn = sb("xn", [P, NT, 2 * P])
        xa_hi = sb("xa_hi", [P, TG], F32R)
        xa_lo = sb("xa_lo", [P, TG], F32R)
        xd = sb("xd", [P, TG], F32R)
        q = sb("q", [P, HP, NT, P])
        k = sb("k", [P, HP, IMG, NK])
        v = sb("v", [P, NT, HD])
        s = sb("s", [P, 2, 2 * HP * NK])
        smax = sb("smax", [P, 2, 2 * HP])
        rsum = sb("rsum", [P, 2, 2 * HP])
        pn = sb("pn", [P, 2, 2 * HP, NQ])
        pcls = sb("pcls", [P, 2, 2, 32])
        pt = sb("pt", [P, 2, HP, P])
        pct = sb("pct", [VR, NT, P])
        silu = sb("silu", [P, 2, TG])
        hid = sb("hid", [P, NE, TG])
        stats1 = sb("stats1", [P, NT, 6])
        mv1 = sb("mv1", [P, NT, 2])
        stats2 = sb("stats2", [P, NT, 6])
        mv2 = sb("mv2", [P, NT, 2])
        g_lg = sb("g_lg", [P, NT, 2 * NR])
        g_sc = sb("g_sc", [P, NT, NR])
        g_s = sb("g_s", [P, NT, NR])
        g_gs = sb("g_gs", [P, NT, NGRP])
        g_cmp, g_eq = (pn[:, b].rearrange("p n c -> p (n c)")[:, 0:NT * NR * NR].rearrange(
            "p (t j i) -> p t j i", t=NT, j=NR) for b in range(2))
        g_rank = sb("g_rank", [P, NT, NR])
        g_sum = sb("g_sum", [P, NT])
        cw = sb("cw", [P, NT, 40])
        cwt = sb("cwt", [40, TG], F32R)
        c_row = sb("c_row", [1, D])
        c_h1 = sb("c_h1", [1, D])
        c_xn = sb("c_xn", [1, 2 * P])
        c_stats = sb("c_stats", [1, 6])
        c_mv = sb("c_mv", [1, 2])
        c_a_hi = sb("c_a_hi", [P, 2], F32R)
        c_a_lo = sb("c_a_lo", [P, 2], F32R)
        c_d = sb("c_d", [P, 2], F32R)
        vblk = silu[:].rearrange("p a t -> p (a t)")[:, 0:HP * VR].rearrange("p (j c) -> p j c", j=HP)
        c_hid = sb("c_hid", [P, NE])
        c_cw = sb("c_cw", [P, NR])
        c_out = sb("c_out", [1, D])

        WT = NW // 3
        stage = hid[:].rearrange("p e t -> p (e t)").rearrange("p (n b c) -> p n b c", n=3, b=2)

        d_cls, d_small, d_proj, d_wo, d_w2, d_gate = (sem(n) for n in (
            "d_cls", "d_small", "d_proj", "d_wo", "d_w2", "d_gate"))
        d_raw = [sem(f"d_raw{i}") for i in range(3)]
        x_loaded = sem("x_loaded")
        stored = sem("stored")
        consts = sem("consts")
        waited = sem("waited")
        pool_step = sem("pool_step")
        w_hi, w_lo = sem("w_hi"), sem("w_lo")
        f_hi, f_lo = sem("f_hi"), sem("f_lo")
        c_pe, c_act, c_dve, c_pool = sem("c_pe"), sem("c_act"), sem("c_dve"), sem("c_pool")
        tok_done = Signal(sem("tok_done"), NT)
        h0_done = Signal(sem("h0_done"), NT)
        ln1 = Signal(sem("ln1"), 2 * NT)
        rstd1 = Signal(sem("rstd1"), 1)
        xn1 = Signal(sem("xn1"), NT)
        x1_turned = Signal(sem("x1_turned"), 2)
        x1_hi = Signal(sem("x1_hi"), 2)
        x1_lo = Signal(sem("x1_lo"), 2)
        NQKV = 2 * HP + 2 * NT
        qkv_done = Signal(sem("qkv_done"), NQKV)
        qkv_kept = Signal(sem("qkv_kept"), NQKV)
        s_done = Signal(sem("s_done"), 2 * NT)
        s_masked = Signal(sem("s_masked"), 2 * NT)
        s_max = Signal(sem("s_max"), NT)
        s_shifted = Signal(sem("s_shifted"), NT)
        s_exp = Signal(sem("s_exp"), NT)
        s_sum = Signal(sem("s_sum"), 2 * NT)
        p_done = Signal(sem("p_done"), NT)
        p_turned = Signal(sem("p_turned"), 2 * NT)
        p_kept = Signal(sem("p_kept"), 2 * NT)
        z_done = Signal(sem("z_done"), 2 * NT)
        z_kept = Signal(sem("z_kept"), 2 * NT)
        wo_done = Signal(sem("wo_done"), NT)
        h1_done = Signal(sem("h1_done"), NT)
        ln2 = Signal(sem("ln2"), 2 * NT)
        rstd2 = Signal(sem("rstd2"), 1)
        xn2 = Signal(sem("xn2"), NT)
        x2_turned = Signal(sem("x2_turned"), 2)
        x2_hi = Signal(sem("x2_hi"), 2)
        x2_lo = Signal(sem("x2_lo"), 2)
        gate_done = Signal(sem("gate_done"), 1)
        NGS = 23
        gate_step = Signal(sem("gate_step"), NGS)
        g_exp = Signal(sem("g_exp"), 1)
        cw_turned = Signal(sem("cw_turned"), 1)
        cw_hi = Signal(sem("cw_hi"), 1)
        cw_lo = Signal(sem("cw_lo"), 1)
        f1_done = Signal(sem("f1_done"), NE)
        f3_done = Signal(sem("f3_done"), NE)
        silu_done = Signal(sem("silu_done"), NE)
        f_prod = Signal(sem("f_prod"), NE)
        f_hid = Signal(sem("f_hid"), NR)
        y_done = Signal(sem("y_done"), 2)
        y_kept = Signal(sem("y_kept"), 2, before=2)
        y_stored = Signal(stored, 32, before=32)

        A_, D_ = slice(0, P), slice(P, D)

        def split_products(a_hi, a_lo, d, w_a, w_d, cols):
            return [(a_hi, w_a[:, 0, cols]), (a_hi, w_a[:, 1, cols]), (a_lo, w_a[:, 0, cols]),
                    (d, w_d[:, 0, cols]), (d, w_d[:, 1, cols])]

        def wait_apart(eng, semaphore, value):
            eng.wait_ge(semaphore, value)
            eng.sem_inc(waited, 1)

        block = ctx.enter_context(nc.Block())

        @block.sync
        def _(sp):
            def rows(t):
                return t.rearrange("(a n) -> a n", a=1)

            sp.dma_start(c_row[:], cls_tok).then_inc(d_cls, 16)
            small = [(bproj[:], rows(b_proj).to_broadcast([P, D])),
                     (gbias[:], rows(gate_bias).to_broadcast([P, NR])),
                     (bo[:], rows(b_o)), (bq[:], b_q), (bk[:], b_k), (bv[:], b_v)]
            for dst, src in small:
                sp.dma_start(dst, src).then_inc(d_small, 16)
            sp.dma_start(wproj[:], w_proj).then_inc(d_proj, 16)
            sp.dma_start(xg[:], xt[0]).then_inc(x_loaded, 16)
            for i in range(3):
                c = slice(i * WT, (i + 1) * WT)
                sp.dma_start(stage[:, i, 0, :], w_qkv[A_, c]).then_inc(d_raw[i], 16)
                sp.dma_start(stage[0:DR, i, 1, :], w_qkv[D_, c]).then_inc(d_raw[i], 16)
                sp.dma_start(stage[DR:P, i, 1, :], w_qkv[D_, c]).then_inc(d_raw[i], 16)
            sp.dma_start(wo[:], w_o).then_inc(d_wo, 16)
            for i in range(3):
                c = slice(i * WT, (i + 1) * WT)
                sp.wait_ge(w_hi, 2 * (i + 1))
                sp.wait_ge(w_lo, 2 * (i + 1))
                sp.dma_start(stage[:, i, 0, :], w_ffn[A_, c]).then_inc(d_raw[i], 16)
                sp.dma_start(stage[0:DR, i, 1, :], w_ffn[D_, c]).then_inc(d_raw[i], 16)
                sp.dma_start(stage[DR:P, i, 1, :], w_ffn[D_, c]).then_inc(d_raw[i], 16)
            sp.dma_start(gate_raw[:, 0, :], w_gate[A_, :]).then_inc(d_gate, 16)
            sp.dma_start(gate_raw[0:DR, 1, :], w_gate[D_, :]).then_inc(d_gate, 16)
            sp.dma_start(gate_raw[DR:P, 1, :], w_gate[D_, :]).then_inc(d_gate, 16)
            sp.dma_start(w2[:], w_2).then_inc(d_w2, 16)
            sp.wait_ge(tok_done.sem, tok_done.at(0, NT))
            sp.dma_start(xg[:], xt[1]).then_inc(x_loaded, 16)

            def store_group(g):
                sp.wait_ge(y_kept.sem, y_kept.at(g, 2))
                for i in range(2):
                    dst = out[bass.ds(g * IMG, IMG), 1:1 + NQ, :].rearrange(
                        "(t i) q n -> i q t n", i=2)[i]
                    sp.dma_start(dst, h1[i * NQ:(i + 1) * NQ, :, :]).then_inc(stored, 16)

            with sp.Fori(0, NG - 2) as g:
                sp.wait_ge(tok_done.sem, tok_done.at(g + 1, NT))
                sp.dma_start(xg[:], xt[bass.ds(g + 2, 1)].rearrange("a p c t -> (a p) c t")
                             ).then_inc(x_loaded, 16)
                store_group(g)
            for g in range(NG - 2, NG):
                store_group(g)
            sp.wait_ge(c_dve, 15)
            sp.dma_start(out[:, 0, :].rearrange("(a b) n -> a b n", a=1),
                         c_out[:].unsqueeze(1).to_broadcast([1, NG * IMG, D])).then_inc(stored, 16)
            sp.wait_ge(stored, 32 + NG * 32 + 16)

        @block.gpsimd
        def _(pool):
            steps = [0]

            def step(ins, at=None):
                ins.then_inc(pool_step, 1)
                steps[0] += 1
                pool.wait_ge(pool_step, steps[0] if at is None else at)

            nc.gpsimd.memset(ones[:], 1.0)
            nc.gpsimd.memset(power[:], -0.5)
            nc.gpsimd.memset(eps[:], LN_EPS)
            nc.gpsimd.memset(ones_row[:], 1.0)
            nc.gpsimd.memset(vblk, 0.0)
            nc.gpsimd.memset(cw[:], 0.0)
            nc.gpsimd.memset(pcls[:], 0.0)
            nc.gpsimd.memset(const_row[:], 0.0)
            nc.gpsimd.memset(earlier[:], 1.0)
            nc.gpsimd.memset(causal[:], HUGE)
            step(nc.gpsimd.memset(ident[:], 0.0))
            step(nc.gpsimd.affine_select(out=ident[:], in_=ident[:], compare_op=ALU.not_equal, fill=1.0,
                                         base=0, pattern=[[-1, P]], channel_multiplier=1))
            nc.gpsimd.memset(const_row[:, CB:CB + 1], 1.0)
            step(nc.gpsimd.memset(pcls[:, :, :, CB:CB + 1].rearrange("p a b c -> p (a b) c"), 1.0))
            for h in range(2):
                m = causal[h * NQ:(h + 1) * NQ, 0:NQ]
                step(nc.gpsimd.affine_select(out=m, in_=m, compare_op=ALU.is_ge, fill=IGNORE,
                                             base=0, pattern=[[-1, NQ]], channel_multiplier=1))
            nc.gpsimd.affine_select(out=earlier[:], in_=earlier[:], compare_op=ALU.is_ge, fill=0.0,
                                    base=-1, pattern=[[1, NR], [-1, NR]], channel_multiplier=0)
            oh = s[0:40].rearrange("p a b -> p (a b)")[:, 0:NR * P].rearrange("p (e n) -> p e n", e=NR)
            step(nc.gpsimd.memset(oh, 0.0))
            step(nc.gpsimd.affine_select(out=oh, in_=oh, compare_op=ALU.not_equal, fill=1.0, base=0,
                                         pattern=[[-1, NR], [0, P]], channel_multiplier=1))
            step(nc.gpsimd.affine_select(out=oh, in_=oh, compare_op=ALU.not_equal, fill=1.0, base=-32,
                                         pattern=[[-1, NR], [0, P]], channel_multiplier=1))
            nc.gpsimd.tensor_copy(onehot[:], oh).then_inc(consts, 1)

            def rstd(var, done, at=None):
                step(nc.gpsimd.tensor_tensor(var, var, eps[0:var.shape[0], 0:var.shape[1]], ALU.add), at)
                nc.gpsimd.tensor_tensor(var, var, power[0:var.shape[0], 0:var.shape[1]], ALU.pow
                                        ).then_inc(done, 1)

            pool.wait_ge(c_dve, 2)
            rstd(c_mv[:, 1:2], c_pool)
            pool.wait_ge(ln1.sem, ln1.at(0, 2 * NT))
            rstd(mv1[:, :, 1], rstd1.sem)

            for i in range(3):
                c = slice(i * WT, (i + 1) * WT)
                pool.wait_ge(d_raw[i], 96)
                for n, w in enumerate((ffn_a, ffn_d)):
                    nc.gpsimd.tensor_copy(w[:, 0, c], stage[:, i, n, :]).then_inc(f_hi, 1)
                    pool.wait_ge(f_hi, 2 * i + n + 1)
                    nc.gpsimd.tensor_tensor(w[:, 1, c], stage[:, i, n, :], w[:, 0, c].bitcast(F32),
                                            ALU.subtract).then_inc(f_lo, 1)
            pool.wait_ge(d_gate, 48)
            for n, w in enumerate((gate_a, gate_d)):
                nc.gpsimd.tensor_copy(w[:, 0, :], gate_raw[:, n, :]).then_inc(f_hi, 1)
                pool.wait_ge(f_hi, 7 + n)
                nc.gpsimd.tensor_tensor(w[:, 1, :], gate_raw[:, n, :], w[:, 0, :].bitcast(F32),
                                        ALU.subtract).then_inc(f_lo, 1)

            def group(g):
                for t in range(NT):
                    b = t % 2
                    pool.wait_ge(s_sum.sem, s_sum.at(g, 2 * t + 2))
                    if t >= 2:
                        pool.wait_ge(p_turned.sem, p_turned.at(g, 2 * (t - 2) + 2))
                    pr = s[:, b, :].rearrange("p (n c) -> p n c", c=NK)
                    r = rsum[:, b, :]
                    nc.gpsimd.tensor_tensor(pn[:, b], pr[:, :, 0:NQ],
                                            r.unsqueeze(2).to_broadcast([P, 2 * HP, NQ]), ALU.mult)
                    nc.gpsimd.tensor_tensor(
                        pcls[:, b, :, 0:HP].rearrange("p i j -> p j i"),
                        pr[:, :, NQ].rearrange("p (j i) -> p j i", i=2),
                        r.rearrange("p (j i) -> p j i", i=2), ALU.mult).then_inc(p_done.sem, 1)

            ahead = steps[0]

            def rstd2_of(g, at):
                pool.wait_ge(ln2.sem, ln2.at(g, 2 * NT))
                rstd(mv2[:, :, 1], rstd2.sem, at)

            with pool.Fori(0, NG - 1) as g:
                group(g)
                rstd2_of(g, g * 2 + (ahead + 1))
                pool.wait_ge(ln1.sem, ln1.at(g + 1, 2 * NT))
                rstd(mv1[:, :, 1], rstd1.sem, g * 2 + (ahead + 2))
            group(NG - 1)
            pool.wait_ge(c_dve, 9)
            rstd(c_mv[:, 1:2], c_pool, 2 * (NG - 1) + ahead + 1)
            rstd2_of(NG - 1, 2 * (NG - 1) + ahead + 2)

        @block.tensor
        def _(pe):
            def embed(g):
                pe.wait_ge(x_loaded, (g + 1) * 16)
                for t in range(NT):
                    for c in range(KC):
                        mm = pe.matmul(bank[4 + t][:, 0:D], xg[:, c, t * P:(t + 1) * P], wproj[:, c, :],
                                       start=(c == 0), stop=(c == KC - 1))
                    mm.then_inc(tok_done.sem, 1)

            def turn(g, normal, turned, to_a, to_d):
                for t in range(NT):
                    pe.wait_ge(normal.sem, normal.at(g, t + 1))
                    a = pe.transpose(to_a[:, t * P:(t + 1) * P], xn[:, t, 0:P], ident[:])
                    if t == NT - 1:
                        a.then_inc(turned.sem, 1)
                    d = pe.transpose(to_d[:, t * P:(t + 1) * P], xn[:, t, P:2 * P], ident[:])
                d.then_inc(turned.sem, 1)

            def qkv(g):
                ring = [bank[0], bank[1], bank[6], bank[7]]
                pe.wait_ge(x1_hi.sem, x1_hi.at(g, 2))
                pe.wait_ge(x1_lo.sem, x1_lo.at(g, 2))
                for n in range(NQKV):
                    if n >= 4:
                        pe.wait_ge(qkv_kept.sem, qkv_kept.at(g, n - 3))
                    dst = ring[n % 4]
                    if n < 2 * HP:
                        parts = split_products(xa_hi[:], xa_lo[:], xd[:], qkv_a, qkv_d,
                                               slice(n * P, (n + 1) * P))
                        for i, (x, w) in enumerate(parts):
                            mm = pe.matmul(dst[:], w, x, start=(i == 0), stop=(i == 4))
                    else:
                        t, half = divmod(n - 2 * HP, 2)
                        tok = slice(t * P, (t + 1) * P)
                        c0 = 2 * HD + half * (HD // 2)
                        parts = split_products(xa_hi[:, tok], xa_lo[:, tok], xd[:, tok], qkv_a, qkv_d,
                                               slice(c0, c0 + HD // 2))
                        for i, (x, w) in enumerate(parts):
                            mm = pe.matmul(dst[:, 0:HD // 2], x, w, start=(i == 0), stop=(i == 4))
                    mm.then_inc(qkv_done.sem, 1)

            def scores(g, t):
                dst = (bank[2], bank[3]) if t % 2 == 0 else (bank[0], bank[1])
                if t == 0:
                    wait_apart(pe, qkv_kept.sem, qkv_kept.at(g, 2 * HP))
                    wait_apart(pe, y_kept.sem, y_kept.at(g, 0))
                if t == 1:
                    wait_apart(pe, qkv_kept.sem, qkv_kept.at(g, NQKV))
                for j in range(HP):
                    if t >= 2 and j % NH2 == 0:
                        wait_apart(pe, s_masked.sem, s_masked.at(g, 2 * (t - 2) + j // NH2 + 1))
                    for i in range(2):
                        c0 = ((j % NH2) * 2 + i) * NK
                        for h in range(2):
                            hs = slice(h * DH, (h + 1) * DH)
                            mm = pe.matmul(dst[j // NH2][hs, c0:c0 + NK], q[hs, j, t, i * NQ:(i + 1) * NQ],
                                           k[hs, j, 2 * t + i, :], start=True, stop=True)
                    if j % NH2 == NH2 - 1:
                        mm.then_inc(s_done.sem, 1)

            def turn_p(g, t):
                pe.wait_ge(p_done.sem, p_done.at(g, t + 1))
                for half in range(2):
                    if t >= 1:
                        pe.wait_ge(p_kept.sem, p_kept.at(g, 2 * (t - 1) + half + 1))
                    for j in range(NH2):
                        jj = half * NH2 + j
                        mm = pe.transpose(bank[4 + half][:, j * P:(j + 1) * P],
                                          pn[:, t % 2, 2 * jj:2 * jj + 2, :].rearrange("p i k -> p (i k)"),
                                          ident[:])
                    if half == 0:
                        for h in range(2):
                            hs = slice(h * NQ, (h + 1) * NQ)
                            for i in range(2):
                                c0 = NH2 * P + i * NQ
                                mm = pe.matmul(bank[4][h * 32:(h + 1) * 32, c0:c0 + NQ],
                                               pcls[hs, t % 2, i, :], ident[hs, hs], start=True, stop=True)
                    mm.then_inc(p_turned.sem, 1)

            def values(g, t):
                if t == 0:
                    wait_apart(pe, qkv_kept.sem, qkv_kept.at(g, NQKV))
                else:
                    wait_apart(pe, z_kept.sem, z_kept.at(g, 2 * t))
                for j in range(HP):
                    if j % NH2 == 0:
                        wait_apart(pe, p_kept.sem, p_kept.at(g, 2 * t + j // NH2 + 1))
                    for h in range(2):
                        for i in range(2):
                            ks = slice(i * NQ, (i + 1) * NQ)
                            mm = pe.matmul(bank[6 + i][h * DH:(h + 1) * DH, j * NQ:(j + 1) * NQ],
                                           v[ks, t, (2 * j + h) * DH:(2 * j + h + 1) * DH],
                                           pt[ks, t % 2, j, h * NQ:(h + 1) * NQ], start=True, stop=True)
                            if j == HP - 1 and h == 1:
                                mm.then_inc(z_done.sem, 1)

            def project(g, t):
                pe.wait_ge(z_kept.sem, z_kept.at(g, 2 * t + 2))
                for j in range(HP):
                    pe.matmul(bank[t][:, 0:D], q[:, j, t, :], wo[:, j, :], start=(j == 0), stop=False)
                pe.matmul(bank[t][:, 0:D], pct[:, t, :], vw[:], start=False, stop=True
                          ).then_inc(wo_done.sem, 1)

            def gate(g):
                pe.wait_ge(x2_hi.sem, x2_hi.at(g, 2))
                pe.wait_ge(x2_lo.sem, x2_lo.at(g, 2))
                for t in range(NT):
                    tok = slice(t * P, (t + 1) * P)
                    dst = bank[2][:, t * 2 * NR:(t + 1) * 2 * NR]
                    for i, (x, w) in enumerate(((xa_hi, gate_a), (xa_lo, gate_a), (xd, gate_d))):
                        mm = pe.matmul(dst, x[:, tok], w[:].rearrange("p a e -> p (a e)"),
                                       start=(i == 0), stop=(i == 2))
                mm.then_inc(gate_done.sem, 1)

            def experts(g):
                for c, e in enumerate([NR] + list(range(NR))):
                    if c == 0:
                        pe.wait_ge(h0_done.sem, h0_done.at(g + 1, NT) if not last(g) else h0_done.at(NG - 1, NT))
                    for n, done in ((0, f1_done), (1, f3_done)):
                        if c >= 2:
                            if n == 0:
                                pe.wait_ge(silu_done.sem, silu_done.at(g, c - 1))
                            else:
                                pe.wait_ge(f_prod.sem, f_prod.at(g, c - 1))
                        c0 = (2 * e + n) * P
                        parts = split_products(xa_hi[:], xa_lo[:], xd[:], ffn_a, ffn_d, slice(c0, c0 + P))
                        for i, (x, w) in enumerate(parts):
                            mm = pe.matmul(bank[4 + 2 * n + c % 2][:], w, x, start=(i == 0), stop=(i == 4))
                        if n == 0:
                            mm.then_inc(done.sem, 1)
                    if c == 0:
                        mm.then_inc(f3_done.sem, 1)
                    if c == 1:
                        pe.wait_ge(gate_step.sem, gate_base(g, NGS))
                        for t in range(NT):
                            mm = pe.matmul(bank[3][0:40, t * P:(t + 1) * P], cw[:, t, :], ident[:],
                                           start=True, stop=True)
                        mm.then_inc(cw_turned.sem, 1)
                        pe.wait_ge(cw_hi.sem, cw_hi.at(g, 1))
                        pe.wait_ge(cw_lo.sem, cw_lo.at(g, 1))
                    if c >= 1:
                        if c >= 3:
                            pe.wait_ge(f_hid.sem, f_hid.at(g, c - 2))
                        pe.matmul(bank[c % 2][:], onehot[:, e, :], cwt[:], start=True, stop=True
                                  ).then_inc(f3_done.sem, 1)

            def down(g):
                order = [NR] + list(range(NR))
                for t in range(NT):
                    dst = bank[2 + t // 2][:, (t % 2) * D:(t % 2 + 1) * D]
                    for n, e in enumerate(order):
                        if t == 0 and n == 0:
                            pe.wait_ge(f_prod.sem, f_prod.at(g, 1))
                        if t == 0 and n >= 1:
                            pe.wait_ge(f_hid.sem, f_hid.at(g, n))
                        mm = pe.matmul(dst, hid[:, e, t * P:(t + 1) * P], w2[:, e, :],
                                       start=(n == 0), stop=(n == NE - 1))
                    if t % 2 == 1:
                        mm.then_inc(y_done.sem, 1)

            def last(g):
                return isinstance(g, int) and g == NG - 1

            def gate_base(g, n):
                return gate_step.at(g, n) + (NGS if last(g) else 0)

            def class_columns(n):
                pe.matmul(bank[n][:, 0:2], c_xn[:, 0:P], ones[0:1, :], start=True, stop=True)
                pe.matmul(bank[n][:, 2:4], c_xn[:, P:2 * P], ones[0:1, :], start=True, stop=True
                          ).then_inc(c_pe, 1)

            def class_products(dst, w_a, w_d, first, count):
                for n in range(count):
                    parts = split_products(c_a_hi[:], c_a_lo[:], c_d[:], w_a, w_d,
                                           slice((first + n) * P, (first + n + 1) * P))
                    for i, (x, w) in enumerate(parts):
                        mm = pe.matmul(dst[:, 2 * n:2 * n + 2], w, x, start=(i == 0), stop=(i == 4))
                return mm

            pe.wait_ge(consts, 1)
            pe.wait_ge(d_proj, 16)
            embed(0)
            turn(0, xn1, x1_turned, bank[2], bank[3])
            pe.wait_ge(c_dve, 3)
            class_columns(0)
            pe.wait_ge(c_act, 2)
            pe.wait_ge(c_dve, 4)
            pe.wait_ge(w_hi, 6)
            pe.wait_ge(w_lo, 6)
            class_products(bank[1], qkv_a, qkv_d, HP, 2 * HP).then_inc(c_pe, 1)
            pe.wait_ge(d_wo, 16)
            pe.wait_ge(d_small, 96)
            pe.wait_ge(c_dve, 6)
            for j in range(HP):
                pe.matmul(bank[6][0:VR, 0:D], vblk[:, j, :], wo[:, j, :], start=(j == 0), stop=False)
            pe.matmul(bank[6][0:VR, 0:D], const_row[:], bo[:], start=False, stop=True).then_inc(c_pe, 1)
            pe.wait_ge(c_act, 3)
            pe.matmul(bank[7][0:1, 0:D], ones[0:VR, 0:1], vw[:], start=True, stop=True).then_inc(c_pe, 1)
            pe.wait_ge(c_dve, 7)

            def attention(g):
                qkv(g)
                for t in range(NT):
                    scores(g, t)
                turn_p(g, 0)
                for t in range(NT):
                    if t + 1 < NT:
                        turn_p(g, t + 1)
                    values(g, t)
                for t in range(NT):
                    project(g, t)

            with pe.Fori(0, NG - 1) as g:
                attention(g)
                embed(g + 1)
                turn(g, xn2, x2_turned, bank[0], bank[1])
                pe.wait_ge(f_lo, 8)
                gate(g)
                experts(g)
                pe.wait_ge(silu_done.sem, silu_done.at(g, NE))
                turn(g + 1, xn1, x1_turned, bank[4], bank[5])
                pe.wait_ge(d_w2, 16)
                down(g)

            g = NG - 1
            attention(g)
            pe.wait_ge(c_dve, 10)
            class_columns(4)
            pe.wait_ge(c_act, 5)
            pe.wait_ge(c_dve, 11)
            for i, (x, w) in enumerate(((c_a_hi, gate_a), (c_a_lo, gate_a), (c_d, gate_d))):
                mm = pe.matmul(bank[5][0:1, 0:2 * NR], x[:, 0:1],
                               w[:].rearrange("p a e -> p (a e)"), start=(i == 0), stop=(i == 2))
            mm.then_inc(c_pe, 1)
            class_products(bank[6], ffn_a, ffn_d, 0, 2 * NE).then_inc(c_pe, 1)
            turn(g, xn2, x2_turned, bank[0], bank[1])
            gate(g)
            pe.wait_ge(gate_step.sem, gate_step.at(g, NGS))
            pe.matmul(bank[7][:, 0:NR], ones_row[:], cw[0:1, 0, 0:NR], start=True, stop=True
                      ).then_inc(c_pe, 1)
            pe.wait_ge(c_dve, 14)
            for e in range(NE):
                mm = pe.matmul(bank[7][0:1, 256:256 + D], c_hid[:, e:e + 1], w2[:, e, :],
                               start=(e == 0), stop=(e == NE - 1))
            mm.then_inc(c_pe, 1)
            pe.wait_ge(c_dve, 15)
            experts(g)
            down(g)

        @block.scalar
        def _(act):
            def split_hi(g, turned, hi, from_a, from_d):
                act.wait_ge(turned.sem, turned.at(g, 1))
                nc.scalar.copy(xa_hi[:], from_a[:]).then_inc(hi.sem, 1)
                act.wait_ge(turned.sem, turned.at(g, 2))
                nc.scalar.copy(xd[:], from_d[:]).then_inc(hi.sem, 1)

            def keep_qkv(g):
                ring = [bank[0], bank[1], bank[6], bank[7]]
                for n in range(NQKV):
                    act.wait_ge(qkv_done.sem, qkv_done.at(g, n + 1))
                    src = ring[n % 4]
                    if n < HP:
                        ins = nc.scalar.activation(q[:, n].rearrange("p t c -> p (t c)"), src[:], ACT.Identity,
                                                   bias=bq[:, n:n + 1])
                    elif n < 2 * HP:
                        ins = nc.scalar.activation(k[:, n - HP, :, 0:NQ],
                                                   src[:].rearrange("p (m c) -> p m c", c=NQ), ACT.Identity,
                                                   bias=bk[:, n - HP:n - HP + 1])
                    else:
                        t, half = divmod(n - 2 * HP, 2)
                        ins = nc.scalar.copy(v[:, t, half * (HD // 2):(half + 1) * (HD // 2)],
                                             src[:, 0:HD // 2])
                    ins.then_inc(qkv_kept.sem, 1)

            def exp(g, t):
                act.wait_ge(s_shifted.sem, s_shifted.at(g, t + 1))
                nc.scalar.activation(s[:, t % 2, :], s[:, t % 2, :], ACT.Exp).then_inc(s_exp.sem, 1)

            def keep_p(g, t):
                for half in range(2):
                    act.wait_ge(p_turned.sem, p_turned.at(g, 2 * t + half + 1))
                    if half == 0:
                        nc.scalar.copy(pct[:, t, :], bank[4][0:VR, NH2 * P:(NH2 + 1) * P])
                    nc.scalar.copy(pt[:, t % 2, half * NH2:(half + 1) * NH2, :].rearrange("p j c -> p (j c)"),
                                   bank[4 + half][:, 0:NH2 * P]).then_inc(p_kept.sem, 1)

            def keep_z(g, t):
                for i in range(2):
                    act.wait_ge(z_done.sem, z_done.at(g, 2 * t + i + 1))
                    nc.scalar.copy(q[:, :, t, i * NQ:(i + 1) * NQ],
                                   bank[6 + i][:, 0:HP * NQ].rearrange("p (j c) -> p j c", c=NQ)
                                   ).then_inc(z_kept.sem, 1)

            def attention(g):
                keep_qkv(g)
                exp(g, 0)
                exp(g, 1)
                keep_p(g, 0)
                exp(g, 2)
                keep_p(g, 1)
                keep_z(g, 0)
                exp(g, 3)
                keep_p(g, 2)
                keep_z(g, 1)
                keep_p(g, 3)
                keep_z(g, 2)
                keep_z(g, 3)

            def experts(g):
                act.wait_ge(gate_step.sem, gate_base(g, 2))
                nc.scalar.activation(g_sc[:], g_sc[:], ACT.Exp, scale=-1.0).then_inc(g_exp.sem, 1)
                for c in range(NE):
                    act.wait_ge(f1_done.sem, f1_done.at(g, c + 1))
                    if c >= 2:
                        act.wait_ge(f_hid.sem, f_hid.at(g, c - 2)) if c >= 3 else act.wait_ge(
                            f_prod.sem, f_prod.at(g, 1))
                    nc.scalar.activation(silu[:, c % 2, :], bank[4 + c % 2][:], ACT.Silu
                                         ).then_inc(silu_done.sem, 1)
                    if c == 1:
                        act.wait_ge(cw_turned.sem, cw_turned.at(g, 1))
                        nc.scalar.copy(cwt[:], bank[3][0:40, :]).then_inc(cw_hi.sem, 1)

            def last(g):
                return isinstance(g, int) and g == NG - 1

            def gate_base(g, n):
                return gate_step.at(g, n) + (NGS if last(g) else 0)

            for i in range(3):
                c = slice(i * WT, (i + 1) * WT)
                act.wait_ge(d_raw[i], 48)
                for n, w in enumerate((qkv_a, qkv_d)):
                    nc.scalar.copy(w[:, 0, c], stage[:, i, n, :]).then_inc(w_hi, 1)
            split_hi(0, x1_turned, x1_hi, bank[2], bank[3])
            act.wait_ge(c_pe, 1)
            nc.scalar.copy(c_a_hi[:], bank[0][:, 0:2]).then_inc(c_act, 1)
            nc.scalar.copy(c_d[:], bank[0][:, 2:4]).then_inc(c_act, 1)
            act.wait_ge(c_pe, 3)
            nc.scalar.copy(vw[:], bank[6][0:VR, 0:D]).then_inc(c_act, 1)

            act.wait_ge(d_small, 96)
            with act.Fori(0, NG - 1) as g:
                attention(g)
                split_hi(g, x2_turned, x2_hi, bank[0], bank[1])
                experts(g)
                split_hi(g + 1, x1_turned, x1_hi, bank[4], bank[5])

            g = NG - 1
            attention(g)
            act.wait_ge(c_pe, 5)
            nc.scalar.copy(c_a_hi[:], bank[4][:, 0:2]).then_inc(c_act, 1)
            nc.scalar.copy(c_d[:], bank[4][:, 2:4]).then_inc(c_act, 1)
            act.wait_ge(gate_step.sem, gate_step.at(g, 2))
            nc.scalar.activation(g_sc[0:1, 0, :], g_sc[0:1, 0, :], ACT.Exp, scale=-1.0).then_inc(c_act, 1)
            split_hi(g, x2_turned, x2_hi, bank[0], bank[1])
            act.wait_ge(c_pe, 7)
            nc.scalar.activation(silu[:, 0, 0:NE],
                                 bank[6][:, 0:4 * NE].rearrange("p (e n) -> p e n", n=4)[:, :, 0],
                                 ACT.Silu).then_inc(c_act, 1)
            experts(g)

        @block.vector
        def _(dve):
            def split_lo(g, hi, lo, from_a, from_d):
                dve.wait_ge(hi.sem, hi.at(g, 1))
                nc.vector.tensor_tensor(xa_lo[:], from_a[:], xa_hi[:].bitcast(F32), ALU.subtract
                                        ).then_inc(lo.sem, 1)
                dve.wait_ge(hi.sem, hi.at(g, 2))
                nc.vector.tensor_tensor(xd[DR:P, :], from_d[DR:P, :], xd[DR:P, :].bitcast(F32),
                                        ALU.subtract).then_inc(lo.sem, 1)

            def keep_h0(g):
                for t in range(NT):
                    dve.wait_ge(tok_done.sem, tok_done.at(g, t + 1))
                    nc.vector.tensor_tensor(h0[:, t, :], bank[4 + t][:, 0:D], bproj[:], ALU.add
                                            ).then_inc(h0_done.sem, 1)
                for t in range(NT):
                    dve.wait_ge(h0_done.sem, h0_done.at(g, t + 1))
                    nc.vector.bn_stats(stats1[:, t, :], h0[:, t, :]).then_inc(ln1.sem, 1)

            def keep_h1(g):
                for t in range(NT):
                    dve.wait_ge(wo_done.sem, wo_done.at(g, t + 1))
                    if t == 0:
                        dve.wait_ge(y_stored.sem, y_stored.at(g, 0))
                    nc.vector.tensor_tensor(h1[:, t, :], bank[t][:, 0:D], h0[:, t, :], ALU.add
                                            ).then_inc(h1_done.sem, 1)
                    dve.wait_ge(h1_done.sem, h1_done.at(g, t + 1))
                    nc.vector.bn_stats(stats2[:, t, :], h1[:, t, :]).then_inc(ln2.sem, 1)

            def normalise(g, h, stats, mv, ln, rstd, normal):
                wait_apart(dve, ln.sem, ln.at(g, NT))
                for t in range(NT):
                    nc.vector.bn_aggr(mv[:, t, :], stats[:, t, :]).then_inc(ln.sem, 1)
                dve.wait_ge(rstd.sem, rstd.at(g, 1))
                for t in range(NT):
                    m, r = mv[:, t, 0:1], mv[:, t, 1:2]
                    nc.vector.tensor_scalar(xn[:, t, 0:P], h[:, t, 0:P], m, r, ALU.subtract, ALU.mult)
                    nc.vector.tensor_scalar(
                        xn[:, t, P:2 * P].rearrange("p (a b) -> p a b", a=2),
                        h[:, t, P:D].unsqueeze(1).to_broadcast([P, 2, DR]), m, r,
                        ALU.subtract, ALU.mult).then_inc(normal.sem, 1)

            def class_norm(row, n):
                nc.vector.bn_stats(c_stats[:], row[:]).then_inc(c_dve, 1)
                dve.wait_ge(c_dve, n + 1)
                nc.vector.bn_aggr(c_mv[:], c_stats[:]).then_inc(c_dve, 1)
                dve.wait_ge(c_pool, 1 if n == 0 else 2)
                m, r = c_mv[:, 0:1], c_mv[:, 1:2]
                nc.vector.tensor_scalar(c_xn[:, 0:P], row[:, 0:P], m, r, ALU.subtract, ALU.mult)
                nc.vector.tensor_scalar(c_xn[:, P:2 * P].rearrange("p (a b) -> p a b", a=2),
                                        row[:, P:D].unsqueeze(1).to_broadcast([1, 2, DR]), m, r,
                                        ALU.subtract, ALU.mult).then_inc(c_dve, 1)

            def masked_scores(g, t):
                b = t % 2
                src = (bank[2], bank[3]) if b == 0 else (bank[0], bank[1])
                if t >= 2:
                    dve.wait_ge(p_done.sem, p_done.at(g, t - 1))
                half_c = NH2 * SC
                for half in range(2):
                    dve.wait_ge(s_done.sem, s_done.at(g, 2 * t + half + 1))
                    nc.vector.scalar_tensor_tensor(
                        out=s[:, b, half * half_c:(half + 1) * half_c].rearrange("p (n c) -> p n c", c=NK),
                        in0=src[half][:, 0:half_c].rearrange("p (n c) -> p n c", c=NK),
                        scalar=float(DH) ** -0.5,
                        in1=causal[:].unsqueeze(1).to_broadcast([P, 2 * NH2, NK]),
                        op0=ALU.mult, op1=ALU.min).then_inc(s_masked.sem, 1)
                sv = s[:, b, :].rearrange("p (n c) -> p n c", c=NK)
                dve.wait_ge(s_masked.sem, s_masked.at(g, 2 * t + 2))
                nc.vector.tensor_reduce(smax[:, b, :], sv, AX_X, ALU.max).then_inc(s_max.sem, 1)
                dve.wait_ge(s_max.sem, s_max.at(g, t + 1))
                nc.vector.tensor_tensor(sv, sv, smax[:, b, :].unsqueeze(2).to_broadcast([P, 2 * HP, NK]),
                                        ALU.subtract).then_inc(s_shifted.sem, 1)

            def sums(g, t):
                b = t % 2
                dve.wait_ge(s_exp.sem, s_exp.at(g, t + 1))
                nc.vector.tensor_reduce(rsum[:, b, :], s[:, b, :].rearrange("p (n c) -> p n c", c=NK),
                                        AX_X, ALU.add).then_inc(s_sum.sem, 1)
                dve.wait_ge(s_sum.sem, s_sum.at(g, 2 * t + 1))
                nc.vector.reciprocal(rsum[:, b, :], rsum[:, b, :]).then_inc(s_sum.sem, 1)

            def route(np, nt, logits, exp_done, at):
                sc, ss, gs = g_sc[0:np, 0:nt], g_s[0:np, 0:nt], g_gs[0:np, 0:nt]
                lg, rank, tot = g_lg[0:np, 0:nt], g_rank[0:np, 0:nt], g_sum[0:np, 0:nt]
                done = [0]

                def step(ins):
                    ins.then_inc(gate_step.sem, 1)
                    done[0] += 1
                    dve.wait_ge(gate_step.sem, at(done[0]))

                def ranks(val, n, dst):
                    cmp, eq = g_cmp[0:np, 0:nt, 0:n, 0:n], g_eq[0:np, 0:nt, 0:n, 0:n]
                    for t in range(nt):
                        vi = val[:, t].unsqueeze(1).to_broadcast([np, n, n])
                        vj = val[:, t].unsqueeze(2).to_broadcast([np, n, n])
                        nc.vector.tensor_tensor(cmp[:, t], vi, vj, ALU.is_gt)
                        last = nc.vector.tensor_tensor(eq[:, t], vi, vj, ALU.is_equal)
                    step(last)
                    step(nc.vector.tensor_tensor(
                        eq, eq, earlier[0:np, 0:n, 0:n].unsqueeze(1).to_broadcast([np, nt, n, n]), ALU.mult))
                    step(nc.vector.tensor_tensor(cmp, cmp, eq, ALU.add))
                    step(nc.vector.tensor_reduce(dst, cmp, AX_X, ALU.add))

                step(nc.vector.tensor_copy(lg, logits))
                step(nc.vector.tensor_tensor(sc, lg[:, :, 0:NR], lg[:, :, NR:2 * NR], ALU.add))
                exp_done()
                step(nc.vector.tensor_scalar(sc, sc, 1.0, None, ALU.add))
                step(nc.vector.reciprocal(sc, sc))
                step(nc.vector.tensor_tensor(
                    ss, sc, gbias[0:np].unsqueeze(1).to_broadcast([np, nt, NR]), ALU.add))
                pairs = ss.rearrange("p t (a b) -> p t a b", b=2)
                step(nc.vector.tensor_tensor(gs, pairs[:, :, :, 0], pairs[:, :, :, 1], ALU.add))
                ranks(gs, NGRP, rank[:, :, 0:NGRP])
                step(nc.vector.tensor_scalar(gs, rank[:, :, 0:NGRP], 1.5, None, ALU.is_lt))
                step(nc.vector.tensor_tensor(pairs, pairs,
                                             gs.unsqueeze(3).to_broadcast([np, nt, NGRP, 2]), ALU.mult))
                step(nc.vector.tensor_scalar(gs, gs, 1.0, HUGE, ALU.subtract, ALU.mult))
                step(nc.vector.tensor_tensor(pairs, pairs,
                                             gs.unsqueeze(3).to_broadcast([np, nt, NGRP, 2]), ALU.add))
                ranks(ss, NR, rank)
                step(nc.vector.scalar_tensor_tensor(out=ss, in0=rank, scalar=1.5, in1=sc,
                                                    op0=ALU.is_lt, op1=ALU.mult))
                step(nc.vector.tensor_reduce(tot, ss, AX_X, ALU.add))
                step(nc.vector.tensor_scalar(tot, tot, SUM_EPS, None, ALU.add))
                nc.vector.reciprocal(tot, tot).then_inc(gate_step.sem, 1)
                done[0] += 1
                return done[0], ss, tot

            def weights(np, nt, ss, tot):
                for c in (0, 32):
                    ins = nc.vector.tensor_tensor(cw[0:np, 0:nt, c:c + NR], ss,
                                                  tot.unsqueeze(2).to_broadcast([np, nt, NR]), ALU.mult)
                return ins

            def last(g):
                return isinstance(g, int) and g == NG - 1

            def gate_base(g, n):
                return gate_step.at(g, n) + (NGS if last(g) else 0)

            def gating(g):
                dve.wait_ge(gate_done.sem, gate_done.at(g, 1))
                n, ss, tot = route(
                    P, NT, bank[2][:, 0:2 * NR * NT].rearrange("p (t c) -> p t c", t=NT),
                    lambda: dve.wait_ge(g_exp.sem, g_exp.at(g, 1)), lambda n: gate_base(g, n))
                assert n + 1 == NGS, n
                dve.wait_ge(gate_step.sem, gate_base(g, n))
                weights(P, NT, ss, tot).then_inc(gate_step.sem, 1)
                dve.wait_ge(cw_turned.sem, cw_turned.at(g, 1))
                dve.wait_ge(cw_hi.sem, cw_hi.at(g, 1))
                nc.vector.tensor_tensor(cwt[32:40, :], bank[3][32:40, :], cwt[32:40, :].bitcast(F32),
                                        ALU.subtract).then_inc(cw_lo.sem, 1)

            def product(g, c, e):
                dve.wait_ge(silu_done.sem, silu_done.at(g, c + 1))
                dve.wait_ge(f3_done.sem, f3_done.at(g, c + 1))
                dst = hid[:, e, :] if c == 0 else silu[:, c % 2, :]
                nc.vector.tensor_tensor(dst, bank[6 + c % 2][:], silu[:, c % 2, :], ALU.mult
                                        ).then_inc(f_prod.sem, 1)
                if c >= 1:
                    dve.wait_ge(f_prod.sem, f_prod.at(g, c + 1))
                    nc.vector.tensor_tensor(hid[:, e, :], bank[c % 2][:], silu[:, c % 2, :], ALU.mult
                                            ).then_inc(f_hid.sem, 1)

            def keep_y(g):
                for half in range(2):
                    dve.wait_ge(y_done.sem, y_done.at(g, half + 1))
                    hh = h1[:, 2 * half:2 * half + 2, :]
                    nc.vector.tensor_tensor(hh, bank[2 + half][:, 0:2 * D].rearrange("p (t n) -> p t n", t=2),
                                            hh, ALU.add).then_inc(y_kept.sem, 1)

            nc.vector.memset(mv1[:], 0.0).then_inc(y_kept.sem, 2)
            nc.vector.memset(mv2[:], 0.0).then_inc(stored, 32)
            dve.wait_ge(d_cls, 16)
            class_norm(c_row, 0)
            dve.wait_ge(d_small, 96)
            keep_h0(0)
            normalise(0, h0, stats1, mv1, ln1, rstd1, xn1)
            for i in range(3):
                c = slice(i * WT, (i + 1) * WT)
                for n, w in enumerate((qkv_a, qkv_d)):
                    dve.wait_ge(w_hi, 2 * i + n + 1)
                    nc.vector.tensor_tensor(w[:, 1, c], stage[:, i, n, :], w[:, 0, c].bitcast(F32),
                                            ALU.subtract).then_inc(w_lo, 1)
            split_lo(0, x1_hi, x1_lo, bank[2], bank[3])

            def class_lo(b, act_step):
                dve.wait_ge(c_act, act_step)
                nc.vector.tensor_tensor(c_a_lo[:], bank[b][:, 0:2], c_a_hi[:].bitcast(F32), ALU.subtract)
                nc.vector.tensor_tensor(c_d[DR:P, :], bank[b][DR:P, 2:4], c_d[DR:P, :].bitcast(F32),
                                        ALU.subtract).then_inc(c_dve, 1)

            class_lo(0, 2)
            dve.wait_ge(c_pe, 2)
            kv = bank[1][:, 0:4 * HP].rearrange("p (j n) -> p j n", n=2)[:, :, 0]
            nc.vector.tensor_tensor(k[:, :, :, NQ], kv[:, 0:HP].unsqueeze(2).to_broadcast([P, HP, IMG]),
                                    bk[:].unsqueeze(2).to_broadcast([P, HP, IMG]), ALU.add
                                    ).then_inc(c_dve, 1)
            dve.wait_ge(consts, 1)
            flat = vblk.rearrange("p j c -> p (j c)")
            for h in range(2):
                hs = slice(h * DH, (h + 1) * DH)
                nc.vector.tensor_copy(flat[hs, 32 * h:32 * h + (HP - 1) * (VR + 1) + 1:VR + 1],
                                      kv[hs, HP:2 * HP])
            nc.vector.tensor_copy(vblk[:, :, CB], bv[:]).then_inc(c_dve, 1)
            dve.wait_ge(c_pe, 4)
            nc.vector.tensor_tensor(c_h1[:], bank[7][0:1, 0:D], c_row[:], ALU.add).then_inc(c_dve, 1)

            def attention(g):
                masked_scores(g, 0)
                masked_scores(g, 1)
                sums(g, 0)
                masked_scores(g, 2)
                sums(g, 1)
                masked_scores(g, 3)
                sums(g, 2)
                sums(g, 3)
                keep_h1(g)

            with dve.Fori(0, NG - 1) as g:
                attention(g)
                normalise(g, h1, stats2, mv2, ln2, rstd2, xn2)
                keep_h0(g + 1)
                split_lo(g, x2_hi, x2_lo, bank[0], bank[1])
                gating(g)
                for c in range(NE):
                    product(g, c, NR if c == 0 else c - 1)
                    if c == 2:
                        normalise(g + 1, h0, stats1, mv1, ln1, rstd1, xn1)
                split_lo(g + 1, x1_hi, x1_lo, bank[4], bank[5])
                keep_y(g)

            g = NG - 1
            attention(g)
            dve.wait_ge(c_dve, 7)
            class_norm(c_h1, 7)
            normalise(g, h1, stats2, mv2, ln2, rstd2, xn2)
            class_lo(4, 5)
            dve.wait_ge(c_pe, 6)
            n, ss, tot = route(1, 1, bank[5][0:1, 0:2 * NR].rearrange("p (t c) -> p t c", t=1),
                               lambda: dve.wait_ge(c_act, 6), lambda n: gate_step.at(g, n))
            dve.wait_ge(gate_step.sem, gate_step.at(g, n))
            weights(1, 1, ss, tot).then_inc(gate_step.sem, 1)
            split_lo(g, x2_hi, x2_lo, bank[0], bank[1])
            dve.wait_ge(c_pe, 8)
            nc.vector.tensor_copy(c_cw[:], bank[7][:, 0:NR]).then_inc(c_dve, 1)
            dve.wait_ge(c_act, 7)
            nc.vector.tensor_tensor(c_hid[:],
                                    bank[6][:, 0:4 * NE].rearrange("p (e n) -> p e n", n=4)[:, :, 2],
                                    silu[:, 0, 0:NE], ALU.mult).then_inc(c_dve, 1)
            dve.wait_ge(c_dve, 13)
            nc.vector.tensor_tensor(c_hid[:, 0:NR], c_hid[:, 0:NR], c_cw[:], ALU.mult).then_inc(c_dve, 1)
            dve.wait_ge(c_pe, 9)
            nc.vector.tensor_tensor(c_out[:], bank[7][0:1, 256:256 + D], c_h1[:], ALU.add).then_inc(c_dve, 1)
            gating(g)
            for c in range(NE):
                product(g, c, NR if c == 0 else c - 1)
            keep_y(g)


def kernel(x, cls_tok, L0_tok_W_proj, L0_tok_b_proj, L0_attn_W_Q, L0_attn_b_Q, L0_attn_W_K, L0_attn_b_K,
           L0_attn_W_V, L0_attn_b_V, L0_attn_W_O, L0_attn_b_O, L0_ffn_gate_weight, L0_ffn_gate_bias,
           L0_ffn_w1, L0_ffn_w2, L0_ffn_w3, L0_ffn_sw1, L0_ffn_sw2, L0_ffn_sw3):
    import numpy as np
    import concourse.bacc as bacc
    from concourse.bass_utils import run_bass_kernel_spmd

    x = np.asarray(x)
    B, C, H, W = x.shape
    p, groups = 16, 4
    D = L0_tok_W_proj.shape[0]
    nh, _, dh = L0_attn_W_Q.shape
    n = (H // p) * (W // p)
    xt = x.reshape(B, C, H // p, p, W // p, p).transpose(1, 3, 5, 0, 2, 4).reshape(-1, 128, groups, B * n // groups)
    xt = xt.transpose(2, 1, 0, 3)

    def chunks(w):
        return np.asarray(w).reshape(-1, 128, w.shape[-1]).transpose(1, 0, 2)

    def heads_last(w):
        return np.asarray(w).transpose(1, 0, 2).reshape(D, nh * dh)

    def by_pair(b):
        return np.asarray(b).reshape(nh // 2, 2 * dh).T

    w1 = np.concatenate([np.asarray(L0_ffn_w1), np.asarray(L0_ffn_sw1)[None]])
    w3 = np.concatenate([np.asarray(L0_ffn_w3), np.asarray(L0_ffn_sw3)[None]])
    w_ffn = np.stack([w1, w3], 1).transpose(3, 0, 1, 2).reshape(D, -1)
    w_2 = np.concatenate([np.asarray(L0_ffn_w2), np.asarray(L0_ffn_sw2)[None]]).transpose(2, 0, 1)
    arrays = {
        "xt": xt,
        "w_proj": chunks(np.asarray(L0_tok_W_proj).T),
        "w_qkv": np.concatenate([heads_last(w) for w in (L0_attn_W_Q, L0_attn_W_K, L0_attn_W_V)], 1),
        "w_o": chunks(np.asarray(L0_attn_W_O).reshape(nh * dh, D)),
        "w_gate": np.asarray(L0_ffn_gate_weight).T,
        "w_ffn": w_ffn,
        "w_2": w_2,
        "b_proj": np.asarray(L0_tok_b_proj),
        "b_q": by_pair(L0_attn_b_Q),
        "b_k": by_pair(L0_attn_b_K),
        "b_v": by_pair(L0_attn_b_V),
        "b_o": np.asarray(L0_attn_b_O),
        "gate_bias": np.asarray(L0_ffn_gate_bias),
        "cls_tok": np.asarray(cls_tok).reshape(1, D),
    }
    arrays = {name: np.ascontiguousarray(a) for name, a in arrays.items()}
    nc = bacc.Bacc("TRN2", target_bir_lowering=False, num_devices=1, dynamic_dma_scratch_size=1024)
    args = [nc.dram_tensor(name, a.shape, F32, kind="ExternalInput").ap() for name, a in arrays.items()]
    out = nc.dram_tensor("out", (B, n + 1, D), F32, kind="ExternalOutput").ap()
    vit_tower(nc, *args, out)
    r = run_bass_kernel_spmd(nc, [arrays], core_ids=[0])
    return r.results[0]["out"]
```

```python
from contextlib import ExitStack

import concourse.bass as bass
from concourse import mybir

F32 = mybir.dt.float32
F32R = mybir.dt.float32r
ALU = mybir.AluOpType
ACT = mybir.ActivationFunctionType
AX_X = mybir.AxisListType.X

P = 128
HUGE = 3.0e38
IGNORE = -100000.0
LN_EPS = 1e-05
SUM_EPS = 1e-06


class Signal:

    def __init__(self, sem, per_group, before=0):
        self.sem, self.per_group, self.before = sem, per_group, before

    def at(self, g, n):
        return g * self.per_group + (self.before + n)


def vit_tower(nc, xt, w_proj, w_qkv, w_o, w_gate, w_ffn, w_2, b_heads, b_tokens, cls_rows, out):
    NG, _, KC, TG = xt.shape
    D = w_proj.shape[2]
    DR = D - P
    HP = w_o.shape[1]
    DH = 64
    HD = HP * P
    NE = w_2.shape[1]
    NR = NE - 1
    NQ = DH
    NK = NQ + 1
    IMG = TG // NQ
    NT = TG // P
    SC = 2 * NK
    NH2 = HP // 2
    VR = 64
    CB = HP
    NGRP = 4
    assert D == P + DR and DR == 64 and TG == 512 and NQ == 64

    with ExitStack() as ctx:
        def sb(name, shape, dt=F32):
            return ctx.enter_context(nc.sbuf_tensor(name, shape, dt))

        def over(base, first, name, shape, dt=F32):
            return nc.alloc_sbuf_tensor_at(name, shape, dt, offset=base + 4 * first)

        def sem(name):
            return ctx.enter_context(nc.semaphore(name))

        bank = [ctx.enter_context(nc.psum_tensor(f"bank{i}", [P, 512], F32)) for i in range(8)]

        ident = sb("ident", [P, P])
        causal = sb("causal", [P, NK])
        onehot = sb("onehot", [40, NR, P], F32R)
        wproj = sb("wproj", [P, KC, D])
        wo = sb("wo", [P, HP, D])
        w2_base = nc.sbuf_base
        w2 = sb("w2", [P, NE, 2, D], F32R)
        w2_raw = over(w2_base, 0, "w2_raw", [P, NE, 2, D])
        NW = w_qkv.shape[2]
        qkv_a = sb("qkv_a", [P, 2, NW], F32R)
        qkv_d = sb("qkv_d", [P, 2, NW], F32R)
        NF = w_ffn.shape[2]
        ffn_a = sb("ffn_a", [P, 2, NF], F32R)
        ffn_d = sb("ffn_d", [P, 2, NF], F32R)
        gate_a = sb("gate_a", [P, 2, NR], F32R)
        gate_d = sb("gate_d", [P, 2, NR], F32R)
        gate_raw = sb("gate_raw", [P, 2, NR])
        btok = sb("btok", [P, D + NR])
        bproj, gbias = btok[:, 0:D], btok[:, D:D + NR]
        bheads = sb("bheads", [P, 3, HP])
        bq, bk, bv = (bheads[:, n, :] for n in range(3))
        crows = sb("crows", [1, 2, D])
        c_row, bo = crows[:, 0, :], crows[:, 1, :]
        ones = sb("ones", [P, 2])
        power = sb("power", [P, NT])
        const_row = sb("const_row", [1, VR])
        vw = sb("vw", [VR, D])
        earlier = sb("earlier", [P, NR, NR])

        xg = sb("xg", [P, KC, TG])
        h0 = sb("h0", [P, NT, D])
        h1 = sb("h1", [P, NT, D])
        xn = sb("xn", [P, NT, D])
        xa_hi = sb("xa_hi", [P, TG], F32R)
        xa_lo = sb("xa_lo", [P, TG], F32R)
        xd = sb("xd", [P, TG], F32R)
        n_q, n_v, n_pt, n_s = HP * TG, NT * HD, 2 * HP * P, 2 * 2 * HP * NK
        place_base = nc.sbuf_base
        sb("place", [P, max(n_q + n_v + n_pt + n_s, 2 * NE * TG)])
        q = over(place_base, 0, "q", [P, HP, NT, P])
        k = sb("k", [P, HP, IMG, NK])
        v = over(place_base, n_q, "v", [P, NT, HD])
        s = over(place_base, n_q + n_v + n_pt, "s", [P, 2, 2 * HP * NK])
        smax = sb("smax", [P, 2, 2 * HP])
        rsum = sb("rsum", [P, 2, 2 * HP])
        pn = sb("pn", [P, 2, 2 * HP, NQ])
        pcls = sb("pcls", [P, 2, 2, 32])
        pt = over(place_base, n_q + n_v, "pt", [P, 2, HP, P])
        pct = sb("pct", [VR, NT, P])
        silu = sb("silu", [P, 2, TG])
        hid = over(place_base, NE * TG, "hid", [P, NE, TG])
        hid_hi = over(place_base, 0, "hid_hi", [P, NE, TG], F32R)
        hid_lo = over(place_base, NE * TG, "hid_lo", [P, NE, TG], F32R)
        stats1 = sb("stats1", [P, NT, 6])
        mv1 = sb("mv1", [P, NT, 2])
        stats2 = sb("stats2", [P, NT, 6])
        mv2 = sb("mv2", [P, NT, 2])
        g_lg = sb("g_lg", [P, NT, 2 * NR])
        g_sc = sb("g_sc", [P, NT, NR])
        g_s = sb("g_s", [P, NT, NR])
        g_gs = sb("g_gs", [P, NT, NGRP])
        g_cmp, g_eq = (pn[:, b].rearrange("p n c -> p (n c)")[:, 0:NT * NR * NR].rearrange(
            "p (t j i) -> p t j i", t=NT, j=NR) for b in range(2))
        g_rank = sb("g_rank", [P, NT, NR])
        g_sum = sb("g_sum", [P, NT])
        cw = sb("cw", [P, NT, 40])
        cwt = sb("cwt", [40, TG], F32R)
        c_h1 = sb("c_h1", [1, D])
        c_xn = sb("c_xn", [1, 2 * P])
        c_stats = sb("c_stats", [1, 6])
        c_mv = sb("c_mv", [1, 2])
        c_a_hi = sb("c_a_hi", [P, 2], F32R)
        c_a_lo = sb("c_a_lo", [P, 2], F32R)
        c_d = sb("c_d", [P, 2], F32R)
        vblk = silu[:].rearrange("p a t -> p (a t)")[:, 0:HP * VR].rearrange("p (j c) -> p j c", j=HP)
        c_kv = pn[0:1].rearrange("p b n c -> p (b n c)")
        c_ffn = xg[0:1].rearrange("p c t -> p (c t)")[:, 0:NF]
        c_raw = c_ffn.rearrange("p (e a n) -> p e a n", a=2, n=P)
        c_hid = sb("c_hid", [P, 2, NE], F32R)
        c_cw = sb("c_cw", [1, NR])
        c_out = sb("c_out", [1, D])

        WT = NW // 3
        stage = over(place_base, n_q, "stage", [P, 3, 2, WT])
        assert 6 * WT <= n_v + n_pt

        d_cls, d_small, d_wo, d_w2, d_gate = (sem(n) for n in (
            "d_cls", "d_small", "d_wo", "d_w2", "d_gate"))
        d_first = [sem(f"d_first{i}") for i in range(KC // 2)]
        d_raw = [sem(f"d_raw{i}") for i in range(3)]
        x_loaded = sem("x_loaded")
        stored = sem("stored")
        consts = sem("consts")
        waited = sem("waited")
        pool_step = sem("pool_step")
        w_hi, w_lo = sem("w_hi"), sem("w_lo")
        f_hi, f_lo = sem("f_hi"), sem("f_lo")
        c_pe, c_act, c_dve, c_pool = sem("c_pe"), sem("c_act"), sem("c_dve"), sem("c_pool")
        tok_done = Signal(sem("tok_done"), NT)
        h0_done = Signal(sem("h0_done"), NT)
        ln1 = Signal(sem("ln1"), 2 * NT + 1)
        rstd1 = Signal(sem("rstd1"), 1)
        xn1 = Signal(sem("xn1"), NT)
        x1_turned = Signal(sem("x1_turned"), 2)
        x1_hi = Signal(sem("x1_hi"), 2)
        x1_lo = Signal(sem("x1_lo"), 2)
        NQKV = 2 * HP + 2 * NT
        qkv_done = Signal(sem("qkv_done"), NQKV)
        qkv_kept = Signal(sem("qkv_kept"), NQKV)
        s_done = Signal(sem("s_done"), 2 * NT)
        s_masked = Signal(sem("s_masked"), 2 * NT)
        s_max = Signal(sem("s_max"), NT)
        s_shifted = Signal(sem("s_shifted"), NT)
        s_exp = Signal(sem("s_exp"), NT)
        s_sum = Signal(sem("s_sum"), 2 * NT)
        p_done = Signal(sem("p_done"), NT)
        p_turned = Signal(sem("p_turned"), 2 * NT)
        p_kept = Signal(sem("p_kept"), 2 * NT)
        z_done = Signal(sem("z_done"), 2 * NT)
        z_kept = Signal(sem("z_kept"), 2 * NT)
        wo_done = Signal(sem("wo_done"), NT)
        h1_done = Signal(sem("h1_done"), NT)
        ln2 = Signal(sem("ln2"), 2 * NT + 1)
        rstd2 = Signal(sem("rstd2"), 1)
        xn2 = Signal(sem("xn2"), NT)
        x2_turned = Signal(sem("x2_turned"), 2)
        x2_hi = Signal(sem("x2_hi"), 2)
        x2_lo = Signal(sem("x2_lo"), 2)
        gate_done = Signal(sem("gate_done"), 1)
        NGS = 23
        gate_step = Signal(sem("gate_step"), NGS)
        g_exp = Signal(sem("g_exp"), 1)
        cw_turned = Signal(sem("cw_turned"), 1)
        cw_hi = Signal(sem("cw_hi"), 1)
        cw_lo = Signal(sem("cw_lo"), 1)
        f1_done = Signal(sem("f1_done"), NE)
        f3_done = Signal(sem("f3_done"), NE)
        silu_done = Signal(sem("silu_done"), NE)
        w_spread = Signal(sem("w_spread"), NR)
        f_prod = Signal(sem("f_prod"), NE)
        f_hid = Signal(sem("f_hid"), NR)
        f_up = Signal(sem("f_up"), NE)
        f_low = Signal(sem("f_low"), NE - 1)
        f_last = Signal(sem("f_last"), 1)
        y_done = Signal(sem("y_done"), NT)
        y_kept = Signal(sem("y_kept"), 2 * NT, before=2)
        y_stored = Signal(stored, 32, before=32)

        A_, D_ = slice(0, P), slice(P, D)

        RW = 384
        EARLY = 4

        def expert(c):
            return NR if c == 0 else c - 1

        def spread_after(c):
            return {EARLY: (1, 2, 3), EARLY + 1: (4, 5)}.get(c, (c,) if c > EARLY else ())

        def weighed_after(c):
            return {EARLY: (1, 2), EARLY + 1: (3, 4), EARLY + 2: (5, 6)}.get(c, (c,) if c > EARLY else ())

        def spread_bank(c):
            return bank[(0, 1, 3)[c % 3]]

        def split_products(a_hi, a_lo, d, w_a, w_d, cols):
            return [(a_hi, w_a[:, 0, cols]), (a_hi, w_a[:, 1, cols]), (a_lo, w_a[:, 0, cols]),
                    (d, w_d[:, 0, cols]), (d, w_d[:, 1, cols])]

        def qkv_third(i):
            n = (i + 1) % 3
            return slice(n * WT, (n + 1) * WT)

        def wait_apart(eng, semaphore, value):
            eng.wait_ge(semaphore, value)
            eng.sem_inc(waited, 1)

        def y_bank(t):
            return bank[(2, 3, 0, 1)[t]]

        def qkv_place(n):
            if n < 2 * HP:
                return bank[(6, 7, 4, 5)[n % 4]], n - 4 if n >= 4 else None
            m = n - 2 * HP
            return bank[m % 2], n - 2 if m >= 2 else None

        block = ctx.enter_context(nc.Block())

        @block.sync
        def _(sp):
            def third(i, w, c):
                sp.dma_start(stage[:, i, :, :], w[:, :, c]).then_inc(d_raw[i], 16)

            def first(i):
                c = slice(2 * i, 2 * i + 2)
                sp.dma_start(wproj[:, c, :], w_proj[:, c, :]).then_inc(d_first[i], 16)
                sp.dma_start(xg[:, c, :], xt[0][:, c, :]).then_inc(d_first[i], 16)

            sp.dma_start(crows[:], cls_rows).then_inc(d_cls, 16)
            first(0)
            third(0, w_qkv, qkv_third(0))
            third(1, w_qkv, qkv_third(1))
            first(1)
            third(2, w_qkv, qkv_third(2))
            first(2)
            sp.dma_start(btok[:], b_tokens.to_broadcast([P, D + NR])).then_inc(d_small, 16)
            sp.dma_start(bheads[:], b_heads).then_inc(d_small, 16)
            sp.dma_start(wo[:], w_o).then_inc(d_wo, 16)
            for i in range(3):
                sp.wait_ge(w_hi, 2 * (i + 1))
                sp.wait_ge(w_lo, 2 * (i + 1))
                third(i, w_ffn, slice(i * WT, (i + 1) * WT))
            sp.dma_start(gate_raw[:], w_gate).then_inc(d_gate, 16)
            sp.dma_start(w2_raw[:, :, 1, :], w_2).then_inc(d_w2, 16)
            sp.wait_ge(tok_done.sem, tok_done.at(0, NT))
            sp.dma_start(xg[:], xt[1]).then_inc(x_loaded, 16)

            def store_group(g, t0=0, t1=NT):
                sp.wait_ge(y_kept.sem, y_kept.at(g, 2 * t1))
                for i in range(2):
                    dst = out[bass.ds(g * IMG + 2 * t0, 2 * (t1 - t0)), 1:1 + NQ, :].rearrange(
                        "(t i) q n -> i q t n", i=2)[i]
                    sp.dma_start(dst, h1[i * NQ:(i + 1) * NQ, t0:t1, :]).then_inc(stored, 16)

            with sp.Fori(0, NG - 2) as g:
                sp.wait_ge(tok_done.sem, tok_done.at(g + 1, NT))
                sp.dma_start(xg[:], xt[bass.ds(g + 2, 1)].rearrange("a p c t -> (a p) c t")
                             ).then_inc(x_loaded, 16)
                store_group(g)
            store_group(NG - 2)
            sp.wait_ge(c_dve, 18)
            sp.dma_start(out[:, 0, :].rearrange("(a b) n -> a b n", a=1),
                         c_out[:].unsqueeze(1).to_broadcast([1, NG * IMG, D])).then_inc(stored, 16)
            store_group(NG - 1, 0, 2)
            store_group(NG - 1, 2, 4)
            sp.wait_ge(stored, 32 + NG * 32 + 32 + 16)

        @block.gpsimd
        def _(pool):
            steps = [0]

            def step(ins):
                ins.then_inc(pool_step, 1)
                steps[0] += 1
                pool.wait_ge(pool_step, steps[0])

            nc.gpsimd.memset(ones[:], 1.0)
            nc.gpsimd.memset(power[:], -0.5)
            nc.gpsimd.memset(vblk, 0.0)
            nc.gpsimd.memset(cw[:], 0.0)
            nc.gpsimd.memset(pcls[:], 0.0)
            nc.gpsimd.memset(const_row[:], 0.0)
            nc.gpsimd.memset(earlier[:], 1.0)
            nc.gpsimd.memset(causal[:], HUGE)
            step(nc.gpsimd.memset(ident[:], 0.0))
            step(nc.gpsimd.affine_select(out=ident[:], in_=ident[:], compare_op=ALU.not_equal, fill=1.0,
                                         base=0, pattern=[[-1, P]], channel_multiplier=1))
            nc.gpsimd.memset(const_row[:, CB:CB + 1], 1.0)
            step(nc.gpsimd.memset(pcls[:, :, :, CB:CB + 1].rearrange("p a b c -> p (a b) c"), 1.0))
            for h in range(2):
                m = causal[h * NQ:(h + 1) * NQ, 0:NQ]
                step(nc.gpsimd.affine_select(out=m, in_=m, compare_op=ALU.is_ge, fill=IGNORE,
                                             base=0, pattern=[[-1, NQ]], channel_multiplier=1))
            nc.gpsimd.affine_select(out=earlier[:], in_=earlier[:], compare_op=ALU.is_ge, fill=0.0,
                                    base=-1, pattern=[[1, NR], [-1, NR]], channel_multiplier=0
                                    ).then_inc(consts, 1)

            def rstd(var, done):
                nc.gpsimd.tensor_tensor(var, var, power[0:var.shape[0], 0:var.shape[1]], ALU.pow
                                        ).then_inc(done, 1)

            pool.wait_ge(c_dve, 3)
            rstd(c_mv[:, 1:2], c_pool)

            oh = s[0:40].rearrange("p a b -> p (a b)")[:, 0:NR * P].rearrange("p (e n) -> p e n", e=NR)
            step(nc.gpsimd.memset(oh, 0.0))
            step(nc.gpsimd.affine_select(out=oh, in_=oh, compare_op=ALU.not_equal, fill=1.0, base=0,
                                         pattern=[[-1, NR], [0, P]], channel_multiplier=1))
            step(nc.gpsimd.affine_select(out=oh, in_=oh, compare_op=ALU.not_equal, fill=1.0, base=-32,
                                         pattern=[[-1, NR], [0, P]], channel_multiplier=1))
            nc.gpsimd.tensor_copy(onehot[:], oh).then_inc(consts, 1)

            pool.wait_ge(ln1.sem, ln1.at(0, 2 * NT + 1))
            rstd(mv1[:, :, 1], rstd1.sem)

            for i in range(3):
                c = slice(i * WT, (i + 1) * WT)
                for n, w in enumerate((ffn_a, ffn_d)):
                    pool.wait_ge(f_hi, 2 * i + n + 1)
                    nc.gpsimd.tensor_tensor(w[:, 1, c], stage[:, i, n, :], w[:, 0, c].bitcast(F32),
                                            ALU.subtract).then_inc(f_lo, 1)
            pool.wait_ge(d_gate, 16)
            for n, w in enumerate((gate_a, gate_d)):
                step(nc.gpsimd.tensor_copy(w[:, 0, :], gate_raw[:, n, :]))
                nc.gpsimd.tensor_tensor(w[:, 1, :], gate_raw[:, n, :], w[:, 0, :].bitcast(F32),
                                        ALU.subtract).then_inc(f_lo, 1)

            pool.wait_ge(d_w2, 16)
            step(nc.gpsimd.tensor_copy(w2[:, :, 0, :], w2_raw[:, :, 1, :]))
            nc.gpsimd.tensor_tensor(w2[:, :, 1, :], w2_raw[:, :, 1, :], w2[:, :, 0, :].bitcast(F32),
                                    ALU.subtract).then_inc(f_lo, 1)

            def hidden_low(g, c):
                pool.wait_ge(f_up.sem, f_up.at(g, c + 1))
                e = expert(c)
                nc.gpsimd.tensor_tensor(hid_lo[:, e, :], hid[:, e, :], hid_hi[:, e, :].bitcast(F32),
                                        ALU.subtract).then_inc(f_low.sem, 1)

            def group(g):
                for t in range(NT):
                    b = t % 2
                    pool.wait_ge(s_sum.sem, s_sum.at(g, 2 * t + 2))
                    if t >= 2:
                        pool.wait_ge(p_turned.sem, p_turned.at(g, 2 * (t - 2) + 2))
                    pr = s[:, b, :].rearrange("p (n c) -> p n c", c=NK)
                    r = rsum[:, b, :]
                    nc.gpsimd.tensor_tensor(pn[:, b], pr[:, :, 0:NQ],
                                            r.unsqueeze(2).to_broadcast([P, 2 * HP, NQ]), ALU.mult)
                    nc.gpsimd.tensor_tensor(
                        pcls[:, b, :, 0:HP].rearrange("p i j -> p j i"),
                        pr[:, :, NQ].rearrange("p (j i) -> p j i", i=2),
                        r.rearrange("p (j i) -> p j i", i=2), ALU.mult).then_inc(p_done.sem, 1)

            def rstd2_of(g):
                pool.wait_ge(ln2.sem, ln2.at(g, 2 * NT + 1))
                rstd(mv2[:, :, 1], rstd2.sem)

            with pool.Fori(0, NG - 1) as g:
                group(g)
                rstd2_of(g)
                hidden_low(g, 0)
                pool.wait_ge(ln1.sem, ln1.at(g + 1, 2 * NT + 1))
                rstd(mv1[:, :, 1], rstd1.sem)
                for c in range(1, NE - 1):
                    hidden_low(g, c)
            pool.wait_ge(c_dve, 11)
            rstd(c_mv[:, 1:2], c_pool)
            group(NG - 1)
            rstd2_of(NG - 1)
            pool.wait_ge(c_act, 14)
            nc.gpsimd.tensor_tensor(c_raw[:, :, 0, :], c_raw[:, :, 0, :], c_raw[:, :, 1, :], ALU.mult
                                    ).then_inc(c_pool, 1)
            pool.wait_ge(c_pool, 3)
            pool.wait_ge(c_dve, 14)
            nc.gpsimd.tensor_tensor(c_raw[:, 0:NR, 0, :], c_raw[:, 0:NR, 0, :],
                                    c_cw[:].unsqueeze(2).to_broadcast([1, NR, P]), ALU.mult
                                    ).then_inc(c_pool, 1)
            for c in range(NE - 1):
                hidden_low(NG - 1, c)

        @block.tensor
        def _(pe):
            def embed(g, tiles):
                if tiles[0] == 0:
                    pe.wait_ge(x_loaded, g * 16)
                for t in tiles:
                    for c in range(KC):
                        mm = pe.matmul(bank[4 + t][:, 0:D], xg[:, c, t * P:(t + 1) * P], wproj[:, c, :],
                                       start=(c == 0), stop=(c == KC - 1))
                    mm.then_inc(tok_done.sem, 1)

            def embed_first(i):
                pe.wait_ge(d_first[i], 32)
                for c in (2 * i, 2 * i + 1):
                    for t in range(NT):
                        mm = pe.matmul(bank[4 + t][:, 0:D], xg[:, c, t * P:(t + 1) * P], wproj[:, c, :],
                                       start=(c == 0), stop=(c == KC - 1))
                        if c == KC - 1:
                            mm.then_inc(tok_done.sem, 1)

            def turn(g, normal, turned, to_a, to_d):
                for t in range(NT):
                    pe.wait_ge(normal.sem, normal.at(g, t + 1))
                    a = pe.transpose(to_a[:, t * P:(t + 1) * P], xn[:, t, 0:P], ident[:])
                    if t == NT - 1:
                        a.then_inc(turned.sem, 1)
                    d = pe.transpose(to_d[0:DR, t * P:(t + 1) * P], xn[:, t, P:D], ident[:])
                d.then_inc(turned.sem, 1)

            def wait_tokens(g, part, hi, lo):
                if part == 0:
                    pe.wait_ge(hi.sem, hi.at(g, 1))
                else:
                    pe.wait_ge(lo.sem, lo.at(g, part))

            def qkv(g, chunks):
                for n in chunks:
                    if n == 2 * HP:
                        pe.wait_ge(y_kept.sem, y_kept.at(g, 0))
                    dst, before = qkv_place(n)
                    if before is not None:
                        pe.wait_ge(qkv_kept.sem, qkv_kept.at(g, before + 1))
                    if n < 2 * HP:
                        parts = split_products(xa_hi[:], xa_lo[:], xd[:], qkv_a, qkv_d,
                                               slice(n * P, (n + 1) * P))
                        for i, (x, w) in enumerate(parts):
                            if n == 0 and i in (0, 2, 3):
                                wait_tokens(g, (0, None, 1, 2)[i], x1_hi, x1_lo)
                            mm = pe.matmul(dst[:], w, x, start=(i == 0), stop=(i == 4))
                    else:
                        t, half = divmod(n - 2 * HP, 2)
                        tok = slice(t * P, (t + 1) * P)
                        c0 = 2 * HD + half * (HD // 2)
                        parts = split_products(xa_hi[:, tok], xa_lo[:, tok], xd[:, tok], qkv_a, qkv_d,
                                               slice(c0, c0 + HD // 2))
                        for i, (x, w) in enumerate(parts):
                            mm = pe.matmul(dst[:, 0:HD // 2], x, w, start=(i == 0), stop=(i == 4))
                    mm.then_inc(qkv_done.sem, 1)

            def scores(g, t):
                dst = (bank[2], bank[3])
                if t == 0:
                    wait_apart(pe, qkv_kept.sem, qkv_kept.at(g, 2 * HP))
                for j in range(HP):
                    if t >= 1 and j % NH2 == 0:
                        wait_apart(pe, s_masked.sem, s_masked.at(g, 2 * (t - 1) + j // NH2 + 1))
                    for i in range(2):
                        c0 = ((j % NH2) * 2 + i) * NK
                        for h in range(2):
                            hs = slice(h * DH, (h + 1) * DH)
                            mm = pe.matmul(dst[j // NH2][hs, c0:c0 + NK], q[hs, j, t, i * NQ:(i + 1) * NQ],
                                           k[hs, j, 2 * t + i, :], start=True, stop=True)
                    if j % NH2 == NH2 - 1:
                        mm.then_inc(s_done.sem, 1)

            def turn_p(g, t):
                pe.wait_ge(p_done.sem, p_done.at(g, t + 1))
                for half in range(2):
                    if t >= 1:
                        pe.wait_ge(p_kept.sem, p_kept.at(g, 2 * (t - 1) + half + 1))
                    for j in range(NH2):
                        jj = half * NH2 + j
                        mm = pe.transpose(bank[4 + half][:, j * P:(j + 1) * P],
                                          pn[:, t % 2, 2 * jj:2 * jj + 2, :].rearrange("p i k -> p (i k)"),
                                          ident[:])
                    if half == 0:
                        for h in range(2):
                            hs = slice(h * NQ, (h + 1) * NQ)
                            for i in range(2):
                                c0 = NH2 * P + i * NQ
                                mm = pe.matmul(bank[4][h * 32:(h + 1) * 32, c0:c0 + NQ],
                                               pcls[hs, t % 2, i, :], ident[hs, hs], start=True, stop=True)
                    mm.then_inc(p_turned.sem, 1)

            def values(g, t):
                wait_apart(pe, qkv_kept.sem, qkv_kept.at(g, 2 * HP + 2 * t + 2))
                if t >= 1:
                    wait_apart(pe, z_kept.sem, z_kept.at(g, 2 * t))
                for j in range(HP):
                    if j % NH2 == 0:
                        wait_apart(pe, p_kept.sem, p_kept.at(g, 2 * t + j // NH2 + 1))
                    for h in range(2):
                        for i in range(2):
                            ks = slice(i * NQ, (i + 1) * NQ)
                            mm = pe.matmul(bank[6 + i][h * DH:(h + 1) * DH, j * NQ:(j + 1) * NQ],
                                           v[ks, t, (2 * j + h) * DH:(2 * j + h + 1) * DH],
                                           pt[ks, t % 2, j, h * NQ:(h + 1) * NQ], start=True, stop=True)
                            if j == HP - 1 and h == 1:
                                mm.then_inc(z_done.sem, 1)

            def project(g, t):
                pe.wait_ge(z_kept.sem, z_kept.at(g, 2 * t + 2))
                for j in range(HP):
                    pe.matmul(bank[t][:, 0:D], q[:, j, t, :], wo[:, j, :], start=(j == 0), stop=False)
                pe.matmul(bank[t][:, 0:D], pct[:, t, :], vw[:], start=False, stop=True
                          ).then_inc(wo_done.sem, 1)

            def gate(g):
                for t in range(NT):
                    tok = slice(t * P, (t + 1) * P)
                    dst = bank[2][:, t * 2 * NR:(t + 1) * 2 * NR]
                    for i, (x, w) in enumerate(((xa_hi, gate_a), (xa_lo, gate_a), (xd, gate_d))):
                        if t == 0:
                            wait_tokens(g, i, x2_hi, x2_lo)
                        mm = pe.matmul(dst, x[:, tok], w[:].rearrange("p a e -> p (a e)"),
                                       start=(i == 0), stop=(i == 2))
                mm.then_inc(gate_done.sem, 1)

            def hidden(g, c):
                e = expert(c)
                if c == 0 and not last(g):
                    pe.wait_ge(h0_done.sem, h0_done.at(g + 1, NT))
                for n, done in ((0, f1_done), (1, f3_done)):
                    if c >= 2 and n == 0:
                        pe.wait_ge(silu_done.sem, silu_done.at(g, c - 1))
                    if c >= 2 and n == 1:
                        pe.wait_ge(f_prod.sem, f_prod.at(g, c - 1))
                    c0 = (2 * e + n) * P
                    parts = split_products(xa_hi[:], xa_lo[:], xd[:], ffn_a, ffn_d, slice(c0, c0 + P))
                    for i, (x, w) in enumerate(parts):
                        mm = pe.matmul(bank[4 + 2 * n + c % 2][:], w, x, start=(i == 0), stop=(i == 4))
                    mm.then_inc(done.sem, 1)

            def spread_weight(g, c):
                if c == 1:
                    pe.wait_ge(cw_hi.sem, cw_hi.at(g, 1))
                    pe.wait_ge(cw_lo.sem, cw_lo.at(g, 1))
                if c >= 4:
                    pe.wait_ge(f_hid.sem, f_hid.at(g, c - 3))
                pe.matmul(spread_bank(c)[:], onehot[:, expert(c), :], cwt[:], start=True, stop=True
                          ).then_inc(w_spread.sem, 1)

            def experts(g):
                for c in range(NE):
                    hidden(g, c)
                    if c == EARLY - 1:
                        pe.wait_ge(gate_step.sem, gate_base(g, NGS))
                        for t in range(NT):
                            mm = pe.matmul(bank[3][0:40, t * P:(t + 1) * P], cw[:, t, :], ident[:],
                                           start=True, stop=True)
                        mm.then_inc(cw_turned.sem, 1)
                    for n in spread_after(c):
                        spread_weight(g, n)
                    if c == 6 and last(g):
                        class_hidden()
                    if c == 7 and last(g):
                        class_output()

            def down(g):
                for t in range(NT):
                    for n in range(NE):
                        e = expert(n)
                        if t == 0:
                            pe.wait_ge(f_up.sem, f_up.at(g, n + 1))
                            if n < NE - 1:
                                pe.wait_ge(f_low.sem, f_low.at(g, n + 1))
                            else:
                                pe.wait_ge(f_last.sem, f_last.at(g, 1))
                        tok = slice(t * P, (t + 1) * P)
                        pe.matmul(y_bank(t)[:, 0:2 * D], hid_hi[:, e, tok],
                                  w2[:, e].rearrange("p a n -> p (a n)"), start=(n == 0), stop=False)
                        mm = pe.matmul(y_bank(t)[:, 0:D], hid_lo[:, e, tok], w2[:, e, 0, :],
                                       start=False, stop=(n == NE - 1))
                    mm.then_inc(y_done.sem, 1)

            def last(g):
                return isinstance(g, int) and g == NG - 1

            def gate_base(g, n):
                return gate_step.at(g, n) + (NGS if last(g) else 0)

            def class_columns(n):
                pe.matmul(bank[n][:, 0:2], c_xn[:, 0:P], ones[0:1, :], start=True, stop=True)
                pe.matmul(bank[n][:, 2:4], c_xn[:, P:2 * P], ones[0:1, :], start=True, stop=True
                          ).then_inc(c_pe, 1)

            def class_row(dst, w_a, w_d, c0):
                parts = split_products(c_a_hi[:, 0:1], c_a_lo[:, 0:1], c_d[:, 0:1], w_a, w_d,
                                       slice(c0, c0 + RW))
                for i, (x, w) in enumerate(parts):
                    mm = pe.matmul(dst[0:1, 0:RW], x, w, start=(i == 0), stop=(i == 4))
                return mm

            def turn_rows(dst, row, count):
                for n in range(count):
                    mm = pe.matmul(dst[:, 2 * n:2 * n + 2], row(n), ones[0:1, :], start=True, stop=True)
                mm.then_inc(c_pe, 1)

            def class_gate():
                for i, (x, w) in enumerate(((c_a_hi, gate_a), (c_a_lo, gate_a), (c_d, gate_d))):
                    mm = pe.matmul(bank[0][0:1, 256:256 + 2 * NR], x[:, 0:1],
                                   w[:].rearrange("p a e -> p (a e)"), start=(i == 0), stop=(i == 2))
                mm.then_inc(c_pe, 1)

            def class_ffn(n):
                if n == 0:
                    pe.wait_ge(p_kept.sem, p_kept.at(NG - 1, 2 * NT))
                if n >= 4:
                    pe.wait_ge(c_act, 7 + n - 3)
                class_row(bank[4 + n % 4], ffn_a, ffn_d, n * RW).then_inc(c_pe, 1)

            def class_hidden():
                pe.wait_ge(c_pool, 4)
                turn_rows(bank[2], lambda e: c_raw[:, e, 0, :], NE)

            def class_output():
                pe.wait_ge(c_dve, 16)
                for e in range(NE):
                    pe.matmul(bank[2][0:1, 0:2 * D], c_hid[:, 0, e:e + 1],
                              w2[:, e].rearrange("p a n -> p (a n)"), start=(e == 0), stop=False)
                    mm = pe.matmul(bank[2][0:1, 0:D], c_hid[:, 1, e:e + 1], w2[:, e, 0, :],
                                   start=False, stop=(e == NE - 1))
                mm.then_inc(c_pe, 1)

            pe.wait_ge(consts, 1)
            pe.wait_ge(c_dve, 4)
            class_columns(0)
            pe.wait_ge(c_act, 2)
            pe.wait_ge(c_dve, 5)
            embed_first(0)
            for n in range(2):
                for i in range(2):
                    pe.wait_ge(w_hi, 2 * n + 2)
                    pe.wait_ge(w_lo, 2 * n + 2)
                    mm = class_row(bank[2 * n + i], qkv_a, qkv_d, HD + (2 * n + i) * RW)
                if n == 1:
                    mm.then_inc(c_pe, 1)
                embed_first(n + 1)
            pe.wait_ge(c_act, 3)
            turn_rows(bank[0], lambda n: c_kv[:, n * P:(n + 1) * P], 2 * HP)
            turn(0, xn1, x1_turned, bank[2], bank[4])
            pe.wait_ge(d_wo, 16)
            pe.wait_ge(c_dve, 7)
            for j in range(HP):
                pe.matmul(bank[3][0:VR, 0:D], vblk[:, j, :], wo[:, j, :], start=(j == 0), stop=False)
            pe.matmul(bank[3][0:VR, 0:D], const_row[:], bo, start=False, stop=True).then_inc(c_pe, 1)
            pe.wait_ge(consts, 2)
            pe.wait_ge(w_hi, 6)
            pe.wait_ge(w_lo, 6)

            def attention(g):
                if last(g):
                    qkv(g, range(1))
                    pe.wait_ge(y_kept.sem, y_kept.at(g, 0))
                    pe.matmul(bank[0][0:1, 0:D], ones[0:VR, 0:1], vw[:], start=True, stop=True
                              ).then_inc(c_pe, 1)
                    qkv(g, range(1, 4))
                    pe.wait_ge(c_dve, 12)
                    class_columns(1)
                    qkv(g, range(4, 6))
                    pe.wait_ge(c_act, 6)
                    pe.wait_ge(c_dve, 13)
                    class_gate()
                    qkv(g, range(6, 2 * HP))
                    pe.wait_ge(gate_step.sem, gate_step.at(g, 1))
                else:
                    qkv(g, range(2 * HP))
                qkv(g, range(2 * HP, 2 * HP + 1))
                scores(g, 0)
                qkv(g, range(2 * HP + 1, 2 * HP + 2))
                scores(g, 1)
                qkv(g, values_of(1))
                qkv(g, values_of(2))
                scores(g, 2)
                turn_p(g, 0)
                qkv(g, values_of(3))
                values(g, 0)
                turn_p(g, 1)
                scores(g, 3)
                project(g, 0)
                values(g, 1)
                turn_p(g, 2)
                project(g, 1)
                values(g, 2)
                turn_p(g, 3)
                project(g, 2)
                values(g, 3)
                if last(g):
                    class_ffn(0)
                    class_ffn(1)
                else:
                    embed(g + 1, [0])
                project(g, 3)

            def values_of(t):
                return range(2 * HP + 2 * t, 2 * HP + 2 * t + 2)

            with pe.Fori(0, NG - 1) as g:
                attention(g)
                embed(g + 1, [1, 2])
                turn(g, xn2, x2_turned, bank[0], bank[1])
                embed(g + 1, [3])
                pe.wait_ge(f_lo, 9)
                gate(g)
                experts(g)
                pe.wait_ge(silu_done.sem, silu_done.at(g, NE))
                turn(g + 1, xn1, x1_turned, bank[4], bank[5])
                down(g)

            g = NG - 1
            attention(g)
            for n in range(2, NF // RW):
                class_ffn(n)
            turn(g, xn2, x2_turned, bank[0], bank[1])
            gate(g)
            experts(g)
            pe.wait_ge(c_dve, 18)
            down(g)

        @block.scalar
        def _(act):
            def split_hi(g, turned, hi, from_a, from_d):
                act.wait_ge(turned.sem, turned.at(g, 1))
                nc.scalar.copy(xa_hi[:], from_a[:]).then_inc(hi.sem, 1)
                act.wait_ge(turned.sem, turned.at(g, 2))
                nc.scalar.copy(xd[0:DR, :], from_d[0:DR, :]).then_inc(hi.sem, 1)

            def keep_qkv(g, chunks):
                for n in chunks:
                    act.wait_ge(qkv_done.sem, qkv_done.at(g, n + 1))
                    src = qkv_place(n)[0]
                    if n < HP:
                        ins = nc.scalar.activation(q[:, n].rearrange("p t c -> p (t c)"), src[:], ACT.Identity,
                                                   bias=bq[:, n:n + 1])
                    elif n < 2 * HP:
                        ins = nc.scalar.activation(k[:, n - HP, :, 0:NQ],
                                                   src[:].rearrange("p (m c) -> p m c", c=NQ), ACT.Identity,
                                                   bias=bk[:, n - HP:n - HP + 1])
                    else:
                        if n == 2 * HP:
                            act.wait_ge(f_lo, 8)
                        t, half = divmod(n - 2 * HP, 2)
                        ins = nc.scalar.copy(v[:, t, half * (HD // 2):(half + 1) * (HD // 2)],
                                             src[:, 0:HD // 2])
                    ins.then_inc(qkv_kept.sem, 1)

            def exp(g, t):
                act.wait_ge(s_shifted.sem, s_shifted.at(g, t + 1))
                nc.scalar.activation(s[:, t % 2, :], s[:, t % 2, :], ACT.Exp).then_inc(s_exp.sem, 1)

            def keep_p(g, t):
                for half in range(2):
                    act.wait_ge(p_turned.sem, p_turned.at(g, 2 * t + half + 1))
                    if half == 0:
                        nc.scalar.copy(pct[:, t, :], bank[4][0:VR, NH2 * P:(NH2 + 1) * P])
                    nc.scalar.copy(pt[:, t % 2, half * NH2:(half + 1) * NH2, :].rearrange("p j c -> p (j c)"),
                                   bank[4 + half][:, 0:NH2 * P]).then_inc(p_kept.sem, 1)

            def keep_z(g, t):
                for i in range(2):
                    act.wait_ge(z_done.sem, z_done.at(g, 2 * t + i + 1))
                    nc.scalar.copy(q[:, :, t, i * NQ:(i + 1) * NQ],
                                   bank[6 + i][:, 0:HP * NQ].rearrange("p (j c) -> p j c", c=NQ)
                                   ).then_inc(z_kept.sem, 1)

            def attention(g):
                v0 = 2 * HP
                if last(g):
                    keep_qkv(g, range(4))
                    class_hi(1, 6)
                    keep_qkv(g, range(4, 9))
                    act.wait_ge(gate_step.sem, gate_step.at(g, 2))
                    nc.scalar.activation(g_sc[0:1, 0, :], g_sc[0:1, 0, :], ACT.Exp, scale=-1.0
                                         ).then_inc(c_act, 1)
                    keep_qkv(g, range(9, v0 + 2))
                else:
                    keep_qkv(g, range(v0 + 2))
                exp(g, 0)
                keep_qkv(g, range(v0 + 2, v0 + 4))
                exp(g, 1)
                keep_qkv(g, range(v0 + 4, v0 + 6))
                keep_p(g, 0)
                keep_qkv(g, range(v0 + 6, NQKV))
                exp(g, 2)
                keep_z(g, 0)
                keep_p(g, 1)
                exp(g, 3)
                keep_z(g, 1)
                keep_p(g, 2)
                keep_z(g, 2)
                keep_p(g, 3)
                keep_z(g, 3)

            def experts(g):
                act.wait_ge(gate_step.sem, gate_base(g, 2))
                nc.scalar.activation(g_sc[:], g_sc[:], ACT.Exp, scale=-1.0).then_inc(g_exp.sem, 1)
                if last(g):
                    nc.scalar.activation(c_raw[:, :, 0, :], c_raw[:, :, 0, :], ACT.Silu).then_inc(c_act, 1)
                for c in range(NE):
                    act.wait_ge(f1_done.sem, f1_done.at(g, c + 1))
                    if c >= 2:
                        act.wait_ge(f_prod.sem, f_prod.at(g, c - 1))
                    nc.scalar.activation(silu[:, c % 2, :], bank[4 + c % 2][:], ACT.Silu
                                         ).then_inc(silu_done.sem, 1)
                    for n in (0,) if c == 2 else weighed_after(c - 1):
                        hidden_up(g, n)
                    if c == EARLY - 1:
                        act.wait_ge(cw_turned.sem, cw_turned.at(g, 1))
                        nc.scalar.copy(cwt[:], bank[3][0:40, :]).then_inc(cw_hi.sem, 1)
                for n in weighed_after(NE - 1):
                    hidden_up(g, n)

            def hidden_up(g, c):
                if c == 0:
                    act.wait_ge(f_prod.sem, f_prod.at(g, 1))
                else:
                    act.wait_ge(f_hid.sem, f_hid.at(g, c))
                nc.scalar.copy(hid_hi[:, expert(c), :], hid[:, expert(c), :]
                               ).then_inc(f_up.sem, 1)

            def last(g):
                return isinstance(g, int) and g == NG - 1

            def gate_base(g, n):
                return gate_step.at(g, n) + (NGS if last(g) else 0)

            def class_hi(b, c_pe_step):
                act.wait_ge(c_pe, c_pe_step)
                nc.scalar.copy(c_a_hi[:], bank[b][:, 0:2]).then_inc(c_act, 1)
                nc.scalar.copy(c_d[:], bank[b][:, 2:4]).then_inc(c_act, 1)

            def expert_weights_hi(i):
                act.wait_ge(d_raw[i], 32)
                c = slice(i * WT, (i + 1) * WT)
                for n, w in enumerate((ffn_a, ffn_d)):
                    nc.scalar.copy(w[:, 0, c], stage[:, i, n, :]).then_inc(f_hi, 1)

            class_hi(0, 1)
            for i in range(3):
                act.wait_ge(d_raw[i], 16)
                for n, w in enumerate((qkv_a, qkv_d)):
                    nc.scalar.copy(w[:, 0, qkv_third(i)], stage[:, i, n, :]).then_inc(w_hi, 1)
            act.wait_ge(c_pe, 2)
            for n in range(4):
                ins = nc.scalar.copy(c_kv[:, n * RW:(n + 1) * RW], bank[n][0:1, 0:RW])
            ins.then_inc(c_act, 1)
            expert_weights_hi(0)
            expert_weights_hi(1)
            split_hi(0, x1_turned, x1_hi, bank[2], bank[4])
            act.wait_ge(c_pe, 4)
            nc.scalar.copy(vw[:], bank[3][0:VR, 0:D]).then_inc(c_act, 1)
            expert_weights_hi(2)

            act.wait_ge(d_small, 32)
            with act.Fori(0, NG - 1) as g:
                attention(g)
                split_hi(g, x2_turned, x2_hi, bank[0], bank[1])
                experts(g)
                split_hi(g + 1, x1_turned, x1_hi, bank[4], bank[5])

            g = NG - 1
            attention(g)
            for n in range(NF // RW):
                act.wait_ge(c_pe, 8 + n)
                nc.scalar.copy(c_ffn[:, n * RW:(n + 1) * RW], bank[4 + n % 4][0:1, 0:RW]).then_inc(c_act, 1)
            split_hi(g, x2_turned, x2_hi, bank[0], bank[1])
            experts(g)

        @block.vector
        def _(dve):
            def split_lo(g, hi, lo, from_a, from_d):
                dve.wait_ge(hi.sem, hi.at(g, 1))
                nc.vector.tensor_tensor(xa_lo[:], from_a[:], xa_hi[:].bitcast(F32), ALU.subtract
                                        ).then_inc(lo.sem, 1)
                dve.wait_ge(hi.sem, hi.at(g, 2))
                nc.vector.tensor_tensor(xd[DR:P, :], from_d[0:DR, :], xd[0:DR, :].bitcast(F32),
                                        ALU.subtract).then_inc(lo.sem, 1)

            def keep_h0(g, tiles):
                for t in tiles:
                    dve.wait_ge(tok_done.sem, tok_done.at(g, t + 1))
                    nc.vector.tensor_tensor(h0[:, t, :], bank[4 + t][:, 0:D], bproj, ALU.add
                                            ).then_inc(h0_done.sem, 1)
                for t in tiles:
                    dve.wait_ge(h0_done.sem, h0_done.at(g, t + 1))
                    nc.vector.bn_stats(stats1[:, t, :], h0[:, t, :]).then_inc(ln1.sem, 1)

            def keep_h1(g):
                for t in range(NT):
                    dve.wait_ge(wo_done.sem, wo_done.at(g, t + 1))
                    if t == 0:
                        dve.wait_ge(y_stored.sem, y_stored.at(g, 0))
                    nc.vector.tensor_tensor(h1[:, t, :], bank[t][:, 0:D], h0[:, t, :], ALU.add
                                            ).then_inc(h1_done.sem, 1)
                    dve.wait_ge(h1_done.sem, h1_done.at(g, t + 1))
                    nc.vector.bn_stats(stats2[:, t, :], h1[:, t, :]).then_inc(ln2.sem, 1)

            def aggregate(g, stats, mv, ln):
                wait_apart(dve, ln.sem, ln.at(g, NT))
                for t in range(NT):
                    nc.vector.bn_aggr(mv[:, t, :], stats[:, t, :]).then_inc(ln.sem, 1)
                dve.wait_ge(ln.sem, ln.at(g, 2 * NT))
                nc.vector.tensor_scalar(mv[:, :, 1], mv[:, :, 1], LN_EPS, None, ALU.add).then_inc(ln.sem, 1)

            def normalise(g, tiles, h, mv, rstd, normal):
                if tiles[0] == 0:
                    dve.wait_ge(rstd.sem, rstd.at(g, 1))
                for t in tiles:
                    m, r = mv[:, t, 0:1], mv[:, t, 1:2]
                    nc.vector.tensor_scalar(xn[:, t, :], h[:, t, :], m, r, ALU.subtract, ALU.mult
                                            ).then_inc(normal.sem, 1)

            def class_norm(row, n):
                nc.vector.bn_stats(c_stats[:], row).then_inc(c_dve, 1)
                dve.wait_ge(c_dve, n + 1)
                nc.vector.bn_aggr(c_mv[:], c_stats[:]).then_inc(c_dve, 1)
                dve.wait_ge(c_dve, n + 2)
                nc.vector.tensor_scalar(c_mv[:, 1:2], c_mv[:, 1:2], LN_EPS, None, ALU.add).then_inc(c_dve, 1)
                dve.wait_ge(c_pool, 1 if n == 0 else 2)
                m, r = c_mv[:, 0:1], c_mv[:, 1:2]
                nc.vector.tensor_scalar(c_xn[:, 0:P], row[:, 0:P], m, r, ALU.subtract, ALU.mult)
                nc.vector.tensor_scalar(c_xn[:, P:2 * P].rearrange("p (a b) -> p a b", a=2),
                                        row[:, P:D].unsqueeze(1).to_broadcast([1, 2, DR]), m, r,
                                        ALU.subtract, ALU.mult).then_inc(c_dve, 1)

            def masked_scores(g, t):
                b = t % 2
                src = (bank[2], bank[3])
                if t >= 2:
                    dve.wait_ge(p_done.sem, p_done.at(g, t - 1))
                half_c = NH2 * SC
                for half in range(2):
                    dve.wait_ge(s_done.sem, s_done.at(g, 2 * t + half + 1))
                    nc.vector.scalar_tensor_tensor(
                        out=s[:, b, half * half_c:(half + 1) * half_c].rearrange("p (n c) -> p n c", c=NK),
                        in0=src[half][:, 0:half_c].rearrange("p (n c) -> p n c", c=NK),
                        scalar=float(DH) ** -0.5,
                        in1=causal[:].unsqueeze(1).to_broadcast([P, 2 * NH2, NK]),
                        op0=ALU.mult, op1=ALU.min).then_inc(s_masked.sem, 1)
                sv = s[:, b, :].rearrange("p (n c) -> p n c", c=NK)
                dve.wait_ge(s_masked.sem, s_masked.at(g, 2 * t + 2))
                nc.vector.tensor_reduce(smax[:, b, :], sv, AX_X, ALU.max).then_inc(s_max.sem, 1)
                dve.wait_ge(s_max.sem, s_max.at(g, t + 1))
                nc.vector.tensor_tensor(sv, sv, smax[:, b, :].unsqueeze(2).to_broadcast([P, 2 * HP, NK]),
                                        ALU.subtract).then_inc(s_shifted.sem, 1)

            def sums(g, t):
                b = t % 2
                dve.wait_ge(s_exp.sem, s_exp.at(g, t + 1))
                nc.vector.tensor_reduce(rsum[:, b, :], s[:, b, :].rearrange("p (n c) -> p n c", c=NK),
                                        AX_X, ALU.add).then_inc(s_sum.sem, 1)
                dve.wait_ge(s_sum.sem, s_sum.at(g, 2 * t + 1))
                nc.vector.reciprocal(rsum[:, b, :], rsum[:, b, :]).then_inc(s_sum.sem, 1)

            def route(np, nt, logits, exp_done, at, between={}):
                sc, ss, gs = g_sc[0:np, 0:nt], g_s[0:np, 0:nt], g_gs[0:np, 0:nt]
                lg, rank, tot = g_lg[0:np, 0:nt], g_rank[0:np, 0:nt], g_sum[0:np, 0:nt]
                done = [0]

                def step(ins):
                    ins.then_inc(gate_step.sem, 1)
                    done[0] += 1
                    if done[0] in between:
                        between[done[0]]()
                    dve.wait_ge(gate_step.sem, at(done[0]))

                def ranks(val, n, dst):
                    cmp, eq = g_cmp[0:np, 0:nt, 0:n, 0:n], g_eq[0:np, 0:nt, 0:n, 0:n]
                    vi = val.unsqueeze(2).to_broadcast([np, nt, n, n])
                    vj = val.unsqueeze(3).to_broadcast([np, nt, n, n])
                    nc.vector.tensor_tensor(cmp, vi, vj, ALU.is_gt)
                    step(nc.vector.tensor_tensor(eq, vi, vj, ALU.is_equal))
                    step(nc.vector.tensor_tensor(
                        eq, eq, earlier[0:np, 0:n, 0:n].unsqueeze(1).to_broadcast([np, nt, n, n]), ALU.mult))
                    step(nc.vector.tensor_tensor(cmp, cmp, eq, ALU.add))
                    step(nc.vector.tensor_reduce(dst, cmp, AX_X, ALU.add))

                step(nc.vector.tensor_copy(lg, logits))
                step(nc.vector.tensor_tensor(sc, lg[:, :, 0:NR], lg[:, :, NR:2 * NR], ALU.add))
                exp_done()
                step(nc.vector.tensor_scalar(sc, sc, 1.0, None, ALU.add))
                step(nc.vector.reciprocal(sc, sc))
                step(nc.vector.tensor_tensor(
                    ss, sc, gbias[0:np].unsqueeze(1).to_broadcast([np, nt, NR]), ALU.add))
                pairs = ss.rearrange("p t (a b) -> p t a b", b=2)
                step(nc.vector.tensor_tensor(gs, pairs[:, :, :, 0], pairs[:, :, :, 1], ALU.add))
                ranks(gs, NGRP, rank[:, :, 0:NGRP])
                step(nc.vector.tensor_scalar(gs, rank[:, :, 0:NGRP], 1.5, None, ALU.is_lt))
                step(nc.vector.tensor_tensor(pairs, pairs,
                                             gs.unsqueeze(3).to_broadcast([np, nt, NGRP, 2]), ALU.mult))
                step(nc.vector.tensor_scalar(gs, gs, 1.0, HUGE, ALU.subtract, ALU.mult))
                step(nc.vector.tensor_tensor(pairs, pairs,
                                             gs.unsqueeze(3).to_broadcast([np, nt, NGRP, 2]), ALU.add))
                ranks(ss, NR, rank)
                step(nc.vector.scalar_tensor_tensor(out=ss, in0=rank, scalar=1.5, in1=sc,
                                                    op0=ALU.is_lt, op1=ALU.mult))
                step(nc.vector.tensor_reduce(tot, ss, AX_X, ALU.add))
                step(nc.vector.tensor_scalar(tot, tot, SUM_EPS, None, ALU.add))
                nc.vector.reciprocal(tot, tot).then_inc(gate_step.sem, 1)
                done[0] += 1
                return done[0], ss, tot

            def weights(np, nt, ss, tot):
                for c in (0, 32):
                    ins = nc.vector.tensor_tensor(cw[0:np, 0:nt, c:c + NR], ss,
                                                  tot.unsqueeze(2).to_broadcast([np, nt, NR]), ALU.mult)
                return ins

            def last(g):
                return isinstance(g, int) and g == NG - 1

            def gate_base(g, n):
                return gate_step.at(g, n) + (NGS if last(g) else 0)

            def gating(g):
                if not last(g):
                    keep_h0(g + 1, [3])
                dve.wait_ge(gate_done.sem, gate_done.at(g, 1))
                between = {11: lambda: product(g, 0), 15: lambda: product(g, 1)}
                n, ss, tot = route(
                    P, NT, bank[2][:, 0:2 * NR * NT].rearrange("p (t c) -> p t c", t=NT),
                    lambda: dve.wait_ge(g_exp.sem, g_exp.at(g, 1)), lambda n: gate_base(g, n), between)
                assert n + 1 == NGS, n
                dve.wait_ge(gate_step.sem, gate_base(g, n))
                weights(P, NT, ss, tot).then_inc(gate_step.sem, 1)

            def keep_weights(g):
                dve.wait_ge(cw_turned.sem, cw_turned.at(g, 1))
                dve.wait_ge(cw_hi.sem, cw_hi.at(g, 1))
                nc.vector.tensor_tensor(cwt[32:40, :], bank[3][32:40, :], cwt[32:40, :].bitcast(F32),
                                        ALU.subtract).then_inc(cw_lo.sem, 1)

            def product(g, c):
                dve.wait_ge(silu_done.sem, silu_done.at(g, c + 1))
                dve.wait_ge(f3_done.sem, f3_done.at(g, c + 1))
                nc.vector.tensor_tensor(hid[:, expert(c), :], bank[6 + c % 2][:], silu[:, c % 2, :], ALU.mult
                                        ).then_inc(f_prod.sem, 1)

            def weigh(g, c):
                dve.wait_ge(f_prod.sem, f_prod.at(g, c + 1))
                dve.wait_ge(w_spread.sem, w_spread.at(g, c))
                h = hid[:, expert(c), :]
                nc.vector.tensor_tensor(h, spread_bank(c)[:], h, ALU.mult).then_inc(f_hid.sem, 1)

            def experts(g):
                for c in range(2, NE):
                    if c == 8 and last(g):
                        dve.wait_ge(c_pe, 15)
                        nc.vector.tensor_tensor(c_out[:], bank[2][0:1, 0:D], c_h1[:], ALU.add
                                                ).then_inc(c_dve, 1)
                        dve.wait_ge(c_dve, 17)
                        nc.vector.tensor_tensor(c_out[:], bank[2][0:1, D:2 * D], c_out[:], ALU.add
                                                ).then_inc(c_dve, 1)
                    product(g, c)
                    if c == EARLY - 1:
                        keep_weights(g)
                    for n in weighed_after(c):
                        weigh(g, n)
                    if c == 6 and last(g):
                        dve.wait_ge(c_pe, 14)
                        cols = bank[2][:, 0:2 * NE].rearrange("p (e n) -> p e n", n=2)[:, :, 0]
                        nc.vector.tensor_copy(c_hid[:, 0, :], cols).then_inc(c_dve, 1)
                        dve.wait_ge(c_dve, 15)
                        nc.vector.tensor_tensor(c_hid[:, 1, :], cols, c_hid[:, 0, :].bitcast(F32),
                                                ALU.subtract).then_inc(c_dve, 1)
                    if not last(g):
                        if c == 3:
                            aggregate(g + 1, stats1, mv1, ln1)
                        if c in (4, 5):
                            normalise(g + 1, [c - 4], h0, mv1, rstd1, xn1)
                        if c == 7:
                            normalise(g + 1, [2, 3], h0, mv1, rstd1, xn1)

            def last_low(g):
                e = expert(NE - 1)
                dve.wait_ge(f_up.sem, f_up.at(g, NE))
                nc.vector.tensor_tensor(hid_lo[:, e, :], hid[:, e, :], hid_hi[:, e, :].bitcast(F32),
                                        ALU.subtract).then_inc(f_last.sem, 1)

            def keep_y(g):
                for t in range(NT):
                    dve.wait_ge(y_done.sem, y_done.at(g, t + 1))
                    for n in range(2):
                        nc.vector.tensor_tensor(h1[:, t, :], y_bank(t)[:, n * D:(n + 1) * D], h1[:, t, :],
                                                ALU.add).then_inc(y_kept.sem, 1)
                        if n == 0:
                            dve.wait_ge(y_kept.sem, y_kept.at(g, 2 * t + 1))

            nc.vector.memset(mv1[:], 0.0).then_inc(y_kept.sem, 2)
            nc.vector.memset(mv2[:], 0.0).then_inc(stored, 32)
            dve.wait_ge(d_cls, 16)
            class_norm(c_row, 0)
            def class_lo(b, act_step):
                dve.wait_ge(c_act, act_step)
                nc.vector.tensor_tensor(c_a_lo[:], bank[b][:, 0:2], c_a_hi[:].bitcast(F32), ALU.subtract)
                nc.vector.tensor_tensor(c_d[DR:P, :], bank[b][DR:P, 2:4], c_d[DR:P, :].bitcast(F32),
                                        ALU.subtract).then_inc(c_dve, 1)

            def weights_lo(i):
                c = qkv_third(i)
                for n, w in enumerate((qkv_a, qkv_d)):
                    dve.wait_ge(w_hi, 2 * i + n + 1)
                    nc.vector.tensor_tensor(w[:, 1, c], stage[:, i, n, :], w[:, 0, c].bitcast(F32),
                                            ALU.subtract).then_inc(w_lo, 1)

            class_lo(0, 2)
            weights_lo(0)
            weights_lo(1)
            weights_lo(2)
            dve.wait_ge(d_small, 32)
            keep_h0(0, range(NT))
            aggregate(0, stats1, mv1, ln1)
            dve.wait_ge(c_pe, 3)
            kv = bank[0][:, 0:4 * HP].rearrange("p (j n) -> p j n", n=2)[:, :, 0]
            nc.vector.tensor_tensor(k[:, :, :, NQ], kv[:, 0:HP].unsqueeze(2).to_broadcast([P, HP, IMG]),
                                    bk.unsqueeze(2).to_broadcast([P, HP, IMG]), ALU.add
                                    ).then_inc(c_dve, 1)
            flat = vblk.rearrange("p j c -> p (j c)")
            dve.wait_ge(consts, 1)
            for h in range(2):
                hs = slice(h * DH, (h + 1) * DH)
                nc.vector.tensor_copy(flat[hs, 32 * h:32 * h + (HP - 1) * (VR + 1) + 1:VR + 1],
                                      kv[hs, HP:2 * HP])
            nc.vector.tensor_copy(vblk[:, :, CB], bv).then_inc(c_dve, 1)
            normalise(0, range(NT), h0, mv1, rstd1, xn1)
            split_lo(0, x1_hi, x1_lo, bank[2], bank[4])

            def attention(g):
                for t in range(NT):
                    masked_scores(g, t)
                    sums(g, t)
                keep_h1(g)
                aggregate(g, stats2, mv2, ln2)

            with dve.Fori(0, NG - 1) as g:
                attention(g)
                normalise(g, range(NT), h1, mv2, rstd2, xn2)
                keep_h0(g + 1, [0, 1, 2])
                split_lo(g, x2_hi, x2_lo, bank[0], bank[1])
                gating(g)
                experts(g)
                last_low(g)
                split_lo(g + 1, x1_hi, x1_lo, bank[4], bank[5])
                keep_y(g)

            g = NG - 1
            dve.wait_ge(c_pe, 5)
            nc.vector.tensor_tensor(c_h1[:], bank[0][0:1, 0:D], c_row, ALU.add).then_inc(c_dve, 1)
            dve.wait_ge(c_dve, 8)
            class_norm(c_h1[:], 8)
            class_lo(1, 6)
            dve.wait_ge(c_pe, 7)
            n, ss, tot = route(1, 1, bank[0][0:1, 256:256 + 2 * NR].rearrange("p (t c) -> p t c", t=1),
                               lambda: dve.wait_ge(c_act, 7), lambda n: gate_step.at(g, n))
            dve.wait_ge(gate_step.sem, gate_step.at(g, n))
            weights(1, 1, ss, tot).then_inc(gate_step.sem, 1)
            dve.wait_ge(gate_step.sem, gate_step.at(g, NGS))
            nc.vector.tensor_copy(c_cw[:], cw[0:1, 0, 0:NR]).then_inc(c_dve, 1)
            attention(g)
            normalise(g, range(NT), h1, mv2, rstd2, xn2)
            split_lo(g, x2_hi, x2_lo, bank[0], bank[1])
            gating(g)
            experts(g)
            last_low(g)
            keep_y(g)


def kernel(x, cls_tok, L0_tok_W_proj, L0_tok_b_proj, L0_attn_W_Q, L0_attn_b_Q, L0_attn_W_K, L0_attn_b_K,
           L0_attn_W_V, L0_attn_b_V, L0_attn_W_O, L0_attn_b_O, L0_ffn_gate_weight, L0_ffn_gate_bias,
           L0_ffn_w1, L0_ffn_w2, L0_ffn_w3, L0_ffn_sw1, L0_ffn_sw2, L0_ffn_sw3):
    import numpy as np
    import concourse.bacc as bacc
    from concourse.bass_utils import run_bass_kernel_spmd

    x = np.asarray(x)
    B, C, H, W = x.shape
    p, groups = 16, 4
    D = L0_tok_W_proj.shape[0]
    nh, _, dh = L0_attn_W_Q.shape
    n = (H // p) * (W // p)
    xt = x.reshape(B, C, H // p, p, W // p, p).transpose(1, 3, 5, 0, 2, 4).reshape(-1, 128, groups, B * n // groups)
    xt = xt.transpose(2, 1, 0, 3)

    def chunks(w):
        return np.asarray(w).reshape(-1, 128, w.shape[-1]).transpose(1, 0, 2)

    def blocks(w):
        return np.stack([w[0:128], np.concatenate([w[128:], w[128:]])], 1)

    def heads_last(w):
        return np.asarray(w).transpose(1, 0, 2).reshape(D, nh * dh)

    def by_pair(b):
        return np.asarray(b).reshape(nh // 2, 2 * dh).T

    w1 = np.concatenate([np.asarray(L0_ffn_w1), np.asarray(L0_ffn_sw1)[None]])
    w3 = np.concatenate([np.asarray(L0_ffn_w3), np.asarray(L0_ffn_sw3)[None]])
    w_ffn = np.stack([w1, w3], 1).transpose(3, 0, 1, 2).reshape(D, -1)
    w_2 = np.concatenate([np.asarray(L0_ffn_w2), np.asarray(L0_ffn_sw2)[None]]).transpose(2, 0, 1)
    arrays = {
        "xt": xt,
        "w_proj": chunks(np.asarray(L0_tok_W_proj).T),
        "w_qkv": blocks(np.concatenate([heads_last(w) for w in (L0_attn_W_Q, L0_attn_W_K, L0_attn_W_V)], 1)),
        "w_o": chunks(np.asarray(L0_attn_W_O).reshape(nh * dh, D)),
        "w_gate": blocks(np.asarray(L0_ffn_gate_weight).T),
        "w_ffn": blocks(w_ffn),
        "w_2": w_2,
        "b_heads": np.stack([by_pair(b) for b in (L0_attn_b_Q, L0_attn_b_K, L0_attn_b_V)], 1),
        "b_tokens": np.concatenate([np.asarray(L0_tok_b_proj), np.asarray(L0_ffn_gate_bias)])[None],
        "cls_rows": np.stack([np.asarray(cls_tok).reshape(D), np.asarray(L0_attn_b_O)])[None],
    }
    arrays = {name: np.ascontiguousarray(a) for name, a in arrays.items()}
    nc = bacc.Bacc("TRN2", target_bir_lowering=False, num_devices=1, dynamic_dma_scratch_size=1024)
    args = [nc.dram_tensor(name, a.shape, F32, kind="ExternalInput").ap() for name, a in arrays.items()]
    out = nc.dram_tensor("out", (B, n + 1, D), F32, kind="ExternalOutput").ap()
    vit_tower(nc, *args, out)
    r = run_bass_kernel_spmd(nc, [arrays], core_ids=[0])
    return r.results[0]["out"]
```

```python
from contextlib import ExitStack

import concourse.bass as bass
from concourse import mybir

F32 = mybir.dt.float32
F32R = mybir.dt.float32r
ALU = mybir.AluOpType
ACT = mybir.ActivationFunctionType
AX_X = mybir.AxisListType.X

P = 128
HUGE = 3.0e38
IGNORE = -100000.0
LN_EPS = 1e-05
SUM_EPS = 1e-06


class Signal:

    def __init__(self, sem, per_group, before=0):
        self.sem, self.per_group, self.before = sem, per_group, before

    def at(self, g, n):
        return g * self.per_group + (self.before + n)


def vit_tower(nc, xt, w_proj, w_qkv, w_o, w_gate, w_ffn, w_2, b_heads, b_tokens, cls_rows, out):
    NG, _, KC, TG = xt.shape
    D = w_proj.shape[2]
    DR = D - P
    HP = w_o.shape[1]
    DH = 64
    HD = HP * P
    NE = w_2.shape[1]
    NR = NE - 1
    NQ = DH
    NK = NQ + 1
    IMG = TG // NQ
    NT = TG // P
    SC = 2 * NK
    NH2 = HP // 2
    VR = 64
    CB = HP
    NGRP = 4
    assert D == P + DR and DR == 64 and TG == 512 and NQ == 64

    with ExitStack() as ctx:
        def sb(name, shape, dt=F32):
            return ctx.enter_context(nc.sbuf_tensor(name, shape, dt))

        def over(base, first, name, shape, dt=F32):
            return nc.alloc_sbuf_tensor_at(name, shape, dt, offset=base + 4 * first)

        def sem(name):
            return ctx.enter_context(nc.semaphore(name))

        bank = [ctx.enter_context(nc.psum_tensor(f"bank{i}", [P, 512], F32)) for i in range(8)]

        ident = sb("ident", [P, P])
        causal = sb("causal", [P, NK])
        onehot = sb("onehot", [40, NR, P], F32R)
        wproj = sb("wproj", [P, KC, D])
        wo_base = nc.sbuf_base
        wo = sb("wo", [P, HP, 2, D], F32R)
        wo_raw = over(wo_base, 0, "wo_raw", [P, HP, 2, D])
        w2_base = nc.sbuf_base
        w2 = sb("w2", [P, NE, 2, D], F32R)
        w2_raw = over(w2_base, 0, "w2_raw", [P, NE, 2, D])
        NW = w_qkv.shape[2]
        qkv_a = sb("qkv_a", [P, 2, NW], F32R)
        qkv_d = sb("qkv_d", [P, 2, NW], F32R)
        NF = w_ffn.shape[2]
        ffn_a = sb("ffn_a", [P, 2, NF], F32R)
        ffn_d = sb("ffn_d", [P, 2, NF], F32R)
        gate_a = sb("gate_a", [P, 2, NR], F32R)
        gate_d = sb("gate_d", [P, 2, NR], F32R)
        gate_raw = sb("gate_raw", [P, 2, NR])
        btok = sb("btok", [P, D + NR])
        bproj, gbias = btok[:, 0:D], btok[:, D:D + NR]
        bheads = sb("bheads", [P, 3, HP])
        bq, bk, bv = (bheads[:, n, :] for n in range(3))
        crows = sb("crows", [1, 2, D])
        c_row, bo = crows[:, 0, :], crows[:, 1, :]
        ones = sb("ones", [P, 2])
        power = sb("power", [P, NT])
        const_row = sb("const_row", [1, VR])
        vw = sb("vw", [P, 2, D], F32R)
        earlier = sb("earlier", [P, NR, NR])

        xg = sb("xg", [P, KC, TG])
        h0 = sb("h0", [P, NT, D])
        h1 = sb("h1", [P, NT, D])
        xn = sb("xn", [P, NT, D])
        xa_hi = sb("xa_hi", [P, TG], F32R)
        xa_lo = sb("xa_lo", [P, TG], F32R)
        xd = sb("xd", [P, TG], F32R)
        n_q, n_v, n_pt, n_s = HP * TG, NT * HD, 2 * HP * P, 2 * 2 * HP * NK
        place_base = nc.sbuf_base
        sb("place", [P, max(n_q + n_v + n_pt + n_s, 2 * NE * TG)])
        q = over(place_base, 0, "q", [P, HP, NT, P])
        z_hi = over(place_base, 0, "z_hi", [P, HP, NT, P], F32R)
        z_lo = sb("z_lo", [P, HP, NT, P], F32R)
        k = sb("k", [P, HP, IMG, NK])
        v = over(place_base, n_q, "v", [P, NT, HD])
        s = over(place_base, n_q + n_v + n_pt, "s", [P, 2, 2 * HP * NK])
        smax = sb("smax", [P, 2, 2 * HP])
        rsum = sb("rsum", [P, 2, 2 * HP])
        pn = sb("pn", [P, 2, 2 * HP, NQ])
        pcls = sb("pcls", [P, 2, 2, 32])
        pt = over(place_base, n_q + n_v, "pt", [P, 2, HP, P])
        pct = sb("pct", [P, NT, P], F32R)
        silu = sb("silu", [P, 2, TG])
        hid = over(place_base, NE * TG, "hid", [P, NE, TG])
        hid_hi = over(place_base, 0, "hid_hi", [P, NE, TG], F32R)
        hid_lo = over(place_base, NE * TG, "hid_lo", [P, NE, TG], F32R)
        stats1 = sb("stats1", [P, NT, 6])
        mv1 = sb("mv1", [P, NT, 2])
        stats2 = sb("stats2", [P, NT, 6])
        mv2 = sb("mv2", [P, NT, 2])
        g_lg = sb("g_lg", [P, NT, 2 * NR])
        g_sc = sb("g_sc", [P, NT, NR])
        g_s = sb("g_s", [P, NT, NR])
        g_gs = sb("g_gs", [P, NT, NGRP])
        g_cmp, g_eq = (pn[:, b].rearrange("p n c -> p (n c)")[:, 0:NT * NR * NR].rearrange(
            "p (t j i) -> p t j i", t=NT, j=NR) for b in range(2))
        g_rank = sb("g_rank", [P, NT, NR])
        g_sum = sb("g_sum", [P, NT])
        cw = sb("cw", [P, NT, 40])
        cwt = sb("cwt", [40, TG], F32R)
        c_h1 = sb("c_h1", [1, D])
        c_xn = sb("c_xn", [1, 2 * P])
        c_stats = sb("c_stats", [1, 6])
        c_mv = sb("c_mv", [1, 2])
        c_a_hi = sb("c_a_hi", [P, 2], F32R)
        c_a_lo = sb("c_a_lo", [P, 2], F32R)
        c_d = sb("c_d", [P, 2], F32R)
        vblk = silu[:].rearrange("p a t -> p (a t)")[:, 0:HP * VR].rearrange("p (j c) -> p j c", j=HP)
        c_kv = pn[0:1].rearrange("p b n c -> p (b n c)")
        c_ffn = xg[0:1].rearrange("p c t -> p (c t)")[:, 0:NF]
        c_raw = c_ffn.rearrange("p (e a n) -> p e a n", a=2, n=P)
        c_hid = sb("c_hid", [P, 2, NE], F32R)
        c_cw = sb("c_cw", [1, NR])
        c_out = sb("c_out", [1, D])

        WT = NW // 3
        stage = over(place_base, n_q, "stage", [P, 3, 2, WT])
        assert 6 * WT <= n_v + n_pt

        d_cls, d_small, d_wo, d_w2, d_gate = (sem(n) for n in (
            "d_cls", "d_small", "d_wo", "d_w2", "d_gate"))
        d_first = [sem(f"d_first{i}") for i in range(KC // 2)]
        d_raw = [sem(f"d_raw{i}") for i in range(3)]
        x_loaded = sem("x_loaded")
        stored = sem("stored")
        consts = sem("consts")
        waited = sem("waited")
        pool_step = sem("pool_step")
        vw_low = sem("vw_low")
        w_hi, w_lo = sem("w_hi"), sem("w_lo")
        o_split = sem("o_split")
        f_hi, f_lo = sem("f_hi"), sem("f_lo")
        c_pe, c_act, c_dve, c_pool = sem("c_pe"), sem("c_act"), sem("c_dve"), sem("c_pool")
        tok_done = Signal(sem("tok_done"), NT)
        h0_done = Signal(sem("h0_done"), NT)
        ln1 = Signal(sem("ln1"), 2 * NT + 1)
        rstd1 = Signal(sem("rstd1"), 1)
        xn1 = Signal(sem("xn1"), NT)
        x1_turned = Signal(sem("x1_turned"), 2)
        x1_hi = Signal(sem("x1_hi"), 2)
        x1_lo = Signal(sem("x1_lo"), 2)
        NQKV = 2 * HP + 2 * NT
        qkv_done = Signal(sem("qkv_done"), NQKV)
        qkv_kept = Signal(sem("qkv_kept"), NQKV)
        s_done = Signal(sem("s_done"), 2 * NT)
        s_masked = Signal(sem("s_masked"), 2 * NT)
        s_max = Signal(sem("s_max"), NT)
        s_shifted = Signal(sem("s_shifted"), NT)
        s_exp = Signal(sem("s_exp"), NT)
        s_sum = Signal(sem("s_sum"), 2 * NT)
        p_done = Signal(sem("p_done"), NT)
        p_turned = Signal(sem("p_turned"), 2 * NT)
        p_kept = Signal(sem("p_kept"), 2 * NT)
        z_done = Signal(sem("z_done"), 2 * NT)
        z_kept = Signal(sem("z_kept"), 2 * NT)
        z_low = Signal(sem("z_low"), 2 * NT)
        pc_low = Signal(sem("pc_low"), NT)
        wo_done = Signal(sem("wo_done"), NT)
        h1_done = Signal(sem("h1_done"), 2 * NT)
        ln2 = Signal(sem("ln2"), 2 * NT + 2)
        rstd2 = Signal(sem("rstd2"), 2)
        xn2 = Signal(sem("xn2"), NT)
        x2_turned = Signal(sem("x2_turned"), 2)
        x2_hi = Signal(sem("x2_hi"), 2)
        x2_lo = Signal(sem("x2_lo"), 2)
        gate_done = Signal(sem("gate_done"), 1)
        NGS = 23
        gate_step = Signal(sem("gate_step"), NGS)
        g_exp = Signal(sem("g_exp"), 1)
        cw_turned = Signal(sem("cw_turned"), 1)
        cw_hi = Signal(sem("cw_hi"), 1)
        cw_lo = Signal(sem("cw_lo"), 1)
        f1_done = Signal(sem("f1_done"), NE)
        f3_done = Signal(sem("f3_done"), NE)
        silu_done = Signal(sem("silu_done"), NE)
        w_spread = Signal(sem("w_spread"), NR)
        f_prod = Signal(sem("f_prod"), NE)
        f_hid = Signal(sem("f_hid"), NR)
        f_up = Signal(sem("f_up"), NE)
        f_low = Signal(sem("f_low"), NE - 1)
        f_last = Signal(sem("f_last"), 1)
        y_done = Signal(sem("y_done"), NT)
        y_kept = Signal(sem("y_kept"), 2 * NT, before=2)
        y_stored = Signal(stored, 32, before=32)

        A_, D_ = slice(0, P), slice(P, D)

        RW = 384
        EARLY = 4

        def expert(c):
            return NR if c == 0 else c - 1

        def spread_after(c):
            return {EARLY: (1, 2, 3), EARLY + 1: (4, 5)}.get(c, (c,) if c > EARLY else ())

        def weighed_after(c):
            return {EARLY: (1, 2), EARLY + 1: (3, 4), EARLY + 2: (5, 6)}.get(c, (c,) if c > EARLY else ())

        def spread_bank(c):
            return bank[(0, 1, 3)[c % 3]]

        def split_products(a_hi, a_lo, d, w_a, w_d, cols):
            return [(a_hi, w_a[:, 0, cols]), (a_hi, w_a[:, 1, cols]), (a_lo, w_a[:, 0, cols]),
                    (d, w_d[:, 0, cols]), (d, w_d[:, 1, cols])]

        def qkv_third(i):
            n = (i + 1) % 3
            return slice(n * WT, (n + 1) * WT)

        def wait_apart(eng, semaphore, value):
            eng.wait_ge(semaphore, value)
            eng.sem_inc(waited, 1)

        def y_bank(t):
            return bank[(2, 3, 0, 1)[t]]

        def qkv_place(n):
            if n < 2 * HP:
                return bank[(6, 7, 4, 5)[n % 4]], n - 4 if n >= 4 else None
            banks = (0, 1, 0, 1, 0, 1, 1, 1)
            m = n - 2 * HP
            before = [i for i in range(m) if banks[i] == banks[m]]
            return bank[banks[m]], 2 * HP + before[-1] if before else None

        def projected(t):
            return bank[(0, 2, 3, 4)[t]]

        def embedded(t, first=False):
            return bank[4 + t] if first else bank[(1, 5, 6, 7)[t]]

        def class_place(n):
            return ((bank[1], None), (bank[5], None), (bank[1], 0), (bank[6], None), (bank[7], None),
                    (bank[5], 1))[n]

        block = ctx.enter_context(nc.Block())

        @block.sync
        def _(sp):
            def third(i, w, c):
                sp.dma_start(stage[:, i, :, :], w[:, :, c]).then_inc(d_raw[i], 16)

            def first(i):
                c = slice(2 * i, 2 * i + 2)
                sp.dma_start(wproj[:, c, :], w_proj[:, c, :]).then_inc(d_first[i], 16)
                sp.dma_start(xg[:, c, :], xt[0][:, c, :]).then_inc(d_first[i], 16)

            sp.dma_start(crows[:], cls_rows).then_inc(d_cls, 16)
            first(0)
            third(0, w_qkv, qkv_third(0))
            third(1, w_qkv, qkv_third(1))
            first(1)
            third(2, w_qkv, qkv_third(2))
            first(2)
            sp.dma_start(btok[:], b_tokens.to_broadcast([P, D + NR])).then_inc(d_small, 16)
            sp.dma_start(bheads[:], b_heads).then_inc(d_small, 16)
            sp.dma_start(wo_raw[:, :, 1, :], w_o).then_inc(d_wo, 16)
            for i in range(3):
                sp.wait_ge(w_hi, 2 * (i + 1))
                sp.wait_ge(w_lo, 2 * (i + 1))
                third(i, w_ffn, slice(i * WT, (i + 1) * WT))
            sp.dma_start(gate_raw[:], w_gate).then_inc(d_gate, 16)
            sp.dma_start(w2_raw[:, :, 1, :], w_2).then_inc(d_w2, 16)
            sp.wait_ge(tok_done.sem, tok_done.at(0, NT))
            sp.dma_start(xg[:], xt[1]).then_inc(x_loaded, 16)

            def store_group(g, t0=0, t1=NT):
                sp.wait_ge(y_kept.sem, y_kept.at(g, 2 * t1))
                for i in range(2):
                    dst = out[bass.ds(g * IMG + 2 * t0, 2 * (t1 - t0)), 1:1 + NQ, :].rearrange(
                        "(t i) q n -> i q t n", i=2)[i]
                    sp.dma_start(dst, h1[i * NQ:(i + 1) * NQ, t0:t1, :]).then_inc(stored, 16)

            with sp.Fori(0, NG - 2) as g:
                sp.wait_ge(tok_done.sem, tok_done.at(g + 1, NT))
                sp.dma_start(xg[:], xt[bass.ds(g + 2, 1)].rearrange("a p c t -> (a p) c t")
                             ).then_inc(x_loaded, 16)
                store_group(g)
            store_group(NG - 2)
            sp.wait_ge(c_dve, 18)
            sp.dma_start(out[:, 0, :].rearrange("(a b) n -> a b n", a=1),
                         c_out[:].unsqueeze(1).to_broadcast([1, NG * IMG, D])).then_inc(stored, 16)
            store_group(NG - 1, 0, 2)
            store_group(NG - 1, 2, 4)
            sp.wait_ge(stored, 32 + NG * 32 + 32 + 16)

        @block.gpsimd
        def _(pool):
            steps = [0]

            def step(ins):
                ins.then_inc(pool_step, 1)
                steps[0] += 1
                pool.wait_ge(pool_step, steps[0])

            nc.gpsimd.memset(ones[:], 1.0)
            nc.gpsimd.memset(power[:], -0.5)
            nc.gpsimd.memset(vblk, 0.0)
            nc.gpsimd.memset(cw[:], 0.0)
            nc.gpsimd.memset(pcls[:], 0.0)
            nc.gpsimd.memset(const_row[:], 0.0)
            nc.gpsimd.memset(earlier[:], 1.0)
            nc.gpsimd.memset(causal[:], HUGE)
            step(nc.gpsimd.memset(ident[:], 0.0))
            step(nc.gpsimd.affine_select(out=ident[:], in_=ident[:], compare_op=ALU.not_equal, fill=1.0,
                                         base=0, pattern=[[-1, P]], channel_multiplier=1))
            nc.gpsimd.memset(const_row[:, CB:CB + 1], 1.0)
            step(nc.gpsimd.memset(pcls[:, :, :, CB:CB + 1].rearrange("p a b c -> p (a b) c"), 1.0))
            for h in range(2):
                m = causal[h * NQ:(h + 1) * NQ, 0:NQ]
                step(nc.gpsimd.affine_select(out=m, in_=m, compare_op=ALU.is_ge, fill=IGNORE,
                                             base=0, pattern=[[-1, NQ]], channel_multiplier=1))
            nc.gpsimd.affine_select(out=earlier[:], in_=earlier[:], compare_op=ALU.is_ge, fill=0.0,
                                    base=-1, pattern=[[1, NR], [-1, NR]], channel_multiplier=0
                                    ).then_inc(consts, 1)

            def rstd(var, done):
                nc.gpsimd.tensor_tensor(var, var, power[0:var.shape[0], 0:var.shape[1]], ALU.pow
                                        ).then_inc(done, 1)

            pool.wait_ge(c_dve, 3)
            rstd(c_mv[:, 1:2], c_pool)

            oh = s[0:40].rearrange("p a b -> p (a b)")[:, 0:NR * P].rearrange("p (e n) -> p e n", e=NR)
            step(nc.gpsimd.memset(oh, 0.0))
            step(nc.gpsimd.affine_select(out=oh, in_=oh, compare_op=ALU.not_equal, fill=1.0, base=0,
                                         pattern=[[-1, NR], [0, P]], channel_multiplier=1))
            step(nc.gpsimd.affine_select(out=oh, in_=oh, compare_op=ALU.not_equal, fill=1.0, base=-32,
                                         pattern=[[-1, NR], [0, P]], channel_multiplier=1))
            nc.gpsimd.tensor_copy(onehot[:], oh).then_inc(consts, 1)

            pool.wait_ge(ln1.sem, ln1.at(0, 2 * NT + 1))
            rstd(mv1[:, :, 1], rstd1.sem)

            for i in range(3):
                c = slice(i * WT, (i + 1) * WT)
                for n, w in enumerate((ffn_a, ffn_d)):
                    pool.wait_ge(f_hi, 2 * i + n + 1)
                    nc.gpsimd.tensor_tensor(w[:, 1, c], stage[:, i, n, :], w[:, 0, c].bitcast(F32),
                                            ALU.subtract).then_inc(f_lo, 1)
            pool.wait_ge(d_gate, 16)
            for n, w in enumerate((gate_a, gate_d)):
                step(nc.gpsimd.tensor_copy(w[:, 0, :], gate_raw[:, n, :]))
                nc.gpsimd.tensor_tensor(w[:, 1, :], gate_raw[:, n, :], w[:, 0, :].bitcast(F32),
                                        ALU.subtract).then_inc(f_lo, 1)

            def hidden_low(g, c):
                pool.wait_ge(f_up.sem, f_up.at(g, c + 1))
                e = expert(c)
                nc.gpsimd.tensor_tensor(hid_lo[:, e, :], hid[:, e, :], hid_hi[:, e, :].bitcast(F32),
                                        ALU.subtract).then_inc(f_low.sem, 1)

            def group(g):
                for t in range(NT):
                    b = t % 2
                    pool.wait_ge(s_sum.sem, s_sum.at(g, 2 * t + 2))
                    if t >= 2:
                        pool.wait_ge(p_turned.sem, p_turned.at(g, 2 * (t - 2) + 2))
                    pr = s[:, b, :].rearrange("p (n c) -> p n c", c=NK)
                    r = rsum[:, b, :]
                    nc.gpsimd.tensor_tensor(pn[:, b], pr[:, :, 0:NQ],
                                            r.unsqueeze(2).to_broadcast([P, 2 * HP, NQ]), ALU.mult)
                    nc.gpsimd.tensor_tensor(
                        pcls[:, b, :, 0:HP].rearrange("p i j -> p j i"),
                        pr[:, :, NQ].rearrange("p (j i) -> p j i", i=2),
                        r.rearrange("p (j i) -> p j i", i=2), ALU.mult).then_inc(p_done.sem, 1)

            def rstd2_of(g):
                pool.wait_ge(ln2.sem, ln2.at(g, 7))
                rstd(mv2[:, 0:3, 1], rstd2.sem)
                pool.wait_ge(ln2.sem, ln2.at(g, 10))
                rstd(mv2[:, 3:NT, 1], rstd2.sem)

            with pool.Fori(0, NG - 1) as g:
                group(g)
                rstd2_of(g)
                hidden_low(g, 0)
                pool.wait_ge(ln1.sem, ln1.at(g + 1, 2 * NT + 1))
                rstd(mv1[:, :, 1], rstd1.sem)
                for c in range(1, NE - 1):
                    hidden_low(g, c)
            pool.wait_ge(c_dve, 11)
            rstd(c_mv[:, 1:2], c_pool)
            group(NG - 1)
            rstd2_of(NG - 1)
            pool.wait_ge(c_act, 14)
            nc.gpsimd.tensor_tensor(c_raw[:, :, 0, :], c_raw[:, :, 0, :], c_raw[:, :, 1, :], ALU.mult
                                    ).then_inc(c_pool, 1)
            pool.wait_ge(c_pool, 3)
            pool.wait_ge(c_dve, 14)
            nc.gpsimd.tensor_tensor(c_raw[:, 0:NR, 0, :], c_raw[:, 0:NR, 0, :],
                                    c_cw[:].unsqueeze(2).to_broadcast([1, NR, P]), ALU.mult
                                    ).then_inc(c_pool, 1)
            for c in range(NE - 1):
                hidden_low(NG - 1, c)

        @block.tensor
        def _(pe):
            def embed(g, tiles):
                if tiles[0] == 0:
                    pe.wait_ge(x_loaded, g * 16)
                for t in tiles:
                    for c in range(KC):
                        mm = pe.matmul(embedded(t)[:, 0:D], xg[:, c, t * P:(t + 1) * P], wproj[:, c, :],
                                       start=(c == 0), stop=(c == KC - 1))
                    mm.then_inc(tok_done.sem, 1)

            def embed_first(i):
                pe.wait_ge(d_first[i], 32)
                for c in (2 * i, 2 * i + 1):
                    for t in range(NT):
                        mm = pe.matmul(embedded(t, first=True)[:, 0:D], xg[:, c, t * P:(t + 1) * P],
                                       wproj[:, c, :], start=(c == 0), stop=(c == KC - 1))
                        if c == KC - 1:
                            mm.then_inc(tok_done.sem, 1)

            def turn(g, normal, turned, to_a, to_d):
                for t in range(NT):
                    pe.wait_ge(normal.sem, normal.at(g, t + 1))
                    a = pe.transpose(to_a[:, t * P:(t + 1) * P], xn[:, t, 0:P], ident[:])
                    if t == NT - 1:
                        a.then_inc(turned.sem, 1)
                    d = pe.transpose(to_d[0:DR, t * P:(t + 1) * P], xn[:, t, P:D], ident[:])
                d.then_inc(turned.sem, 1)

            def wait_tokens(g, part, hi, lo):
                if part == 0:
                    pe.wait_ge(hi.sem, hi.at(g, 1))
                else:
                    pe.wait_ge(lo.sem, lo.at(g, part))

            def qkv(g, chunks):
                for n in chunks:
                    if n == 2 * HP:
                        pe.wait_ge(y_kept.sem, y_kept.at(g, 0))
                    dst, before = qkv_place(n)
                    if before is not None:
                        pe.wait_ge(qkv_kept.sem, qkv_kept.at(g, before + 1))
                    if n < 2 * HP:
                        parts = split_products(xa_hi[:], xa_lo[:], xd[:], qkv_a, qkv_d,
                                               slice(n * P, (n + 1) * P))
                        for i, (x, w) in enumerate(parts):
                            if n == 0 and i in (0, 2, 3):
                                wait_tokens(g, (0, None, 1, 2)[i], x1_hi, x1_lo)
                            mm = pe.matmul(dst[:], w, x, start=(i == 0), stop=(i == 4))
                    else:
                        t, half = divmod(n - 2 * HP, 2)
                        tok = slice(t * P, (t + 1) * P)
                        c0 = 2 * HD + half * (HD // 2)
                        parts = split_products(xa_hi[:, tok], xa_lo[:, tok], xd[:, tok], qkv_a, qkv_d,
                                               slice(c0, c0 + HD // 2))
                        for i, (x, w) in enumerate(parts):
                            mm = pe.matmul(dst[:, 0:HD // 2], x, w, start=(i == 0), stop=(i == 4))
                    mm.then_inc(qkv_done.sem, 1)

            def scores(g, t):
                dst = (bank[2], bank[3])
                if t == 0:
                    wait_apart(pe, qkv_kept.sem, qkv_kept.at(g, 2 * HP))
                    wait_apart(pe, vw_low, 2)
                for j in range(HP):
                    if t >= 1 and j % NH2 == 0:
                        wait_apart(pe, s_masked.sem, s_masked.at(g, 2 * (t - 1) + j // NH2 + 1))
                    for i in range(2):
                        c0 = ((j % NH2) * 2 + i) * NK
                        for h in range(2):
                            hs = slice(h * DH, (h + 1) * DH)
                            mm = pe.matmul(dst[j // NH2][hs, c0:c0 + NK], q[hs, j, t, i * NQ:(i + 1) * NQ],
                                           k[hs, j, 2 * t + i, :], start=True, stop=True)
                    if j % NH2 == NH2 - 1:
                        mm.then_inc(s_done.sem, 1)

            def turn_p(g, t):
                pe.wait_ge(p_done.sem, p_done.at(g, t + 1))
                for half in range(2):
                    if t >= 1:
                        pe.wait_ge(p_kept.sem, p_kept.at(g, 2 * (t - 1) + half + 1))
                    if t >= 1 and half == 0:
                        pe.wait_ge(pc_low.sem, pc_low.at(g, t))
                    for j in range(NH2):
                        jj = half * NH2 + j
                        mm = pe.transpose(bank[4 + half][:, j * P:(j + 1) * P],
                                          pn[:, t % 2, 2 * jj:2 * jj + 2, :].rearrange("p i k -> p (i k)"),
                                          ident[:])
                    if half == 0:
                        for h in range(2):
                            hs = slice(h * NQ, (h + 1) * NQ)
                            for i in range(2):
                                c0 = NH2 * P + i * NQ
                                mm = pe.matmul(bank[4][h * 32:(h + 1) * 32, c0:c0 + NQ],
                                               pcls[hs, t % 2, i, :], ident[hs, hs], start=True, stop=True)
                    mm.then_inc(p_turned.sem, 1)

            def values(g, t):
                wait_apart(pe, qkv_kept.sem, qkv_kept.at(g, 2 * HP + 2 * t + 2))
                if t >= 1:
                    wait_apart(pe, z_low.sem, z_low.at(g, 2 * t))
                for j in range(HP):
                    if j % NH2 == 0:
                        wait_apart(pe, p_kept.sem, p_kept.at(g, 2 * t + j // NH2 + 1))
                    for h in range(2):
                        for i in range(2):
                            ks = slice(i * NQ, (i + 1) * NQ)
                            mm = pe.matmul(bank[6 + i][h * DH:(h + 1) * DH, j * NQ:(j + 1) * NQ],
                                           v[ks, t, (2 * j + h) * DH:(2 * j + h + 1) * DH],
                                           pt[ks, t % 2, j, h * NQ:(h + 1) * NQ], start=True, stop=True)
                            if j == HP - 1 and h == 1:
                                mm.then_inc(z_done.sem, 1)

            def project(g, t):
                if t == 0:
                    pe.wait_ge(o_split, 4)
                pe.wait_ge(z_low.sem, z_low.at(g, 2 * t + 2))
                for j in range(HP):
                    pe.matmul(projected(t)[:, 0:2 * D], z_hi[:, j, t, :], wo[:, j].rearrange("p a n -> p (a n)"),
                              start=(j == 0), stop=False)
                    pe.matmul(projected(t)[:, 0:D], z_lo[:, j, t, :], wo[:, j, 0, :], start=False, stop=False)
                pe.wait_ge(pc_low.sem, pc_low.at(g, t + 1))
                pe.matmul(projected(t)[:, 0:2 * D], pct[:, t, :], vw[:].rearrange("p a n -> p (a n)"),
                          start=False, stop=True).then_inc(wo_done.sem, 1)

            def gate(g):
                for t in range(NT):
                    tok = slice(t * P, (t + 1) * P)
                    dst = bank[2][:, t * 2 * NR:(t + 1) * 2 * NR]
                    for i, (x, w) in enumerate(((xa_hi, gate_a), (xa_lo, gate_a), (xd, gate_d))):
                        if t == 0:
                            wait_tokens(g, i, x2_hi, x2_lo)
                        mm = pe.matmul(dst, x[:, tok], w[:].rearrange("p a e -> p (a e)"),
                                       start=(i == 0), stop=(i == 2))
                mm.then_inc(gate_done.sem, 1)

            def hidden(g, c):
                e = expert(c)
                if c == 0 and not last(g):
                    pe.wait_ge(h0_done.sem, h0_done.at(g + 1, NT))
                if c == 1 and last(g):
                    pe.wait_ge(c_act, 13)
                for n, done in ((0, f1_done), (1, f3_done)):
                    if c >= 2 and n == 0:
                        pe.wait_ge(silu_done.sem, silu_done.at(g, c - 1))
                    if c >= 2 and n == 1:
                        pe.wait_ge(f_prod.sem, f_prod.at(g, c - 1))
                    c0 = (2 * e + n) * P
                    parts = split_products(xa_hi[:], xa_lo[:], xd[:], ffn_a, ffn_d, slice(c0, c0 + P))
                    for i, (x, w) in enumerate(parts):
                        mm = pe.matmul(bank[4 + 2 * n + c % 2][:], w, x, start=(i == 0), stop=(i == 4))
                    mm.then_inc(done.sem, 1)

            def spread_weight(g, c):
                if c == 1:
                    pe.wait_ge(cw_hi.sem, cw_hi.at(g, 1))
                    pe.wait_ge(cw_lo.sem, cw_lo.at(g, 1))
                if c >= 4:
                    pe.wait_ge(f_hid.sem, f_hid.at(g, c - 3))
                pe.matmul(spread_bank(c)[:], onehot[:, expert(c), :], cwt[:], start=True, stop=True
                          ).then_inc(w_spread.sem, 1)

            def experts(g):
                for c in range(NE):
                    hidden(g, c)
                    if c == EARLY - 1:
                        pe.wait_ge(gate_step.sem, gate_base(g, NGS))
                        for t in range(NT):
                            mm = pe.matmul(bank[3][0:40, t * P:(t + 1) * P], cw[:, t, :], ident[:],
                                           start=True, stop=True)
                        mm.then_inc(cw_turned.sem, 1)
                    for n in spread_after(c):
                        spread_weight(g, n)
                    if c == 6 and last(g):
                        class_hidden()
                    if c == 7 and last(g):
                        class_output()

            def down(g):
                for t in range(NT):
                    for n in range(NE):
                        e = expert(n)
                        if t == 0:
                            pe.wait_ge(f_up.sem, f_up.at(g, n + 1))
                            if n < NE - 1:
                                pe.wait_ge(f_low.sem, f_low.at(g, n + 1))
                            else:
                                pe.wait_ge(f_last.sem, f_last.at(g, 1))
                        tok = slice(t * P, (t + 1) * P)
                        pe.matmul(y_bank(t)[:, 0:2 * D], hid_hi[:, e, tok],
                                  w2[:, e].rearrange("p a n -> p (a n)"), start=(n == 0), stop=False)
                        mm = pe.matmul(y_bank(t)[:, 0:D], hid_lo[:, e, tok], w2[:, e, 0, :],
                                       start=False, stop=(n == NE - 1))
                    mm.then_inc(y_done.sem, 1)

            def last(g):
                return isinstance(g, int) and g == NG - 1

            def gate_base(g, n):
                return gate_step.at(g, n) + (NGS if last(g) else 0)

            def class_columns(n):
                pe.matmul(bank[n][:, 0:2], c_xn[:, 0:P], ones[0:1, :], start=True, stop=True)
                pe.matmul(bank[n][:, 2:4], c_xn[:, P:2 * P], ones[0:1, :], start=True, stop=True
                          ).then_inc(c_pe, 1)

            def class_row(dst, w_a, w_d, c0):
                parts = split_products(c_a_hi[:, 0:1], c_a_lo[:, 0:1], c_d[:, 0:1], w_a, w_d,
                                       slice(c0, c0 + RW))
                for i, (x, w) in enumerate(parts):
                    mm = pe.matmul(dst[0:1, 0:RW], x, w, start=(i == 0), stop=(i == 4))
                return mm

            def turn_rows(dst, row, count):
                for n in range(count):
                    mm = pe.matmul(dst[:, 2 * n:2 * n + 2], row(n), ones[0:1, :], start=True, stop=True)
                mm.then_inc(c_pe, 1)

            def class_gate():
                for i, (x, w) in enumerate(((c_a_hi, gate_a), (c_a_lo, gate_a), (c_d, gate_d))):
                    mm = pe.matmul(bank[0][0:1, 256:256 + 2 * NR], x[:, 0:1],
                                   w[:].rearrange("p a e -> p (a e)"), start=(i == 0), stop=(i == 2))
                mm.then_inc(c_pe, 1)

            def class_ffn(n):
                dst, before = class_place(n)
                if before is not None:
                    pe.wait_ge(c_act, 8 + before)
                class_row(dst, ffn_a, ffn_d, n * RW).then_inc(c_pe, 1)

            def class_hidden():
                pe.wait_ge(c_pool, 4)
                turn_rows(bank[2], lambda e: c_raw[:, e, 0, :], NE)

            def class_output():
                pe.wait_ge(c_dve, 16)
                for e in range(NE):
                    pe.matmul(bank[2][0:1, 0:2 * D], c_hid[:, 0, e:e + 1],
                              w2[:, e].rearrange("p a n -> p (a n)"), start=(e == 0), stop=False)
                    mm = pe.matmul(bank[2][0:1, 0:D], c_hid[:, 1, e:e + 1], w2[:, e, 0, :],
                                   start=False, stop=(e == NE - 1))
                mm.then_inc(c_pe, 1)

            pe.wait_ge(consts, 1)
            pe.wait_ge(c_dve, 4)
            class_columns(0)
            pe.wait_ge(c_act, 2)
            pe.wait_ge(c_dve, 5)
            embed_first(0)
            for n in range(2):
                for i in range(2):
                    pe.wait_ge(w_hi, 2 * n + 2)
                    pe.wait_ge(w_lo, 2 * n + 2)
                    mm = class_row(bank[2 * n + i], qkv_a, qkv_d, HD + (2 * n + i) * RW)
                if n == 1:
                    mm.then_inc(c_pe, 1)
                embed_first(n + 1)
            pe.wait_ge(c_act, 3)
            turn_rows(bank[0], lambda n: c_kv[:, n * P:(n + 1) * P], 2 * HP)
            pe.wait_ge(d_wo, 16)
            pe.wait_ge(c_dve, 7)
            for j in range(HP):
                if j == 2:
                    turn(0, xn1, x1_turned, bank[2], bank[4])
                pe.matmul(bank[3][0:VR, 0:D], vblk[:, j, :], wo_raw[:, j, 1, :], start=(j == 0), stop=False)
            pe.matmul(bank[3][0:VR, 0:D], const_row[:], bo, start=False, stop=True).then_inc(c_pe, 1)
            pe.wait_ge(consts, 2)
            pe.wait_ge(w_hi, 6)
            pe.wait_ge(w_lo, 6)

            def attention(g):
                if last(g):
                    pe.wait_ge(x1_lo.sem, x1_lo.at(g, 2))
                    for n in range(2):
                        mm = pe.matmul(bank[5][0:1, 0:D], ones[0:VR, 0:1], vw[0:VR, n, :].bitcast(F32),
                                       start=(n == 0), stop=(n == 1))
                    mm.then_inc(c_pe, 1)
                    qkv(g, range(3))
                    pe.wait_ge(y_kept.sem, y_kept.at(g, 0))
                    pe.wait_ge(c_dve, 12)
                    class_columns(1)
                    qkv(g, range(3, 6))
                    pe.wait_ge(c_act, 6)
                    pe.wait_ge(c_dve, 13)
                    class_gate()
                    qkv(g, range(6, 2 * HP))
                    pe.wait_ge(gate_step.sem, gate_step.at(g, 1))
                else:
                    qkv(g, range(2 * HP))
                v0 = 2 * HP
                qkv(g, range(v0, v0 + 1))
                scores(g, 0)
                qkv(g, range(v0 + 1, v0 + 2))
                scores(g, 1)
                qkv(g, range(v0 + 2, v0 + 4))
                scores(g, 2)
                qkv(g, range(v0 + 4, v0 + 5))
                turn_p(g, 0)
                qkv(g, range(v0 + 5, v0 + 6))
                values(g, 0)
                turn_p(g, 1)
                qkv(g, range(v0 + 6, v0 + 7))
                scores(g, 3)
                project(g, 0)
                values(g, 1)
                qkv(g, range(v0 + 7, v0 + 8))
                turn_p(g, 2)
                project(g, 1)
                values(g, 2)
                turn_p(g, 3)
                pe.wait_ge(qkv_kept.sem, qkv_kept.at(g, NQKV))
                embed_or_class(g, 0)
                project(g, 2)
                values(g, 3)
                embed_or_class(g, 1)
                project(g, 3)

            def embed_or_class(g, n):
                if last(g):
                    class_ffn(n)
                    if n == 1:
                        class_ffn(2)
                else:
                    embed(g + 1, [n])

            with pe.Fori(0, NG - 1) as g:
                attention(g)
                embed(g + 1, [2])
                turn(g, xn2, x2_turned, bank[0], bank[3])
                embed(g + 1, [3])
                pe.wait_ge(f_lo, 8)
                gate(g)
                experts(g)
                pe.wait_ge(silu_done.sem, silu_done.at(g, NE))
                turn(g + 1, xn1, x1_turned, bank[4], bank[5])
                down(g)

            g = NG - 1
            attention(g)
            for n in range(3, 5):
                class_ffn(n)
            turn(g, xn2, x2_turned, bank[0], bank[3])
            for n in range(5, NF // RW):
                class_ffn(n)
            gate(g)
            experts(g)
            pe.wait_ge(c_dve, 18)
            down(g)

        @block.scalar
        def _(act):
            def split_hi(g, turned, hi, from_a, from_d):
                act.wait_ge(turned.sem, turned.at(g, 1))
                nc.scalar.copy(xa_hi[:], from_a[:]).then_inc(hi.sem, 1)
                act.wait_ge(turned.sem, turned.at(g, 2))
                nc.scalar.copy(xd[0:DR, :], from_d[0:DR, :]).then_inc(hi.sem, 1)

            def keep_qkv(g, chunks):
                for n in chunks:
                    act.wait_ge(qkv_done.sem, qkv_done.at(g, n + 1))
                    src = qkv_place(n)[0]
                    if n < HP:
                        ins = nc.scalar.activation(q[:, n].rearrange("p t c -> p (t c)"), src[:], ACT.Identity,
                                                   bias=bq[:, n:n + 1])
                    elif n < 2 * HP:
                        ins = nc.scalar.activation(k[:, n - HP, :, 0:NQ],
                                                   src[:].rearrange("p (m c) -> p m c", c=NQ), ACT.Identity,
                                                   bias=bk[:, n - HP:n - HP + 1])
                    else:
                        if n == 2 * HP:
                            act.wait_ge(f_lo, 8)
                        t, half = divmod(n - 2 * HP, 2)
                        ins = nc.scalar.copy(v[:, t, half * (HD // 2):(half + 1) * (HD // 2)],
                                             src[:, 0:HD // 2])
                    ins.then_inc(qkv_kept.sem, 1)

            def exp(g, t):
                act.wait_ge(s_shifted.sem, s_shifted.at(g, t + 1))
                nc.scalar.activation(s[:, t % 2, :], s[:, t % 2, :], ACT.Exp).then_inc(s_exp.sem, 1)

            def keep_p(g, t):
                for half in range(2):
                    act.wait_ge(p_turned.sem, p_turned.at(g, 2 * t + half + 1))
                    if half == 0:
                        nc.scalar.copy(pct[0:VR, t, :], bank[4][0:VR, NH2 * P:(NH2 + 1) * P])
                    nc.scalar.copy(pt[:, t % 2, half * NH2:(half + 1) * NH2, :].rearrange("p j c -> p (j c)"),
                                   bank[4 + half][:, 0:NH2 * P]).then_inc(p_kept.sem, 1)

            def keep_z(g, t):
                for i in range(2):
                    act.wait_ge(z_done.sem, z_done.at(g, 2 * t + i + 1))
                    nc.scalar.copy(z_hi[:, :, t, i * NQ:(i + 1) * NQ],
                                   bank[6 + i][:, 0:HP * NQ].rearrange("p (j c) -> p j c", c=NQ)
                                   ).then_inc(z_kept.sem, 1)

            def attention(g):
                v0 = 2 * HP
                if last(g):
                    keep_qkv(g, range(3))
                    class_hi(1, 6)
                    keep_qkv(g, range(3, 7))
                    act.wait_ge(gate_step.sem, gate_step.at(g, 2))
                    nc.scalar.activation(g_sc[0:1, 0, :], g_sc[0:1, 0, :], ACT.Exp, scale=-1.0
                                         ).then_inc(c_act, 1)
                    keep_qkv(g, range(7, v0 + 2))
                else:
                    keep_qkv(g, range(v0 + 2))
                exp(g, 0)
                keep_qkv(g, range(v0 + 2, v0 + 4))
                exp(g, 1)
                keep_qkv(g, range(v0 + 4, v0 + 5))
                keep_p(g, 0)
                keep_qkv(g, range(v0 + 5, v0 + 6))
                exp(g, 2)
                keep_z(g, 0)
                keep_p(g, 1)
                keep_qkv(g, range(v0 + 6, v0 + 7))
                exp(g, 3)
                keep_z(g, 1)
                keep_qkv(g, range(v0 + 7, v0 + 8))
                keep_p(g, 2)
                keep_z(g, 2)
                keep_p(g, 3)
                if last(g):
                    keep_class_row(0)
                keep_z(g, 3)

            def keep_class_row(n):
                act.wait_ge(c_pe, 8 + n)
                nc.scalar.copy(c_ffn[:, n * RW:(n + 1) * RW], class_place(n)[0][0:1, 0:RW]).then_inc(c_act, 1)

            def experts(g):
                act.wait_ge(gate_step.sem, gate_base(g, 2))
                nc.scalar.activation(g_sc[:], g_sc[:], ACT.Exp, scale=-1.0).then_inc(g_exp.sem, 1)
                if last(g):
                    act.wait_ge(c_act, 13)
                    nc.scalar.activation(c_raw[:, :, 0, :], c_raw[:, :, 0, :], ACT.Silu).then_inc(c_act, 1)
                for c in range(NE):
                    act.wait_ge(f1_done.sem, f1_done.at(g, c + 1))
                    if c >= 2:
                        act.wait_ge(f_prod.sem, f_prod.at(g, c - 1))
                    nc.scalar.activation(silu[:, c % 2, :], bank[4 + c % 2][:], ACT.Silu
                                         ).then_inc(silu_done.sem, 1)
                    for n in (0,) if c == 2 else weighed_after(c - 1):
                        hidden_up(g, n)
                    if c == EARLY - 1:
                        act.wait_ge(cw_turned.sem, cw_turned.at(g, 1))
                        nc.scalar.copy(cwt[:], bank[3][0:40, :]).then_inc(cw_hi.sem, 1)
                for n in weighed_after(NE - 1):
                    hidden_up(g, n)

            def hidden_up(g, c):
                if c == 0:
                    act.wait_ge(f_prod.sem, f_prod.at(g, 1))
                else:
                    act.wait_ge(f_hid.sem, f_hid.at(g, c))
                nc.scalar.copy(hid_hi[:, expert(c), :], hid[:, expert(c), :]
                               ).then_inc(f_up.sem, 1)

            def last(g):
                return isinstance(g, int) and g == NG - 1

            def gate_base(g, n):
                return gate_step.at(g, n) + (NGS if last(g) else 0)

            def class_hi(b, c_pe_step):
                act.wait_ge(c_pe, c_pe_step)
                nc.scalar.copy(c_a_hi[:], bank[b][:, 0:2]).then_inc(c_act, 1)
                nc.scalar.copy(c_d[:], bank[b][:, 2:4]).then_inc(c_act, 1)

            def expert_weights_hi(i):
                act.wait_ge(d_raw[i], 32)
                c = slice(i * WT, (i + 1) * WT)
                for n, w in enumerate((ffn_a, ffn_d)):
                    nc.scalar.copy(w[:, 0, c], stage[:, i, n, :]).then_inc(f_hi, 1)

            class_hi(0, 1)
            for i in range(3):
                act.wait_ge(d_raw[i], 16)
                for n, w in enumerate((qkv_a, qkv_d)):
                    nc.scalar.copy(w[:, 0, qkv_third(i)], stage[:, i, n, :]).then_inc(w_hi, 1)
            act.wait_ge(c_pe, 2)
            for n in range(4):
                ins = nc.scalar.copy(c_kv[:, n * RW:(n + 1) * RW], bank[n][0:1, 0:RW])
            ins.then_inc(c_act, 1)
            expert_weights_hi(0)
            expert_weights_hi(1)
            split_hi(0, x1_turned, x1_hi, bank[2], bank[4])
            act.wait_ge(c_pe, 4)
            nc.scalar.copy(vw[0:VR, 0, :], bank[3][0:VR, 0:D])
            nc.scalar.copy(vw[VR:P, 0, :], bank[3][0:VR, 0:D]).then_inc(c_act, 1)
            expert_weights_hi(2)

            act.wait_ge(d_small, 32)
            with act.Fori(0, NG - 1) as g:
                attention(g)
                split_hi(g, x2_turned, x2_hi, bank[0], bank[3])
                experts(g)
                split_hi(g + 1, x1_turned, x1_hi, bank[4], bank[5])

            g = NG - 1
            attention(g)
            for n in range(1, 5):
                keep_class_row(n)
            split_hi(g, x2_turned, x2_hi, bank[0], bank[3])
            for n in range(5, NF // RW):
                keep_class_row(n)
            experts(g)

        @block.vector
        def _(dve):
            def split_lo(g, hi, lo, from_a, from_d):
                dve.wait_ge(hi.sem, hi.at(g, 1))
                nc.vector.tensor_tensor(xa_lo[:], from_a[:], xa_hi[:].bitcast(F32), ALU.subtract
                                        ).then_inc(lo.sem, 1)
                dve.wait_ge(hi.sem, hi.at(g, 2))
                nc.vector.tensor_tensor(xd[DR:P, :], from_d[0:DR, :], xd[0:DR, :].bitcast(F32),
                                        ALU.subtract).then_inc(lo.sem, 1)

            def keep_h0(g, tiles, first=False):
                for t in tiles:
                    dve.wait_ge(tok_done.sem, tok_done.at(g, t + 1))
                    nc.vector.tensor_tensor(h0[:, t, :], embedded(t, first)[:, 0:D], bproj, ALU.add
                                            ).then_inc(h0_done.sem, 1)

            def h0_stats(g, tiles):
                for t in tiles:
                    dve.wait_ge(h0_done.sem, h0_done.at(g, t + 1))
                    nc.vector.bn_stats(stats1[:, t, :], h0[:, t, :]).then_inc(ln1.sem, 1)

            def keep_h1(g, t):
                dve.wait_ge(wo_done.sem, wo_done.at(g, t + 1))
                if t == 0:
                    dve.wait_ge(y_stored.sem, y_stored.at(g, 0))
                nc.vector.tensor_tensor(h1[:, t, :], projected(t)[:, 0:D], h0[:, t, :], ALU.add
                                        ).then_inc(h1_done.sem, 1)
                dve.wait_ge(h1_done.sem, h1_done.at(g, 2 * t + 1))
                nc.vector.tensor_tensor(h1[:, t, :], projected(t)[:, D:2 * D], h1[:, t, :], ALU.add
                                        ).then_inc(h1_done.sem, 1)
                dve.wait_ge(h1_done.sem, h1_done.at(g, 2 * t + 2))
                nc.vector.bn_stats(stats2[:, t, :], h1[:, t, :]).then_inc(ln2.sem, 1)

            def low_z(g, t):
                for i in range(2):
                    dve.wait_ge(z_kept.sem, z_kept.at(g, 2 * t + i + 1))
                    img = slice(i * NQ, (i + 1) * NQ)
                    nc.vector.tensor_tensor(z_lo[:, :, t, img],
                                            bank[6 + i][:, 0:HP * NQ].rearrange("p (j c) -> p j c", c=NQ),
                                            z_hi[:, :, t, img].bitcast(F32), ALU.subtract
                                            ).then_inc(z_low.sem, 1)

            def low_pc(g, t):
                dve.wait_ge(p_kept.sem, p_kept.at(g, 2 * t + 1))
                nc.vector.tensor_tensor(pct[VR:P, t, :], bank[4][0:VR, NH2 * P:(NH2 + 1) * P],
                                        pct[0:VR, t, :].bitcast(F32), ALU.subtract).then_inc(pc_low.sem, 1)

            def aggregate(g, tiles, stats, mv, ln, before=0):
                n = before + len(tiles)
                wait_apart(dve, ln.sem, ln.at(g, n))
                for t in tiles:
                    nc.vector.bn_aggr(mv[:, t, :], stats[:, t, :]).then_inc(ln.sem, 1)
                dve.wait_ge(ln.sem, ln.at(g, n + len(tiles)))
                var = mv[:, tiles[0]:tiles[-1] + 1, 1]
                nc.vector.tensor_scalar(var, var, LN_EPS, None, ALU.add).then_inc(ln.sem, 1)

            def normalise(g, tiles, h, mv, rstd, normal, after=1):
                dve.wait_ge(rstd.sem, rstd.at(g, after))
                for t in tiles:
                    m, r = mv[:, t, 0:1], mv[:, t, 1:2]
                    nc.vector.tensor_scalar(xn[:, t, :], h[:, t, :], m, r, ALU.subtract, ALU.mult
                                            ).then_inc(normal.sem, 1)

            def class_norm(row, n):
                nc.vector.bn_stats(c_stats[:], row).then_inc(c_dve, 1)
                dve.wait_ge(c_dve, n + 1)
                nc.vector.bn_aggr(c_mv[:], c_stats[:]).then_inc(c_dve, 1)
                dve.wait_ge(c_dve, n + 2)
                nc.vector.tensor_scalar(c_mv[:, 1:2], c_mv[:, 1:2], LN_EPS, None, ALU.add).then_inc(c_dve, 1)
                dve.wait_ge(c_pool, 1 if n == 0 else 2)
                m, r = c_mv[:, 0:1], c_mv[:, 1:2]
                nc.vector.tensor_scalar(c_xn[:, 0:P], row[:, 0:P], m, r, ALU.subtract, ALU.mult)
                nc.vector.tensor_scalar(c_xn[:, P:2 * P].rearrange("p (a b) -> p a b", a=2),
                                        row[:, P:D].unsqueeze(1).to_broadcast([1, 2, DR]), m, r,
                                        ALU.subtract, ALU.mult).then_inc(c_dve, 1)

            def mask(g, t):
                b = t % 2
                src = (bank[2], bank[3])
                if t >= 2:
                    dve.wait_ge(p_done.sem, p_done.at(g, t - 1))
                half_c = NH2 * SC
                for half in range(2):
                    dve.wait_ge(s_done.sem, s_done.at(g, 2 * t + half + 1))
                    nc.vector.scalar_tensor_tensor(
                        out=s[:, b, half * half_c:(half + 1) * half_c].rearrange("p (n c) -> p n c", c=NK),
                        in0=src[half][:, 0:half_c].rearrange("p (n c) -> p n c", c=NK),
                        scalar=float(DH) ** -0.5,
                        in1=causal[:].unsqueeze(1).to_broadcast([P, 2 * NH2, NK]),
                        op0=ALU.mult, op1=ALU.min).then_inc(s_masked.sem, 1)

            def shift(g, t):
                b = t % 2
                sv = s[:, b, :].rearrange("p (n c) -> p n c", c=NK)
                dve.wait_ge(s_masked.sem, s_masked.at(g, 2 * t + 2))
                nc.vector.tensor_reduce(smax[:, b, :], sv, AX_X, ALU.max).then_inc(s_max.sem, 1)
                dve.wait_ge(s_max.sem, s_max.at(g, t + 1))
                nc.vector.tensor_tensor(sv, sv, smax[:, b, :].unsqueeze(2).to_broadcast([P, 2 * HP, NK]),
                                        ALU.subtract).then_inc(s_shifted.sem, 1)

            def sums(g, t):
                b = t % 2
                dve.wait_ge(s_exp.sem, s_exp.at(g, t + 1))
                nc.vector.tensor_reduce(rsum[:, b, :], s[:, b, :].rearrange("p (n c) -> p n c", c=NK),
                                        AX_X, ALU.add).then_inc(s_sum.sem, 1)
                dve.wait_ge(s_sum.sem, s_sum.at(g, 2 * t + 1))
                nc.vector.reciprocal(rsum[:, b, :], rsum[:, b, :]).then_inc(s_sum.sem, 1)

            def route(np, nt, logits, exp_done, at, between={}):
                sc, ss, gs = g_sc[0:np, 0:nt], g_s[0:np, 0:nt], g_gs[0:np, 0:nt]
                lg, rank, tot = g_lg[0:np, 0:nt], g_rank[0:np, 0:nt], g_sum[0:np, 0:nt]
                done = [0]

                def step(ins):
                    ins.then_inc(gate_step.sem, 1)
                    done[0] += 1
                    if done[0] in between:
                        between[done[0]]()
                    dve.wait_ge(gate_step.sem, at(done[0]))

                def ranks(val, n, dst):
                    cmp, eq = g_cmp[0:np, 0:nt, 0:n, 0:n], g_eq[0:np, 0:nt, 0:n, 0:n]
                    vi = val.unsqueeze(2).to_broadcast([np, nt, n, n])
                    vj = val.unsqueeze(3).to_broadcast([np, nt, n, n])
                    nc.vector.tensor_tensor(cmp, vi, vj, ALU.is_gt)
                    step(nc.vector.tensor_tensor(eq, vi, vj, ALU.is_equal))
                    step(nc.vector.tensor_tensor(
                        eq, eq, earlier[0:np, 0:n, 0:n].unsqueeze(1).to_broadcast([np, nt, n, n]), ALU.mult))
                    step(nc.vector.tensor_tensor(cmp, cmp, eq, ALU.add))
                    step(nc.vector.tensor_reduce(dst, cmp, AX_X, ALU.add))

                step(nc.vector.tensor_copy(lg, logits))
                step(nc.vector.tensor_tensor(sc, lg[:, :, 0:NR], lg[:, :, NR:2 * NR], ALU.add))
                exp_done()
                step(nc.vector.tensor_scalar(sc, sc, 1.0, None, ALU.add))
                step(nc.vector.reciprocal(sc, sc))
                step(nc.vector.tensor_tensor(
                    ss, sc, gbias[0:np].unsqueeze(1).to_broadcast([np, nt, NR]), ALU.add))
                pairs = ss.rearrange("p t (a b) -> p t a b", b=2)
                step(nc.vector.tensor_tensor(gs, pairs[:, :, :, 0], pairs[:, :, :, 1], ALU.add))
                ranks(gs, NGRP, rank[:, :, 0:NGRP])
                step(nc.vector.tensor_scalar(gs, rank[:, :, 0:NGRP], 1.5, None, ALU.is_lt))
                step(nc.vector.tensor_tensor(pairs, pairs,
                                             gs.unsqueeze(3).to_broadcast([np, nt, NGRP, 2]), ALU.mult))
                step(nc.vector.tensor_scalar(gs, gs, 1.0, HUGE, ALU.subtract, ALU.mult))
                step(nc.vector.tensor_tensor(pairs, pairs,
                                             gs.unsqueeze(3).to_broadcast([np, nt, NGRP, 2]), ALU.add))
                ranks(ss, NR, rank)
                step(nc.vector.scalar_tensor_tensor(out=ss, in0=rank, scalar=1.5, in1=sc,
                                                    op0=ALU.is_lt, op1=ALU.mult))
                step(nc.vector.tensor_reduce(tot, ss, AX_X, ALU.add))
                step(nc.vector.tensor_scalar(tot, tot, SUM_EPS, None, ALU.add))
                nc.vector.reciprocal(tot, tot).then_inc(gate_step.sem, 1)
                done[0] += 1
                return done[0], ss, tot

            def weights(np, nt, ss, tot):
                for c in (0, 32):
                    ins = nc.vector.tensor_tensor(cw[0:np, 0:nt, c:c + NR], ss,
                                                  tot.unsqueeze(2).to_broadcast([np, nt, NR]), ALU.mult)
                return ins

            def last(g):
                return isinstance(g, int) and g == NG - 1

            def gate_base(g, n):
                return gate_step.at(g, n) + (NGS if last(g) else 0)

            def gating(g):
                dve.wait_ge(gate_done.sem, gate_done.at(g, 1))

                def next_stats():
                    if not last(g):
                        h0_stats(g + 1, [0, 1])

                between = {2: next_stats, 11: lambda: product(g, 0), 15: lambda: product(g, 1)}
                n, ss, tot = route(
                    P, NT, bank[2][:, 0:2 * NR * NT].rearrange("p (t c) -> p t c", t=NT),
                    lambda: dve.wait_ge(g_exp.sem, g_exp.at(g, 1)), lambda n: gate_base(g, n), between)
                assert n + 1 == NGS, n
                dve.wait_ge(gate_step.sem, gate_base(g, n))
                weights(P, NT, ss, tot).then_inc(gate_step.sem, 1)

            def keep_weights(g):
                dve.wait_ge(cw_turned.sem, cw_turned.at(g, 1))
                dve.wait_ge(cw_hi.sem, cw_hi.at(g, 1))
                nc.vector.tensor_tensor(cwt[32:40, :], bank[3][32:40, :], cwt[32:40, :].bitcast(F32),
                                        ALU.subtract).then_inc(cw_lo.sem, 1)

            def product(g, c):
                dve.wait_ge(silu_done.sem, silu_done.at(g, c + 1))
                dve.wait_ge(f3_done.sem, f3_done.at(g, c + 1))
                nc.vector.tensor_tensor(hid[:, expert(c), :], bank[6 + c % 2][:], silu[:, c % 2, :], ALU.mult
                                        ).then_inc(f_prod.sem, 1)

            def weigh(g, c):
                dve.wait_ge(f_prod.sem, f_prod.at(g, c + 1))
                dve.wait_ge(w_spread.sem, w_spread.at(g, c))
                h = hid[:, expert(c), :]
                nc.vector.tensor_tensor(h, spread_bank(c)[:], h, ALU.mult).then_inc(f_hid.sem, 1)

            def experts(g):
                for c in range(2, NE):
                    if c == 8 and last(g):
                        dve.wait_ge(c_pe, 15)
                        nc.vector.tensor_tensor(c_out[:], bank[2][0:1, 0:D], c_h1[:], ALU.add
                                                ).then_inc(c_dve, 1)
                        dve.wait_ge(c_dve, 17)
                        nc.vector.tensor_tensor(c_out[:], bank[2][0:1, D:2 * D], c_out[:], ALU.add
                                                ).then_inc(c_dve, 1)
                    product(g, c)
                    if c == EARLY - 1:
                        keep_weights(g)
                    if c == 2 and not last(g):
                        h0_stats(g + 1, [2, 3])
                    for n in weighed_after(c):
                        weigh(g, n)
                    if c == 6 and last(g):
                        dve.wait_ge(c_pe, 14)
                        cols = bank[2][:, 0:2 * NE].rearrange("p (e n) -> p e n", n=2)[:, :, 0]
                        nc.vector.tensor_copy(c_hid[:, 0, :], cols).then_inc(c_dve, 1)
                        dve.wait_ge(c_dve, 15)
                        nc.vector.tensor_tensor(c_hid[:, 1, :], cols, c_hid[:, 0, :].bitcast(F32),
                                                ALU.subtract).then_inc(c_dve, 1)
                    if not last(g):
                        if c == 3:
                            aggregate(g + 1, range(NT), stats1, mv1, ln1)
                        if c in (4, 5):
                            normalise(g + 1, [c - 4], h0, mv1, rstd1, xn1)
                        if c == 7:
                            normalise(g + 1, [2, 3], h0, mv1, rstd1, xn1)

            def last_low(g):
                e = expert(NE - 1)
                dve.wait_ge(f_up.sem, f_up.at(g, NE))
                nc.vector.tensor_tensor(hid_lo[:, e, :], hid[:, e, :], hid_hi[:, e, :].bitcast(F32),
                                        ALU.subtract).then_inc(f_last.sem, 1)

            def keep_y(g):
                for t in range(NT):
                    dve.wait_ge(y_done.sem, y_done.at(g, t + 1))
                    for n in range(2):
                        nc.vector.tensor_tensor(h1[:, t, :], y_bank(t)[:, n * D:(n + 1) * D], h1[:, t, :],
                                                ALU.add).then_inc(y_kept.sem, 1)
                        if n == 0:
                            dve.wait_ge(y_kept.sem, y_kept.at(g, 2 * t + 1))

            nc.vector.memset(mv1[:], 0.0).then_inc(y_kept.sem, 2)
            nc.vector.memset(mv2[:], 0.0).then_inc(stored, 32)
            dve.wait_ge(d_cls, 16)
            class_norm(c_row, 0)

            def class_lo(b, act_step):
                dve.wait_ge(c_act, act_step)
                nc.vector.tensor_tensor(c_a_lo[:], bank[b][:, 0:2], c_a_hi[:].bitcast(F32), ALU.subtract)
                nc.vector.tensor_tensor(c_d[DR:P, :], bank[b][DR:P, 2:4], c_d[DR:P, :].bitcast(F32),
                                        ALU.subtract).then_inc(c_dve, 1)

            def weights_lo(i):
                c = qkv_third(i)
                for n, w in enumerate((qkv_a, qkv_d)):
                    dve.wait_ge(w_hi, 2 * i + n + 1)
                    nc.vector.tensor_tensor(w[:, 1, c], stage[:, i, n, :], w[:, 0, c].bitcast(F32),
                                            ALU.subtract).then_inc(w_lo, 1)

            class_lo(0, 2)
            weights_lo(0)
            weights_lo(1)
            weights_lo(2)
            dve.wait_ge(d_small, 32)
            keep_h0(0, range(NT), first=True)
            h0_stats(0, range(NT))
            aggregate(0, range(NT), stats1, mv1, ln1)
            dve.wait_ge(c_pe, 3)
            kv = bank[0][:, 0:4 * HP].rearrange("p (j n) -> p j n", n=2)[:, :, 0]
            nc.vector.tensor_tensor(k[:, :, :, NQ], kv[:, 0:HP].unsqueeze(2).to_broadcast([P, HP, IMG]),
                                    bk.unsqueeze(2).to_broadcast([P, HP, IMG]), ALU.add
                                    ).then_inc(c_dve, 1)
            flat = vblk.rearrange("p j c -> p (j c)")
            dve.wait_ge(consts, 1)
            for h in range(2):
                hs = slice(h * DH, (h + 1) * DH)
                nc.vector.tensor_copy(flat[hs, 32 * h:32 * h + (HP - 1) * (VR + 1) + 1:VR + 1],
                                      kv[hs, HP:2 * HP])
            nc.vector.tensor_copy(vblk[:, :, CB], bv).then_inc(c_dve, 1)
            normalise(0, range(NT), h0, mv1, rstd1, xn1)
            split_lo(0, x1_hi, x1_lo, bank[2], bank[4])
            dve.wait_ge(c_act, 4)
            for h in range(2):
                nc.vector.tensor_tensor(vw[h * VR:(h + 1) * VR, 1, :], bank[3][0:VR, 0:D],
                                        vw[0:VR, 0, :].bitcast(F32), ALU.subtract).then_inc(vw_low, 1)
            dve.wait_ge(c_pe, 4)
            nc.vector.tensor_copy(wo[:, :, 0, :], wo_raw[:, :, 1, :]).then_inc(o_split, 1)
            dve.wait_ge(o_split, 1)
            nc.vector.tensor_tensor(wo[:, :, 1, :], wo_raw[:, :, 1, :], wo[:, :, 0, :].bitcast(F32),
                                    ALU.subtract).then_inc(o_split, 1)
            dve.wait_ge(d_w2, 16)
            nc.vector.tensor_copy(w2[:, :, 0, :], w2_raw[:, :, 1, :]).then_inc(o_split, 1)
            dve.wait_ge(o_split, 3)
            nc.vector.tensor_tensor(w2[:, :, 1, :], w2_raw[:, :, 1, :], w2[:, :, 0, :].bitcast(F32),
                                    ALU.subtract).then_inc(o_split, 1)

            def attention(g):
                mask(g, 0)
                shift(g, 0)
                mask(g, 1)
                sums(g, 0)
                shift(g, 1)
                mask(g, 2)
                sums(g, 1)
                shift(g, 2)
                low_pc(g, 0)
                low_z(g, 0)
                sums(g, 2)
                low_pc(g, 1)
                mask(g, 3)
                shift(g, 3)
                sums(g, 3)
                low_z(g, 1)
                low_pc(g, 2)
                keep_h1(g, 0)
                low_z(g, 2)
                low_pc(g, 3)
                keep_h1(g, 1)
                keep_h1(g, 2)
                aggregate(g, range(3), stats2, mv2, ln2)
                low_z(g, 3)
                normalise(g, range(3), h1, mv2, rstd2, xn2)
                keep_h1(g, 3)
                aggregate(g, range(3, NT), stats2, mv2, ln2, before=7)
                normalise(g, range(3, NT), h1, mv2, rstd2, xn2, after=2)

            with dve.Fori(0, NG - 1) as g:
                attention(g)
                keep_h0(g + 1, [0])
                split_lo(g, x2_hi, x2_lo, bank[0], bank[3])
                keep_h0(g + 1, [1, 2, 3])
                gating(g)
                experts(g)
                last_low(g)
                split_lo(g + 1, x1_hi, x1_lo, bank[4], bank[5])
                keep_y(g)

            g = NG - 1
            dve.wait_ge(c_pe, 5)
            nc.vector.tensor_tensor(c_h1[:], bank[5][0:1, 0:D], c_row, ALU.add).then_inc(c_dve, 1)
            dve.wait_ge(c_dve, 8)
            class_norm(c_h1[:], 8)
            class_lo(1, 6)
            dve.wait_ge(c_pe, 7)
            n, ss, tot = route(1, 1, bank[0][0:1, 256:256 + 2 * NR].rearrange("p (t c) -> p t c", t=1),
                               lambda: dve.wait_ge(c_act, 7), lambda n: gate_step.at(g, n))
            dve.wait_ge(gate_step.sem, gate_step.at(g, n))
            weights(1, 1, ss, tot).then_inc(gate_step.sem, 1)
            dve.wait_ge(gate_step.sem, gate_step.at(g, NGS))
            nc.vector.tensor_copy(c_cw[:], cw[0:1, 0, 0:NR]).then_inc(c_dve, 1)
            attention(g)
            split_lo(g, x2_hi, x2_lo, bank[0], bank[3])
            gating(g)
            experts(g)
            last_low(g)
            keep_y(g)


def kernel(x, cls_tok, L0_tok_W_proj, L0_tok_b_proj, L0_attn_W_Q, L0_attn_b_Q, L0_attn_W_K, L0_attn_b_K,
           L0_attn_W_V, L0_attn_b_V, L0_attn_W_O, L0_attn_b_O, L0_ffn_gate_weight, L0_ffn_gate_bias,
           L0_ffn_w1, L0_ffn_w2, L0_ffn_w3, L0_ffn_sw1, L0_ffn_sw2, L0_ffn_sw3):
    import numpy as np
    import concourse.bacc as bacc
    from concourse.bass_utils import run_bass_kernel_spmd

    x = np.asarray(x)
    B, C, H, W = x.shape
    p, groups = 16, 4
    D = L0_tok_W_proj.shape[0]
    nh, _, dh = L0_attn_W_Q.shape
    n = (H // p) * (W // p)
    xt = x.reshape(B, C, H // p, p, W // p, p).transpose(1, 3, 5, 0, 2, 4).reshape(-1, 128, groups, B * n // groups)
    xt = xt.transpose(2, 1, 0, 3)

    def chunks(w):
        return np.asarray(w).reshape(-1, 128, w.shape[-1]).transpose(1, 0, 2)

    def blocks(w):
        return np.stack([w[0:128], np.concatenate([w[128:], w[128:]])], 1)

    def heads_last(w):
        return np.asarray(w).transpose(1, 0, 2).reshape(D, nh * dh)

    def by_pair(b):
        return np.asarray(b).reshape(nh // 2, 2 * dh).T

    w1 = np.concatenate([np.asarray(L0_ffn_w1), np.asarray(L0_ffn_sw1)[None]])
    w3 = np.concatenate([np.asarray(L0_ffn_w3), np.asarray(L0_ffn_sw3)[None]])
    w_ffn = np.stack([w1, w3], 1).transpose(3, 0, 1, 2).reshape(D, -1)
    w_2 = np.concatenate([np.asarray(L0_ffn_w2), np.asarray(L0_ffn_sw2)[None]]).transpose(2, 0, 1)
    arrays = {
        "xt": xt,
        "w_proj": chunks(np.asarray(L0_tok_W_proj).T),
        "w_qkv": blocks(np.concatenate([heads_last(w) for w in (L0_attn_W_Q, L0_attn_W_K, L0_attn_W_V)], 1)),
        "w_o": chunks(np.asarray(L0_attn_W_O).reshape(nh * dh, D)),
        "w_gate": blocks(np.asarray(L0_ffn_gate_weight).T),
        "w_ffn": blocks(w_ffn),
        "w_2": w_2,
        "b_heads": np.stack([by_pair(b) for b in (L0_attn_b_Q, L0_attn_b_K, L0_attn_b_V)], 1),
        "b_tokens": np.concatenate([np.asarray(L0_tok_b_proj), np.asarray(L0_ffn_gate_bias)])[None],
        "cls_rows": np.stack([np.asarray(cls_tok).reshape(D), np.asarray(L0_attn_b_O)])[None],
    }
    arrays = {name: np.ascontiguousarray(a) for name, a in arrays.items()}
    nc = bacc.Bacc("TRN2", target_bir_lowering=False, num_devices=1, dynamic_dma_scratch_size=1024)
    args = [nc.dram_tensor(name, a.shape, F32, kind="ExternalInput").ap() for name, a in arrays.items()]
    out = nc.dram_tensor("out", (B, n + 1, D), F32, kind="ExternalOutput").ap()
    vit_tower(nc, *args, out)
    r = run_bass_kernel_spmd(nc, [arrays], core_ids=[0])
    return r.results[0]["out"]
```
